# Optimizing a Trainium2 kernel written in Bass

```python
import numpy as np
import jax
import jax.numpy as jnp

def _softmax(x, axis=-1):
    return jax.nn.softmax(x, axis=axis)

def _gelu(x):
    return jax.nn.gelu(x, approximate=True)

def _silu(x):
    return jax.nn.silu(x)

def _sigmoid(x):
    return jax.nn.sigmoid(x)

def _layernorm(x, axis=-1, eps=1e-05):
    m = jnp.mean(x, axis=axis, keepdims=True)
    v = jnp.var(x, axis=axis, keepdims=True)
    return (x - m) / jnp.sqrt(v + eps)

def _scatter_add(tgt, idx, src, axis=0):
    return tgt.at[idx].add(src)

def _segment_sum(src, seg, n):
    return jax.ops.segment_sum(src, seg, n)
kernel_name = 'mk_decoder_preln_d1_seqx_r2_d578eb'

def setup_inputs(seed: int=0):
    np.random.seed(seed)
    _w = jnp.asarray

    def _rec_inputs():
        import jax
        import jax.numpy as jnp
        _rk = jax.random.key(seed)
        x = -0.0002928 + 1 * jax.random.normal(jax.random.fold_in(_rk, 1), (8, 512, 512), jnp.float32)
        _lenS = 512 - jax.random.randint(jax.random.fold_in(_rk, 7), (8,), 0, max(1, 512 // 4) + 1, jnp.int32)
        _lenS2 = 512 - jax.random.randint(jax.random.fold_in(_rk, 8), (8,), 0, max(1, 512 // 4) + 1, jnp.int32)
        _ctx_1024P = jax.random.normal(jax.random.fold_in(_rk, 11), (8, 16, 512), jnp.float32)
        _ctx_1024c = jax.random.dirichlet(jax.random.fold_in(_rk, 511), 0.3 * jnp.ones((16,), jnp.float32), (8, 512))
        _ctx_1024t = jnp.einsum('bsk,bkd->bsd', _ctx_1024c, _ctx_1024P)
        _ctx_1024t = _ctx_1024t * jax.lax.rsqrt(jnp.mean(jnp.square(_ctx_1024t)) + 1e-12) * 0.953939
        ctx_1024 = -1.39393e-06 + 0.999914 * (_ctx_1024t + 0.3 * jax.random.normal(jax.random.fold_in(_rk, 611), (8, 512, 512), jnp.float32))
        return (x, ctx_1024)
    x, ctx_1024 = _rec_inputs()

    def _L0_attn_setup():
        import jax, jax.numpy as jnp
        import numpy as np
        B, S, H, NH = (2, 1024, 512, 16)
        HD = H // NH
        EPS = 1e-05

        def _layernorm(x, gamma, beta):
            mu = jnp.mean(x, axis=-1, keepdims=True)
            var = jnp.mean(jnp.square(x - mu), axis=-1, keepdims=True)
            return (x - mu) * jax.lax.rsqrt(var + EPS) * gamma + beta
        key = jax.random.key(seed)
        ks = jax.random.split(key, 4)
        return {'hidden_states': jax.random.normal(ks[0], (B, S, H), dtype=jnp.float32), 'W_attn': jax.random.normal(ks[1], (H, 3 * H), dtype=jnp.float32) * (1.0 / np.sqrt(H)), 'b_attn': jnp.zeros((3 * H,), dtype=jnp.float32), 'W_proj': jax.random.normal(ks[2], (H, H), dtype=jnp.float32) * (1.0 / np.sqrt(H)), 'b_proj': jnp.zeros((H,), dtype=jnp.float32), 'q_gamma': jnp.ones((HD,), dtype=jnp.float32), 'q_beta': jnp.zeros((HD,), dtype=jnp.float32), 'k_gamma': jnp.ones((HD,), dtype=jnp.float32), 'k_beta': jnp.zeros((HD,), dtype=jnp.float32)}
    _L0_attn_all = _L0_attn_setup()
    _L0_attn_in = {k: v for k, v in _L0_attn_all.items() if k in ('W_attn', 'b_attn', 'W_proj', 'b_proj', 'q_gamma', 'q_beta', 'k_gamma', 'k_beta')}
    del _L0_attn_all

    def _L0_xattn_setup():
        import jax, jax.numpy as jnp
        import numpy as np
        import math
        D_MODEL = 512
        N_HEADS = 16
        HEAD_DIM = D_MODEL // N_HEADS
        TOP_K = 32
        SCALE = math.sqrt(HEAD_DIM)

        def _split_heads(t, n):
            B, L, _ = t.shape
            return t.reshape(B, L, N_HEADS, HEAD_DIM).transpose(0, 2, 1, 3)
        key = jax.random.key(seed)
        ks = jax.random.split(key, 12)
        B, S, N = (2, 1024, 1024)
        std = 1.0 / math.sqrt(D_MODEL)
        inp = {'x': jax.random.normal(ks[0], (B, S, D_MODEL), dtype=jnp.float32), 'knowledge_embeddings': jax.random.normal(ks[1], (B, N, D_MODEL), dtype=jnp.float32), 'Wq': jax.random.normal(ks[2], (D_MODEL, D_MODEL), dtype=jnp.float32) * std, 'bq': jnp.zeros((D_MODEL,), dtype=jnp.float32), 'Wk': jax.random.normal(ks[3], (D_MODEL, D_MODEL), dtype=jnp.float32) * std, 'bk': jnp.zeros((D_MODEL,), dtype=jnp.float32), 'Wv': jax.random.normal(ks[4], (D_MODEL, D_MODEL), dtype=jnp.float32) * std, 'bv': jnp.zeros((D_MODEL,), dtype=jnp.float32), 'Wo': jax.random.normal(ks[5], (D_MODEL, D_MODEL), dtype=jnp.float32) * std, 'bo': jnp.zeros((D_MODEL,), dtype=jnp.float32)}
        return inp
    _L0_xattn_all = _L0_xattn_setup()
    _L0_xattn_in = {k: v for k, v in _L0_xattn_all.items() if k in ('Wq', 'bq', 'Wk', 'bk', 'Wv', 'bv', 'Wo', 'bo')}
    del _L0_xattn_all

    def _L0_ffn_setup():
        import jax, jax.numpy as jnp
        import numpy as np
        HIDDEN = 512
        INNER = 2048

        def _weight_quant(w):
            scale = 1.0 / jnp.clip(jnp.mean(jnp.abs(w)), 1e-05)
            wq = jnp.clip(jnp.round(w * scale), -1.0, 1.0) / scale
            return w + jax.lax.stop_gradient(wq - w)

        def _act_quant(x):
            scale = 127.0 / jnp.clip(jnp.max(jnp.abs(x), axis=-1, keepdims=True), 1e-05)
            xq = jnp.clip(jnp.round(x * scale), -128.0, 127.0) / scale
            return x + jax.lax.stop_gradient(xq - x)

        def _bitlinear(x, w):
            return jnp.einsum('bsi,oi->bso', _act_quant(x), _weight_quant(w))
        key = jax.random.key(seed)
        k0, k1, k2, k3 = jax.random.split(key, 4)
        x = jax.random.normal(k0, (4, 1024, HIDDEN), dtype=jnp.float32)
        w_gate = jax.random.normal(k1, (INNER, HIDDEN), dtype=jnp.float32) / np.sqrt(HIDDEN)
        w_up = jax.random.normal(k2, (INNER, HIDDEN), dtype=jnp.float32) / np.sqrt(HIDDEN)
        w_down = jax.random.normal(k3, (HIDDEN, INNER), dtype=jnp.float32) / np.sqrt(INNER)
        return {'x': x, 'w_gate': w_gate, 'w_up': w_up, 'w_down': w_down}
    _L0_ffn_all = _L0_ffn_setup()
    _L0_ffn_in = {k: v for k, v in _L0_ffn_all.items() if k in ('w_gate', 'w_up', 'w_down')}
    del _L0_ffn_all
    return {'x': x, 'ctx_1024': ctx_1024, 'L0_attn_W_attn': _L0_attn_in['W_attn'], 'L0_attn_b_attn': _L0_attn_in['b_attn'], 'L0_attn_W_proj': _L0_attn_in['W_proj'], 'L0_attn_b_proj': _L0_attn_in['b_proj'], 'L0_attn_q_gamma': _L0_attn_in['q_gamma'], 'L0_attn_q_beta': _L0_attn_in['q_beta'], 'L0_attn_k_gamma': _L0_attn_in['k_gamma'], 'L0_attn_k_beta': _L0_attn_in['k_beta'], 'L0_xattn_Wq': _L0_xattn_in['Wq'], 'L0_xattn_bq': _L0_xattn_in['bq'], 'L0_xattn_Wk': _L0_xattn_in['Wk'], 'L0_xattn_bk': _L0_xattn_in['bk'], 'L0_xattn_Wv': _L0_xattn_in['Wv'], 'L0_xattn_bv': _L0_xattn_in['bv'], 'L0_xattn_Wo': _L0_xattn_in['Wo'], 'L0_xattn_bo': _L0_xattn_in['bo'], 'L0_ffn_w_gate': _L0_ffn_in['w_gate'], 'L0_ffn_w_up': _L0_ffn_in['w_up'], 'L0_ffn_w_down': _L0_ffn_in['w_down']}

def reference(x, ctx_1024, L0_attn_W_attn, L0_attn_b_attn, L0_attn_W_proj, L0_attn_b_proj, L0_attn_q_gamma, L0_attn_q_beta, L0_attn_k_gamma, L0_attn_k_beta, L0_xattn_Wq, L0_xattn_bq, L0_xattn_Wk, L0_xattn_bk, L0_xattn_Wv, L0_xattn_bv, L0_xattn_Wo, L0_xattn_bo, L0_ffn_w_gate, L0_ffn_w_up, L0_ffn_w_down):
    import jax
    import jax.numpy as jnp

    def _L0_attn_ref(hidden_states, W_attn, b_attn, W_proj, b_proj, q_gamma, q_beta, k_gamma, k_beta):
        import jax, jax.numpy as jnp
        import numpy as np
        B, S, H, NH = (2, 1024, 512, 16)
        HD = H // NH
        EPS = 1e-05

        def _layernorm(x, gamma, beta):
            mu = jnp.mean(x, axis=-1, keepdims=True)
            var = jnp.mean(jnp.square(x - mu), axis=-1, keepdims=True)
            return (x - mu) * jax.lax.rsqrt(var + EPS) * gamma + beta
        b, s, h = hidden_states.shape
        qkv = hidden_states @ W_attn + b_attn
        q, k, v = jnp.split(qkv, 3, axis=-1)

        def to_heads(t):
            return t.reshape(b, s, NH, HD).transpose(0, 2, 1, 3)
        q, k, v = (to_heads(q), to_heads(k), to_heads(v))
        q = _layernorm(q, q_gamma, q_beta)
        k = _layernorm(k, k_gamma, k_beta)
        scale = HD ** (-0.5)
        scores = jnp.einsum('bhqd,bhkd->bhqk', q, k) * scale
        causal = jnp.tril(jnp.ones((s, s), dtype=bool))
        mask_value = jnp.finfo(scores.dtype).min
        scores = jnp.where(causal, scores, mask_value)
        attn = jax.nn.softmax(scores.astype(jnp.float32), axis=-1).astype(q.dtype)
        out = jnp.einsum('bhqk,bhkd->bhqd', attn, v)
        out = out.transpose(0, 2, 1, 3).reshape(b, s, h)
        out = out @ W_proj + b_proj
        return out

    def _L0_xattn_ref(x, knowledge_embeddings, Wq, bq, Wk, bk, Wv, bv, Wo, bo):
        import jax, jax.numpy as jnp
        import numpy as np
        import math
        D_MODEL = 512
        N_HEADS = 16
        HEAD_DIM = D_MODEL // N_HEADS
        TOP_K = 32
        SCALE = math.sqrt(HEAD_DIM)

        def _split_heads(t, n):
            B, L, _ = t.shape
            return t.reshape(B, L, N_HEADS, HEAD_DIM).transpose(0, 2, 1, 3)
        B, S, _ = x.shape
        N = knowledge_embeddings.shape[1]
        Q = _split_heads(x @ Wq.T + bq, N_HEADS)
        K = _split_heads(knowledge_embeddings @ Wk.T + bk, N_HEADS)
        V = _split_heads(knowledge_embeddings @ Wv.T + bv, N_HEADS)
        scores = jnp.einsum('bhsd,bhnd->bhsn', Q, K) / SCALE
        k = min(TOP_K, N)
        topk_scores, topk_indices = jax.lax.top_k(scores, k)
        sparse_weights = jax.nn.softmax(topk_scores, axis=-1)
        sel_V = jnp.take_along_axis(V[:, :, None, :, :], topk_indices[..., None], axis=3)
        context = jnp.einsum('bhsk,bhskd->bhsd', sparse_weights, sel_V)
        context = context.transpose(0, 2, 1, 3).reshape(B, S, D_MODEL)
        return context @ Wo.T + bo

    def _L0_ffn_ref(x, w_gate, w_up, w_down):
        import jax, jax.numpy as jnp
        import numpy as np
        HIDDEN = 512
        INNER = 2048

        def _weight_quant(w):
            scale = 1.0 / jnp.clip(jnp.mean(jnp.abs(w)), 1e-05)
            wq = jnp.clip(jnp.round(w * scale), -1.0, 1.0) / scale
            return w + jax.lax.stop_gradient(wq - w)

        def _act_quant(x):
            scale = 127.0 / jnp.clip(jnp.max(jnp.abs(x), axis=-1, keepdims=True), 1e-05)
            xq = jnp.clip(jnp.round(x * scale), -128.0, 127.0) / scale
            return x + jax.lax.stop_gradient(xq - x)

        def _bitlinear(x, w):
            return jnp.einsum('bsi,oi->bso', _act_quant(x), _weight_quant(w))
        gate = jax.nn.silu(_bitlinear(x, w_gate))
        up = _bitlinear(x, w_up)
        return _bitlinear(gate * up, w_down)
    x = x + _L0_attn_ref(_layernorm(x, axis=-1), L0_attn_W_attn, L0_attn_b_attn, L0_attn_W_proj, L0_attn_b_proj, L0_attn_q_gamma, L0_attn_q_beta, L0_attn_k_gamma, L0_attn_k_beta)
    x = x + _L0_xattn_ref(_layernorm(x, axis=-1), ctx_1024, L0_xattn_Wq, L0_xattn_bq, L0_xattn_Wk, L0_xattn_bk, L0_xattn_Wv, L0_xattn_bv, L0_xattn_Wo, L0_xattn_bo)
    x = x + _L0_ffn_ref(_layernorm(x, axis=-1), L0_ffn_w_gate, L0_ffn_w_up, L0_ffn_w_down)
    return x

_drawn_inputs = setup_inputs


def setup_inputs(seed=0):
    import zlib

    import numpy as np

    out = dict(_drawn_inputs(seed))
    spreads = {'L0_attn_b_attn': (0.0, 0.1),
     'L0_attn_b_proj': (0.0, 0.1),
     'L0_attn_q_gamma': (1.0, 0.2),
     'L0_attn_q_beta': (0.0, 0.352),
     'L0_attn_k_gamma': (1.0, 0.2),
     'L0_attn_k_beta': (0.0, 0.8),
     'L0_xattn_bq': (0.0, 0.1),
     'L0_xattn_bk': (0.0, 0.8),
     'L0_xattn_bv': (0.0, 0.1),
     'L0_xattn_bo': (0.0, 0.1)}
    factors = {}
    for name, (base, spread) in spreads.items():
        noise = np.random.default_rng([zlib.crc32(name.encode()), seed]).standard_normal(out[name].shape)
        drawn = base * np.exp(spread * noise) if base else spread * noise
        out[name] = jnp.asarray(drawn.astype(out[name].dtype))
    for name, factor in factors.items():
        out[name] = (out[name] * factor).astype(out[name].dtype)
    return out
```

```python
from contextlib import ExitStack

import numpy as np

import concourse.bass as bass
from concourse import mybir

F32 = mybir.dt.float32
BF16 = mybir.dt.bfloat16
FP8 = mybir.dt.float8e4
ALU = mybir.AluOpType
ACT = mybir.ActivationFunctionType
AXX = mybir.AxisListType.X

P = 128
NB, S, D = 8, 512, 512
H, HD = 16, 32
F = 2048
NT = S // P
NC = D // P
HG = P // HD
NG = H // HG
NF = F // 512
KF = F // P
ROUNDS = 4
SLOTS = NG * NT
SCALE = float(HD) ** -0.5
EPS = 1e-5
MAGIC = 1.5 * 2.0 ** 23
MASKED = -1e30
REPLACED = -3e38
LO, HI = -1, NB + 2


SIGNALS = ["shared_full", "shared_read", "cscore_full", "cscore_read", "sscore_full", "sscore_read",
           "smax", "sexp", "sbias", "cbias", "cexp", "topk", "spT_full", "spT_read", "so_full", "so_recip",
           "so_norm", "cpT_full", "cpT_read", "crest", "cprob", "co_full", "co_recip", "co_norm",
           "sq_done", "rstd_done", "shat_done", "sumsq_done", "dve_rows", "pool_rows", "feed_stats",
           "feed_pool", "h_dve", "h_pool", "rmax", "wa_in", "wc_in", "feed_in0", "feed_in1", "feed_in2",
           "feed_in3", "xres_in", "x1res_in", "x1_out", "x2_out", "x2res_in", "y_out"]


class Stages:

    def __init__(self, i):
        def on(b):
            return 0 <= b < NB
        self.self_now, self.self_next, self.self_last = on(i), on(i + 1), on(i - 1)
        self.proj1 = on(i - 1)
        self.cross_now, self.cross_next, self.cross_last = on(i - 2), on(i - 1), on(i - 3)
        self.mlp = on(i - 3)

    def key(self):
        return (self.self_now, self.self_next, self.self_last, self.proj1, self.cross_now, self.cross_next,
                self.cross_last, self.mlp)


def feeds(st, s):
    order = [(src, t) for src in ("x", "x1", "ctx") for t in range(NT)]
    slots = [9, 9, 10, 10, 11, 11, 12, 12, 12, 13, 13, 13]
    return [(k, src, t) for k, (src, t) in enumerate(order) if slots[k] == s
            and (st.self_next if src == "x" else st.cross_next)]


def all_feeds(st):
    return [f for s in range(SLOTS) for f in feeds(st, s)]


def groups_self(st, s, first):
    g = (s - first) // 4 + 1
    if (s - first) % 4 or not 1 <= g <= NG:
        return []
    return [g] if (st.self_next if g == NG else st.self_now) else []


def groups_cross(st, s, first):
    g = (s - first) // 4 + 1
    if (s - first) % 4 or not 1 <= g <= NG:
        return []
    return [g] if (st.cross_next if g == NG else st.cross_now) else []


def mlp_chunks(st, s):
    if not st.mlp or not 2 <= s < 2 + 3 * NT:
        return []
    t, r = (s - 2) // 3, (s - 2) % 3
    return [(t, 0), (t, 1)] if r == 0 else [(t, r + 1)]


def mlp_down(st, s):
    return [(s - 5) // 3] if st.mlp and s >= 5 and (s - 5) % 3 == 0 and (s - 5) // 3 < NT else []


def shared_units(st, s):
    u = []
    if st.mlp and s < NT:
        u.append(("cross_oT", s))
    if st.proj1 and s < NT:
        u.append(("self_oT", s))
    if st.mlp and s < NT:
        u.append(("cross_out", s))
    if st.proj1 and s < NT:
        u.append(("self_out", s))
    for t in mlp_down(st, s):
        u += [("hT", t, q) for q in range(NF)]
    if st.mlp and 1 <= s <= NT:
        u.append(("x2T", s - 1))
    for t, n in mlp_chunks(st, s):
        u += [("gate", t, n), ("up", t, n)]
    for g in groups_self(st, s, 1):
        u += [("self_qkv", g, t) for t in range(NT)]
    for g in groups_cross(st, s, 2):
        u += [("cross_qkv", g, t) for t in range(NT)]
    for t in mlp_down(st, s):
        u.append(("down", t))
    for g in groups_self(st, s, 3):
        u += [("self_T", g, 0), ("self_T", g, 1)]
    for g in groups_cross(st, s, 3):
        u += [("cross_T", g, 0), ("cross_T", g, 1)]
    for k, src, t in feeds(st, s):
        u.append(("feed", k, src, t))
    return u


ACT_READS = {"cross_oT": 1, "self_oT": 1, "hT": 1, "x2T": 1, "gate": 2, "self_qkv": 2, "cross_qkv": 2,
             "self_T": 1, "cross_T": 1, "feed": 1}
DVE_READS = {"cross_out", "self_out", "up", "down"}


class Counts:

    def __init__(self, st):
        self.order, self.given = {}, {}
        add = self._add
        apply_self = [s - 1 for s in range(SLOTS) if (st.self_last if s == 0 else st.self_now)]
        apply_cross = [s - 1 for s in range(SLOTS) if (st.cross_last if s == 0 else st.cross_now)]
        self.apply_self, self.apply_cross = apply_self, apply_cross
        self.bank, self.before = {}, {}
        held = [None, None]
        n = 0
        for s in range(SLOTS):
            for u in shared_units(st, s):
                self.bank[u], self.before[u] = n % 2, held[n % 2]
                held[n % 2] = u
                n += 1
                add("shared_full", u)
                for r in range(ACT_READS.get(u[0], 0)):
                    add("shared_read", (u, r))
        for s in range(SLOTS):
            if st.cross_now if s < SLOTS - 1 else st.cross_next:
                for j in range(HG):
                    add("cscore_full", (s + 1, j))
                    add("cscore_read", (s + 1, j))
            if st.self_now:
                for j in range(HG):
                    for name in ("sscore_full", "sscore_read", "smax", "sexp"):
                        add(name, (s, j))
                add("sbias", s)
            if st.cross_now:
                add("rmax", s)
                add("cbias", s)
                for j in range(HG):
                    add("cexp", (s, j))
                for r in range(ROUNDS):
                    for half in ("max", "replace"):
                        for j in range(HG):
                            add("topk", (s, r, half, j))
        for m in apply_self:
            for j in range(HG):
                add("spT_full", (m, j))
                add("spT_read", (m, j))
            add("so_full", m)
            add("so_recip", m)
            add("so_norm", m)
        for m in apply_cross:
            for j in range(HG):
                add("cpT_full", (m, j))
                add("cpT_read", (m, j))
                add("crest", (m, j))
                add("cprob", (m, j))
            add("co_full", m)
            add("co_recip", m)
            add("co_norm", m)

    def _add(self, name, label):
        self.order.setdefault(name, {})[label] = len(self.order.get(name, {})) + 1

    def plan(self, name, label):
        self._add(name, label)

    def upto(self, name, label, each=1):
        return each * self.order.get(name, {}).get(label, 0)

    def step(self, name, label, each=1):
        self.given[name] = self.given.get(name, 0) + 1
        assert self.order[name][label] == self.given[name], (name, label)
        return each

    def end(self):
        for name, labels in self.order.items():
            assert self.given.get(name, 0) == len(labels), (name, self.given.get(name, 0), len(labels))


def decoder_layer(nc, x, ctx_in, W_attn, b_attn, W_proj, b_proj, q_gamma, q_beta, k_gamma, k_beta,
                  Wq, bq, Wk, bk, Wv, bv, Wo, bo, w_gate, w_up, w_down, out):
    x_rows = x.rearrange("b s d -> (b s) d")
    ctx_rows = ctx_in.rearrange("b s d -> (b s) d")
    out_rows = out.rearrange("b s d -> (b s) d")
    wa_dram = nc.dram_tensor("wa_by_group", (NG, P, NC, 3, P), F32, kind="Internal").ap()
    wc_dram = nc.dram_tensor("wc_by_group", (NG, P, NC, 3, P), F32, kind="Internal").ap()
    x1_rows = nc.dram_tensor("x1_rows", (NB * S, D), F32, kind="Internal").ap()
    x2_rows = nc.dram_tensor("x2_rows", (NB * S, D), F32, kind="Internal").ap()

    with ExitStack() as keep:
        def sb(name, shape, dt=F32, stack=keep):
            return stack.enter_context(nc.sbuf_tensor(name, shape, dt))

        def sem(name, stack=keep):
            return stack.enter_context(nc.semaphore(name))

        banks = [keep.enter_context(nc.psum_tensor(f"bank{k}", [P, 512], F32)) for k in range(8)]
        cscore_ps, sscore_ps, cpT_ps, spT_ps, co_ps, so_ps = banks[:6]
        shared_ps = banks[6:]

        ident = sb("ident", [P, P])
        ident16 = sb("ident16", [P, P], BF16)
        mask16 = sb("mask16", [P, P], BF16)
        ones16 = sb("ones16", [96, P], BF16)
        bias16 = sb("bias16", [96, 3 * D], BF16)
        minus_half = sb("minus_half", [P, 32])
        gb = sb("gb", [P, 4])
        wscale = sb("wscale", [P, 3])
        wproj = sb("wproj", [P, NC, D])
        woT = sb("woT", [P, NC, D])
        wgT = sb("wgT", [P, NC, F], FP8)
        wuT = sb("wuT", [P, NC, F], FP8)
        wdT = sb("wdT", [P, KF, D], FP8)

        setup(nc, dict(W_attn=W_attn, b_attn=b_attn, wa_dram=wa_dram, wc_dram=wc_dram, banks=banks,
                       ident=ident, ident16=ident16, mask16=mask16, ones16=ones16, bias16=bias16,
                       minus_half=minus_half, gb=gb, wscale=wscale, wproj=wproj, woT=woT, wgT=wgT, wuT=wuT,
                       wdT=wdT, bq=bq, bk=bk, bv=bv, b_proj=b_proj, bo=bo, q_gamma=q_gamma, q_beta=q_beta,
                       k_gamma=k_gamma, k_beta=k_beta, W_proj=W_proj, Wq=Wq, Wk=Wk, Wv=Wv, Wo=Wo,
                       w_gate=w_gate, w_up=w_up, w_down=w_down))

        wa = sb("wa", [P, NC, 3 * P])
        wc = sb("wc", [P, NC, 3 * P])
        feed = [sb(f"feed{k}", [P, D]) for k in range(4)]
        xT = sb("xT", [P, NC, S])
        x1T = sb("x1T", [P, NC, S])
        ctxT = sb("ctxT", [P, NC, S])
        sqk = sb("sqk", [P, NT, 2 * P])
        ssq = sb("ssq", [P, NT, 2 * P])
        srs = sb("srs", [P, 2 * NT * HG])
        sqT, skT = sb("sqT", [P, S]), sb("skT", [P, S])
        sv = [sb(f"sv{k}", [P, NT, HG, HD + 1]) for k in range(2)]
        sP = [sb(f"sP{j}", [P, S]) for j in range(HG)]
        sPT = [sb(f"sPT{k}", [P, S]) for k in range(2)]
        smx, snb = sb("smx", [P, HG]), sb("snb", [P, HG])
        so_r = sb("so_r", [P, HG])
        so = sb("so", [P, NT, D])
        cqk = sb("cqk", [P, NT, 2 * P])
        cqT, ckT = sb("cqT", [P, S]), sb("ckT", [P, S])
        cv = [sb(f"cv{k}", [P, NT, HG, HD + 1]) for k in range(2)]
        cS = [[sb(f"cS{k}_{j}", [P, S]) for j in range(HG)] for k in range(2)]
        cW = [sb(f"cW{j}", [P, S]) for j in range(HG)]
        top8 = sb("top8", [P, HG, 8])
        rowmax = sb("rowmax", [P, HG])
        cnb = [sb(f"cnb{k}", [P, HG]) for k in range(2)]
        cPT = [sb(f"cPT{k}", [P, S]) for k in range(2)]
        co_r = sb("co_r", [P, HG])
        co = sb("co", [P, NT, D])
        self_oT, cross_oT = sb("self_oT", [P, NC, P]), sb("cross_oT", [P, NC, P])
        xres = sb("xres", [P, D])
        x1res, x2t, x2h = sb("x1res", [P, D]), sb("x2t", [P, D]), sb("x2h", [P, D])
        x2T = sb("x2T", [P, NT, NC, P], BF16)
        mstat = sb("mstat", [P, 6])
        mv, mcol = sb("mv", [P, 2]), sb("mcol", [P, 8])
        gate_scale, up_amax = sb("gate_scale", [P, NT, 2]), sb("up_amax", [P, NT])
        th, gc = sb("th", [P, 512]), sb("gc", [P, 512])
        hh = sb("hh", [P, NF, 512])
        hmx, hcol = sb("hmx", [P, NF]), sb("hcol", [P, 4])
        hT = sb("hT", [P, KF, P], BF16)
        x2res = sb("x2res", [P, D])
        fstat, fmv, fcol = sb("fstat", [P, 6]), sb("fmv", [P, 2]), sb("fcol", [P, 4])

        sems = {n: sem(n) for n in SIGNALS}
        nums = [s.num for s in sems.values()]
        assert max(nums) - min(nums) == len(nums) - 1

        with nc.Block() as block:
            @block.vector
            def _(dve):
                for v in (*sv, *cv):
                    dve.memset(v[:, :, :, HD:HD + 1], 1.0)

        def one_iteration(i, st):
            C = Counts(st)
            upto, step = C.upto, C.step
            (shared_full, shared_read, cscore_full, cscore_read, sscore_full, sscore_read, smax, sexp, sbias, cbias,
             cexp, topk, spT_full, spT_read, so_full, so_recip, so_norm, cpT_full, cpT_read, crest, cprob, co_full,
             co_recip, co_norm, sq_done, rstd_done, shat_done, sumsq_done, dve_rows, pool_rows, feed_stats, feed_pool,
             h_dve, h_pool, rmax_done, wa_in, wc_in) = (sems[n] for n in SIGNALS[:37])
            feed_in = [sems[f"feed_in{k}"] for k in range(4)]
            xres_in, x1res_in, x1_out, x2_out, x2res_in, y_out = (sems[n] for n in (
                "xres_in", "x1res_in", "x1_out", "x2_out", "x2res_in", "y_out"))
            def rows(ap, b, t):
                return ap[bass.ds(b * S + t * P, P), :]

            fs = all_feeds(st)
            ring = {f: n for n, f in enumerate(fs)}
            normed = [f for f in fs if f[1] != "ctx"]
            for f in fs:
                C.plan(f"feed_in{ring[f] % 4}", f)
            for f in normed:
                for k in range(2):
                    C.plan("feed_stats", (f, k))
                for k in range(5):
                    C.plan("feed_pool", (f, k))
            for s in range(SLOTS):
                for g in groups_self(st, s, 1):
                    C.plan("wa_in", g)
                    C.plan("sq_done", g)
                    C.plan("sumsq_done", g)
                    C.plan("rstd_done", (g, 0))
                    C.plan("rstd_done", (g, 1))
                    C.plan("shat_done", g)
                for g in groups_cross(st, s, 2):
                    C.plan("wc_in", g)
            for t in range(NT):
                if st.proj1:
                    C.plan("xres_in", t)
                    C.plan("x1_out", t)
                if st.mlp:
                    C.plan("x1res_in", t)
                    C.plan("x2_out", t)
                    C.plan("x2res_in", t)
                    C.plan("y_out", t)
            for s in range(SLOTS):
                if s < NT:
                    if st.mlp:
                        for k in ("x2", "stats", "aggr"):
                            C.plan("dve_rows", (k, s))
                        for k in range(6):
                            C.plan("pool_rows", ("ln", s, k))
                    if st.proj1:
                        C.plan("dve_rows", ("x1", s))
                    if st.mlp:
                        C.plan("dve_rows", ("amax", s))
                        C.plan("dve_rows", ("clip", s))
                        C.plan("dve_rows", ("inv", s))
                        for k in range(3):
                            C.plan("pool_rows", ("quant", s, k))
                for t, n in mlp_chunks(st, s):
                    C.plan("h_pool", ("t1", t, n))
                    C.plan("h_pool", ("r", t, n))
                    C.plan("h_dve", ("h", t, n))
                    C.plan("h_dve", ("max", t, n))
                    if n == NF - 1:
                        for k in ("amax", "clip", "inv"):
                            C.plan("h_dve", (k, t))
                        C.plan("h_pool", ("scale", t))
                        for q in range(NF):
                            C.plan("h_pool", ("q", t, q))
                for t in mlp_down(st, s):
                    C.plan("h_dve", ("out", t))

            def freed(eng, u):
                b = C.before[u]
                if b is None:
                    return
                if b[0] in ACT_READS:
                    eng.wait_ge(shared_read, upto("shared_read", (b, ACT_READS[b[0]] - 1)))
                elif b[0] == "cross_out":
                    eng.wait_ge(dve_rows, upto("dve_rows", ("x2", b[1])))
                elif b[0] == "self_out":
                    eng.wait_ge(dve_rows, upto("dve_rows", ("x1", b[1])))
                elif b[0] == "up":
                    eng.wait_ge(h_dve, upto("h_dve", ("h", b[1], b[2])))
                else:
                    eng.wait_ge(h_dve, upto("h_dve", ("out", b[1])))

            def four(ap):
                return ap.rearrange("p (c n) -> p c n", c=4)

            with nc.Block() as block:
                @block.sync
                def _(sp):
                    def load_wa(g):
                        if g > 1:
                            sp.wait_ge(shared_full, upto("shared_full", ("self_qkv", g - 1, NT - 1)))
                        sp.dma_start(wa[:].rearrange("p c (k n) -> p c k n", k=3), wa_dram[g % NG]).then_inc(
                            wa_in, step("wa_in", g, 16))

                    def load_wc(g):
                        if g > 1:
                            sp.wait_ge(shared_full, upto("shared_full", ("cross_qkv", g - 1, NT - 1)))
                        sp.dma_start(wc[:].rearrange("p c (k n) -> p c k n", k=3), wc_dram[g % NG]).then_inc(
                            wc_in, step("wc_in", g, 16))

                    def load_feed(f):
                        k, src, t = f
                        n = ring[f]
                        if n >= 4:
                            sp.wait_ge(shared_full, upto("shared_full", ("feed", *fs[n - 4])))
                        if src == "x1":
                            sp.wait_ge(x1_out, upto("x1_out", NT - 1, 16))
                        a, b = {"x": (x_rows, i + 1), "x1": (x1_rows, i - 1), "ctx": (ctx_rows, i - 1)}[src]
                        sp.dma_start(feed[n % 4][:], rows(a, b, t)).then_inc(feed_in[n % 4], step(f"feed_in{n % 4}", f, 16))

                    pending = list(fs)
                    for s in range(SLOTS):
                        if s == 0 and st.self_now:
                            load_wa(1)
                        if s == 0 and st.cross_now:
                            load_wc(1)
                        if 1 <= s <= NT and st.mlp:
                            sp.wait_ge(dve_rows, upto("dve_rows", ("x2", s - 1)))
                            sp.dma_start(rows(x2_rows, i - 3, s - 1), x2t[:]).then_inc(x2_out, step("x2_out", s - 1, 16))
                        if s < NT and st.mlp:
                            sp.dma_start(x1res[:], rows(x1_rows, i - 3, s)).then_inc(x1res_in, step("x1res_in", s, 16))
                        if 1 <= s <= NT and st.proj1:
                            sp.wait_ge(dve_rows, upto("dve_rows", ("x1", s - 1)))
                            sp.dma_start(rows(x1_rows, i - 1, s - 1), xres[:]).then_inc(x1_out, step("x1_out", s - 1, 16))
                        if s < NT and st.proj1:
                            if s:
                                sp.wait_ge(x1_out, upto("x1_out", s - 1, 16))
                            sp.dma_start(xres[:], rows(x_rows, i - 1, s)).then_inc(xres_in, step("xres_in", s, 16))
                        for g in range(2, NG + 1):
                            if groups_self(st, s + 3, 1) == [g]:
                                load_wa(g)
                            if groups_cross(st, s + 3, 2) == [g]:
                                load_wc(g)
                        for t in mlp_down(st, s - 1):
                            sp.wait_ge(h_dve, upto("h_dve", ("out", t)))
                            sp.dma_start(rows(out_rows, i - 3, t), x2res[:]).then_inc(y_out, step("y_out", t, 16))
                        for t in mlp_down(st, s):
                            if t == 0:
                                sp.wait_ge(x2_out, upto("x2_out", NT - 1, 16))
                            else:
                                sp.wait_ge(y_out, upto("y_out", t - 1, 16))
                            sp.dma_start(x2res[:], rows(x2_rows, i - 3, t)).then_inc(x2res_in, step("x2res_in", t, 16))
                        while pending and s >= 7 and (ring[pending[0]] < 4 or ring[pending[0]] - 4 in
                                                      [ring[f] for q in range(s) for f in feeds(st, q)]):
                            load_feed(pending.pop(0))
                    while pending:
                        load_feed(pending.pop(0))
                    if st.proj1:
                        sp.wait_ge(x1_out, 16 * NT)
                    if st.mlp:
                        sp.wait_ge(x2_out, 16 * NT)
                        sp.wait_ge(y_out, 16 * NT)

                @block.tensor
                def _(pe):
                    def probs_self(m, j):
                        qt = m % NT
                        pe.wait_ge(sexp, upto("sexp", (m, j)))
                        if j:
                            pe.wait_ge(spT_read, upto("spT_read", (m, j - 1)))
                        elif m - 1 in C.apply_self:
                            pe.wait_ge(spT_read, upto("spT_read", (m - 1, HG - 1)))
                        for k in range(qt + 1):
                            mm = pe.transpose(spT_ps[:, k * P:(k + 1) * P], sP[j][:, k * P:(k + 1) * P], ident[:])
                        mm.then_inc(spT_full, step("spT_full", (m, j)))

                    def values_self(m, j):
                        qt, g = m % NT, (m // NT) % NG
                        pe.wait_ge(spT_read, upto("spT_read", (m, j)))
                        if j == 0 and m - 1 in C.apply_self:
                            pe.wait_ge(so_norm, upto("so_norm", m - 1))
                        for k in range(qt + 1):
                            mm = pe.matmul(so_ps[:, j * (HD + 1):(j + 1) * (HD + 1)], sPT[j % 2][:, k * P:(k + 1) * P],
                                           sv[g % 2][:, k, j, :], start=k == 0, stop=k == qt)
                        if j == HG - 1:
                            mm.then_inc(so_full, step("so_full", m))

                    def scores_self(s, j):
                        qt = s % NT
                        if j:
                            pe.wait_ge(sscore_read, upto("sscore_read", (s, j - 1)))
                        elif s:
                            pe.wait_ge(sscore_read, upto("sscore_read", (s - 1, HG - 1)))
                            if qt == 0:
                                pe.wait_ge(shared_read, upto("shared_read", (("self_T", s // NT, 1), 0)))
                        h = slice(j * HD, (j + 1) * HD)
                        pe.matmul(sscore_ps[:, 0:(qt + 1) * P], sqT[h, qt * P:(qt + 1) * P], skT[h, 0:(qt + 1) * P],
                                  start=True, stop=False)
                        pe.matmul(sscore_ps[:, qt * P:(qt + 1) * P], ident16[:], mask16[:], start=False,
                                  stop=True).then_inc(sscore_full, step("sscore_full", (s, j)))

                    def probs_cross(m, j):
                        pe.wait_ge(cprob, upto("cprob", (m, j)))
                        if j:
                            pe.wait_ge(cpT_read, upto("cpT_read", (m, j - 1)))
                        elif m - 1 in C.apply_cross:
                            pe.wait_ge(cpT_read, upto("cpT_read", (m - 1, HG - 1)))
                        for k in range(NT):
                            mm = pe.transpose(cpT_ps[:, k * P:(k + 1) * P], cS[m % 2][j][:, k * P:(k + 1) * P], ident[:])
                        mm.then_inc(cpT_full, step("cpT_full", (m, j)))

                    def values_cross(m, j):
                        g = (m // NT) % NG
                        pe.wait_ge(cpT_read, upto("cpT_read", (m, j)))
                        if j == 0 and m - 1 in C.apply_cross:
                            pe.wait_ge(co_norm, upto("co_norm", m - 1))
                        for k in range(NT):
                            mm = pe.matmul(co_ps[:, j * (HD + 1):(j + 1) * (HD + 1)], cPT[j % 2][:, k * P:(k + 1) * P],
                                           cv[g % 2][:, k, j, :], start=k == 0, stop=k == NT - 1)
                        if j == HG - 1:
                            mm.then_inc(co_full, step("co_full", m))

                    def scores_cross(n, j):
                        qt = n % NT
                        if j:
                            pe.wait_ge(cscore_read, upto("cscore_read", (n, j - 1)))
                        else:
                            pe.wait_ge(cscore_read, upto("cscore_read", (n - 1, HG - 1)))
                            if qt == 0:
                                pe.wait_ge(shared_read, upto("shared_read", (("cross_T", n // NT, 1), 0)))
                        h = slice(j * HD, (j + 1) * HD)
                        pe.matmul(cscore_ps[:], cqT[h, qt * P:(qt + 1) * P], ckT[h, :], start=True,
                                  stop=True).then_inc(cscore_full, step("cscore_full", (n, j)))

                    def turn(ps, src):
                        for c in range(4):
                            mm = pe.transpose(ps[:, c * P:(c + 1) * P], src(c), ident[:])
                        return mm

                    def unit(u, s):
                        ps = shared_ps[C.bank[u]]
                        freed(pe, u)
                        kind = u[0]
                        if kind == "cross_oT":
                            if s - 1 in C.apply_cross and s >= 1:
                                pass
                            if u[1] == NT - 1:
                                pe.wait_ge(co_norm, upto("co_norm", -1))
                            mm = turn(ps, lambda c: co[:, u[1], c * P:(c + 1) * P])
                        elif kind == "self_oT":
                            if u[1] == NT - 1:
                                pe.wait_ge(so_norm, upto("so_norm", -1))
                            mm = turn(ps, lambda c: so[:, u[1], c * P:(c + 1) * P])
                        elif kind in ("cross_out", "self_out"):
                            oT, w, b = (cross_oT, woT, D) if kind == "cross_out" else (self_oT, wproj, 0)
                            pe.matmul(ps[:], ones16[64:67, :], bias16[64:67, b:b + D], start=True, stop=False)
                            pe.wait_ge(shared_read, upto("shared_read", ((kind[:-3] + "oT", u[1]), 0)))
                            for c in range(NC):
                                mm = pe.matmul(ps[:], oT[:, c, :], w[:, c, :], start=False, stop=c == NC - 1)
                        elif kind == "x2T":
                            pe.wait_ge(pool_rows, upto("pool_rows", ("quant", u[1], 2)))
                            mm = turn(ps, lambda c: x2h[:, c * P:(c + 1) * P])
                        elif kind in ("gate", "up"):
                            w = wgT if kind == "gate" else wuT
                            pe.wait_ge(shared_read, upto("shared_read", (("x2T", u[1]), 0)))
                            for c in range(NC):
                                mm = pe.matmul(ps[:], x2T[:, u[1], c, :], w[:, c, u[2] * 512:(u[2] + 1) * 512],
                                               start=c == 0, stop=c == NC - 1)
                        elif kind == "hT":
                            pe.wait_ge(h_pool, upto("h_pool", ("q", u[1], u[2])))
                            mm = turn(ps, lambda c: hh[:, u[2], c * P:(c + 1) * P])
                        elif kind == "down":
                            pe.wait_ge(shared_read, upto("shared_read", (("hT", u[1], NF - 1), 0)))
                            for c in range(KF):
                                mm = pe.matmul(ps[:], hT[:, c, :], wdT[:, c, :], start=c == 0, stop=c == KF - 1)
                        elif kind == "self_qkv":
                            g, t = u[1], u[2]
                            if t == 0:
                                pe.wait_ge(wa_in, upto("wa_in", g, 16))
                                if g == NG:
                                    pe.wait_ge(shared_read, upto("shared_read", (("feed", 3, "x", 3), 0)))
                            lo = 0
                            for part in range(3):
                                at = part * D + (g % NG) * P
                                pe.matmul(ps[:, part * P:(part + 1) * P], ones16[0:3, :], bias16[0:3, at:at + P],
                                          start=part == 0, stop=False, skip_group_check=True)
                            for c in range(NC):
                                mm = pe.matmul(ps[:, 0:3 * P], xT[:, c, t * P:(t + 1) * P], wa[:, c, :], start=False,
                                               stop=c == NC - 1, skip_group_check=True)
                        elif kind == "cross_qkv":
                            g, t = u[1], u[2]
                            if t == 0:
                                pe.wait_ge(wc_in, upto("wc_in", g, 16))
                                if g == NG:
                                    pe.wait_ge(shared_read, upto("shared_read", (("feed", 11, "ctx", 3), 0)))
                            at = (g % NG) * 3 * P
                            pe.matmul(ps[:, 0:3 * P], ones16[32:35, :], bias16[32:35, at:at + 3 * P], start=True, stop=False)
                            for c in range(NC):
                                pe.matmul(ps[:, 0:P], x1T[:, c, t * P:(t + 1) * P], wc[:, c, 0:P], start=False, stop=False)
                            for c in range(NC):
                                mm = pe.matmul(ps[:, P:3 * P], ctxT[:, c, t * P:(t + 1) * P], wc[:, c, P:3 * P],
                                               start=False, stop=c == NC - 1)
                        elif kind == "self_T":
                            pe.wait_ge(shat_done, upto("shat_done", u[1]))
                            mm = turn(ps, lambda c: sqk[:, c, u[2] * P:(u[2] + 1) * P])
                        elif kind == "cross_T":
                            pe.wait_ge(shared_read, upto("shared_read", (("cross_qkv", u[1], NT - 1), 1)))
                            mm = turn(ps, lambda c: cqk[:, c, u[2] * P:(u[2] + 1) * P])
                        else:
                            f = u[1:]
                            n = ring[f]
                            if f[1] == "ctx":
                                pe.wait_ge(feed_in[n % 4], upto(f"feed_in{n % 4}", f, 16))
                            else:
                                pe.wait_ge(feed_pool, upto("feed_pool", (f, 4)))
                            mm = turn(ps, lambda c: feed[n % 4][:, c * P:(c + 1) * P])
                        mm.then_inc(shared_full, step("shared_full", u))

                    for s in range(SLOTS):
                        for j in range(HG):
                            if s - 1 in C.apply_self:
                                probs_self(s - 1, j)
                            if st.self_now:
                                scores_self(s, j)
                            if s - 1 in C.apply_self:
                                values_self(s - 1, j)
                        for u in shared_units(st, s):
                            unit(u, s)
                        for j in range(HG):
                            if s - 1 in C.apply_cross:
                                probs_cross(s - 1, j)
                            if st.cross_now if s < SLOTS - 1 else st.cross_next:
                                scores_cross(s + 1, j)
                            if s - 1 in C.apply_cross:
                                values_cross(s - 1, j)

                @block.scalar
                def _(act):
                    def unit(u):
                        ps = shared_ps[C.bank[u]]
                        kind = u[0]
                        act.wait_ge(shared_full, upto("shared_full", u))

                        def read(k, *a, **kw):
                            return act.activation(*a, **kw).then_inc(shared_read, step("shared_read", (u, k)))
                        if kind in ("cross_oT", "self_oT"):
                            if u[1]:
                                act.wait_ge(shared_full, upto("shared_full", (kind[:-2] + "out", u[1] - 1)))
                            read(0, (cross_oT if kind == "cross_oT" else self_oT)[:], four(ps[:]), ACT.Copy)
                        elif kind == "x2T":
                            read(0, x2T[:, u[1], :, :], four(ps[:]), ACT.Copy, bias=-MAGIC)
                        elif kind == "gate":
                            if (u[1], u[2]) != (0, 0):
                                prev = (u[1], u[2] - 1) if u[2] else (u[1] - 1, NF - 1)
                                act.wait_ge(h_dve, upto("h_dve", ("h", *prev)))
                            act.wait_ge(pool_rows, upto("pool_rows", ("quant", u[1], 1)))
                            read(0, th[:], ps[:], ACT.Tanh, scale=gate_scale[:, u[1], 0:1])
                            read(1, gc[:], ps[:], ACT.Copy, scale=gate_scale[:, u[1], 1:2])
                        elif kind == "hT":
                            if u[1] and not u[2]:
                                act.wait_ge(shared_full, upto("shared_full", ("down", u[1] - 1)))
                            read(0, hT[:, 4 * u[2]:4 * u[2] + 4, :], four(ps[:]), ACT.Copy, bias=-MAGIC)
                        elif kind in ("self_qkv", "cross_qkv"):
                            g, t = u[1], u[2]
                            qk, v = (sqk, sv) if kind == "self_qkv" else (cqk, cv)
                            if t == 0:
                                act.wait_ge(shared_full, upto("shared_full", (kind[:-3] + "T", g - 1, 1)))
                            read(0, qk[:, t, :], ps[:, 0:2 * P], ACT.Copy)
                            if t == 0 and g >= 2:
                                full, name = (so_full, "so_full") if kind == "self_qkv" else (co_full, "co_full")
                                act.wait_ge(full, upto(name, 4 * (g - 1) - 1))
                            read(1, v[g % 2][:, t, :, 0:HD], ps[:, 2 * P:3 * P].rearrange("p (h d) -> p h d", h=HG), ACT.Copy)
                        elif kind == "self_T":
                            read(0, (sqT, skT)[u[2]][:], ps[:], ACT.Identity, scale=gb[:, 2 * u[2]:2 * u[2] + 1],
                                 bias=gb[:, 2 * u[2] + 1:2 * u[2] + 2])
                        elif kind == "cross_T":
                            read(0, (cqT, ckT)[u[2]][:], ps[:], ACT.Copy)
                        elif kind == "feed":
                            dst = {"x": xT, "x1": x1T, "ctx": ctxT}[u[2]]
                            read(0, dst[:, :, u[3] * P:(u[3] + 1) * P], four(ps[:]), ACT.Copy)

                    for s in range(SLOTS):
                        m = s - 1
                        if m in C.apply_cross:
                            for j in range(HG):
                                act.wait_ge(topk, upto("topk", (m, ROUNDS - 1, "replace", j)))
                                act.activation(cW[j][:], cW[j][:], ACT.Exp, bias=cnb[m % 2][:, j:j + 1],
                                               scale=SCALE).then_inc(crest, step("crest", (m, j)))
                        for j in range(HG):
                            if m in C.apply_self:
                                n = (m % NT + 1) * P
                                act.wait_ge(spT_full, upto("spT_full", (m, j)))
                                act.activation(sPT[j % 2][:, 0:n], spT_ps[:, 0:n], ACT.Copy).then_inc(spT_read, step("spT_read", (m, j)))
                            if st.self_now:
                                n = (s % NT + 1) * P
                                act.wait_ge(sscore_full, upto("sscore_full", (s, j)))
                                act.activation(sP[j][:, 0:n], sscore_ps[:, 0:n], ACT.Copy).then_inc(sscore_read, step("sscore_read", (s, j)))
                        if st.cross_now:
                            act.wait_ge(cbias, upto("cbias", s))
                            for j in range(HG):
                                act.wait_ge(topk, upto("topk", (s, 0, "replace", j)))
                                act.activation(cS[s % 2][j][:], cS[s % 2][j][:], ACT.Exp, bias=cnb[s % 2][:, j:j + 1],
                                               scale=SCALE).then_inc(cexp, step("cexp", (s, j)))
                        units = [u for u in shared_units(st, s) if u[0] in ACT_READS]
                        for u in units:
                            unit(u)
                        if st.self_now:
                            n = (s % NT + 1) * P
                            act.wait_ge(sbias, upto("sbias", s))
                            for j in range(HG):
                                act.activation(sP[j][:, 0:n], sP[j][:, 0:n], ACT.Exp, bias=snb[:, j:j + 1],
                                               scale=SCALE).then_inc(sexp, step("sexp", (s, j)))
                        for j in range(HG):
                            if m in C.apply_cross:
                                act.wait_ge(cpT_full, upto("cpT_full", (m, j)))
                                act.activation(cPT[j % 2][:], cpT_ps[:], ACT.Copy).then_inc(cpT_read, step("cpT_read", (m, j)))
                            if st.cross_now if s < SLOTS - 1 else st.cross_next:
                                act.wait_ge(cscore_full, upto("cscore_full", (s + 1, j)))
                                act.activation(cS[(s + 1) % 2][j][:], cscore_ps[:], ACT.Copy).then_inc(
                                    cscore_read, step("cscore_read", (s + 1, j)))

                @block.vector
                def _(dve):
                    def top_round(s, r):
                        for j in range(HG):
                            src = cS[s % 2][j] if r == 0 else cW[j]
                            if r == 0:
                                dve.wait_ge(cscore_read, upto("cscore_read", (s, j)))
                                if s:
                                    dve.wait_ge(cbias, upto("cbias", s - 1))
                                    dve.wait_ge(topk, upto("topk", (s - 1, ROUNDS - 1, "replace", j)))
                            else:
                                dve.wait_ge(topk, upto("topk", (s, r - 1, "replace", j)))
                            dve.max(top8[:, j, :], src[:]).then_inc(topk, step("topk", (s, r, "max", j)))
                        if r == 0:
                            for j in range(1):
                                dve.wait_ge(topk, upto("topk", (s, 0, "max", HG - 1)))
                                dve.wait_ge(cbias, upto("cbias", s - 1))
                                dve.tensor_copy(rowmax[:], top8[:, :, 0]).then_inc(rmax_done, step("rmax", s))
                        for j in range(HG):
                            src = cS[s % 2][j] if r == 0 else cW[j]
                            dve.wait_ge(topk, upto("topk", (s, r, "max", j)))
                            if r == 0:
                                dve.wait_ge(cprob, upto("cprob", (s - 1, j)))
                            dve.match_replace(cW[j][:], top8[:, j, :], src[:], REPLACED).then_inc(
                                topk, step("topk", (s, r, "replace", j)))

                    def norm(m, ps, full, recip, done, r_t, o_t, name):
                        qt, g = m % NT, (m // NT) % NG
                        dve.wait_ge(full, upto(name + "_full", m))
                        o = ps[:, 0:HG * (HD + 1)].rearrange("p (h d) -> p h d", h=HG)
                        dve.wait_ge(done, upto(name + "_norm", m - 1))
                        dve.reciprocal(r_t[:], o[:, :, HD]).then_inc(recip, step(name + "_recip", m))
                        dve.wait_ge(recip, upto(name + "_recip", m))
                        if m >= 0 and g == 0:
                            dve.wait_ge(shared_full, upto("shared_full", (("cross_oT" if name == "co" else "self_oT"), qt)))
                        dve.tensor_tensor(o_t[:, qt, g * P:(g + 1) * P].rearrange("p (h d) -> p h d", h=HG), o[:, :, 0:HD],
                                          r_t[:].unsqueeze(2).to_broadcast([P, HG, HD]), ALU.mult).then_inc(
                                              done, step(name + "_norm", m))

                    def rows_now(s):
                        if s >= NT:
                            return
                        if st.mlp:
                            dve.wait_ge(shared_full, upto("shared_full", ("cross_out", s)))
                            dve.wait_ge(x1res_in, upto("x1res_in", s, 16))
                            if s:
                                dve.wait_ge(x2_out, upto("x2_out", s - 1, 16))
                                dve.wait_ge(pool_rows, upto("pool_rows", ("ln", s - 1, 5)))
                            dve.tensor_tensor(x2t[:], shared_ps[C.bank[("cross_out", s)]][:], x1res[:], ALU.add).then_inc(
                                dve_rows, step("dve_rows", ("x2", s)))
                            dve.wait_ge(dve_rows, upto("dve_rows", ("x2", s)))
                            dve.bn_stats(mstat[:], x2t[:]).then_inc(dve_rows, step("dve_rows", ("stats", s)))
                            dve.wait_ge(dve_rows, upto("dve_rows", ("stats", s)))
                            dve.bn_aggr(mv[:], mstat[:]).then_inc(dve_rows, step("dve_rows", ("aggr", s)))
                        if st.proj1:
                            dve.wait_ge(shared_full, upto("shared_full", ("self_out", s)))
                            dve.wait_ge(xres_in, upto("xres_in", s, 16))
                            dve.tensor_tensor(xres[:], shared_ps[C.bank[("self_out", s)]][:], xres[:], ALU.add).then_inc(
                                dve_rows, step("dve_rows", ("x1", s)))

                    def amax(s):
                        if s >= NT or not st.mlp:
                            return
                        dve.wait_ge(pool_rows, upto("pool_rows", ("ln", s, 5)))
                        if s:
                            dve.wait_ge(pool_rows, upto("pool_rows", ("quant", s - 1, 2)))
                        dve.tensor_reduce(up_amax[:, s:s + 1], x2h[:], AXX, ALU.max, apply_absolute_value=True).then_inc(
                            dve_rows, step("dve_rows", ("amax", s)))
                        dve.wait_ge(dve_rows, upto("dve_rows", ("amax", s)))
                        dve.tensor_scalar(up_amax[:, s:s + 1], up_amax[:, s:s + 1], 1e-5, 1.0 / 127.0, ALU.max, ALU.mult).then_inc(
                            dve_rows, step("dve_rows", ("clip", s)))
                        dve.wait_ge(dve_rows, upto("dve_rows", ("clip", s)))
                        dve.reciprocal(mcol[:, 7:8], up_amax[:, s:s + 1]).then_inc(dve_rows, step("dve_rows", ("inv", s)))

                    def mlp(s):
                        for t, n in mlp_chunks(st, s):
                            dve.wait_ge(shared_full, upto("shared_full", ("up", t, n)))
                            dve.wait_ge(h_pool, upto("h_pool", ("r", t, n)))
                            if t and n == 0:
                                dve.wait_ge(shared_full, upto("shared_full", ("hT", t - 1, NF - 1)))
                            dve.tensor_tensor(hh[:, n, :], shared_ps[C.bank[("up", t, n)]][:], gc[:], ALU.mult).then_inc(
                                h_dve, step("h_dve", ("h", t, n)))
                            dve.wait_ge(h_dve, upto("h_dve", ("h", t, n)))
                            dve.tensor_reduce(hmx[:, n:n + 1], hh[:, n, :], AXX, ALU.max, apply_absolute_value=True).then_inc(
                                h_dve, step("h_dve", ("max", t, n)))
                            if n == NF - 1:
                                dve.wait_ge(h_dve, upto("h_dve", ("max", t, n)))
                                if t:
                                    dve.wait_ge(h_pool, upto("h_pool", ("q", t - 1, NF - 1)))
                                dve.tensor_reduce(hcol[:, 0:1], hmx[:], AXX, ALU.max).then_inc(h_dve, step("h_dve", ("amax", t)))
                                dve.wait_ge(h_dve, upto("h_dve", ("amax", t)))
                                dve.tensor_scalar(hcol[:, 1:2], hcol[:, 0:1], 1e-5, 1.0 / 127.0, ALU.max, ALU.mult).then_inc(
                                    h_dve, step("h_dve", ("clip", t)))
                                dve.wait_ge(h_dve, upto("h_dve", ("clip", t)))
                                dve.reciprocal(hcol[:, 2:3], hcol[:, 1:2]).then_inc(h_dve, step("h_dve", ("inv", t)))

                    def down(s):
                        for t in mlp_down(st, s):
                            dve.wait_ge(shared_full, upto("shared_full", ("down", t)))
                            dve.wait_ge(x2res_in, upto("x2res_in", t, 16))
                            dve.wait_ge(h_pool, upto("h_pool", ("scale", t)))
                            dve.scalar_tensor_tensor(x2res[:], shared_ps[C.bank[("down", t)]][:], hcol[:, 3:4], x2res[:],
                                                     ALU.mult, ALU.add).then_inc(h_dve, step("h_dve", ("out", t)))

                    def feed_stats_of(s):
                        for f in feeds(st, s + 1):
                            if f[1] == "ctx":
                                continue
                            n, p = ring[f], normed.index(f)
                            dve.wait_ge(feed_in[n % 4], upto(f"feed_in{n % 4}", f, 16))
                            if p:
                                dve.wait_ge(feed_stats, upto("feed_stats", (normed[p - 1], 1)))
                            dve.bn_stats(fstat[:], feed[n % 4][:]).then_inc(feed_stats, step("feed_stats", (f, 0)))
                            dve.wait_ge(feed_stats, upto("feed_stats", (f, 0)))
                            if p:
                                dve.wait_ge(feed_pool, upto("feed_pool", (normed[p - 1], 4)))
                            dve.bn_aggr(fmv[:], fstat[:]).then_inc(feed_stats, step("feed_stats", (f, 1)))

                    for s in range(SLOTS):
                        if st.cross_now:
                            top_round(s, 0)
                        if s - 1 in C.apply_self:
                            norm(s - 1, so_ps, so_full, so_recip, so_norm, so_r, so, "so")
                        if st.cross_now:
                            top_round(s, 1)
                        if st.self_now:
                            n = (s % NT + 1) * P
                            for j in range(HG):
                                dve.wait_ge(sscore_read, upto("sscore_read", (s, j)))
                                if j == 0 and s:
                                    dve.wait_ge(sbias, upto("sbias", s - 1))
                                    dve.wait_ge(smax, upto("smax", (s - 1, HG - 1)))
                                dve.reduce_max(smx[:, j:j + 1], sP[j][:, 0:n], AXX).then_inc(smax, step("smax", (s, j)))
                        rows_now(s)
                        if st.cross_now:
                            top_round(s, 2)
                        mlp(s)
                        amax(s)
                        for g in groups_self(st, s, 2):
                            dve.wait_ge(sq_done, upto("sq_done", g))
                            dve.wait_ge(shat_done, upto("shat_done", g - 1))
                            dve.tensor_reduce(srs[:], ssq[:].rearrange("p t (h d) -> p (t h) d", d=HD), AXX, ALU.add).then_inc(
                                sumsq_done, step("sumsq_done", g))
                        if st.cross_now:
                            top_round(s, 3)
                        down(s)
                        feed_stats_of(s)
                        if s - 1 in C.apply_cross:
                            norm(s - 1, co_ps, co_full, co_recip, co_norm, co_r, co, "co")

                @block.gpsimd
                def _(pool):
                    def layer_norm(src, dst, mvt, col, name, sem_, label, ready):
                        ready()
                        pool.tensor_scalar(col[:, 0:1], mvt[:, 1:2], 1.0, EPS, ALU.mult, ALU.add).then_inc(sem_, step(name, label(0)))
                        pool.wait_ge(sem_, upto(name, label(0)))
                        pool.tensor_tensor(col[:, 1:2], col[:, 0:1], minus_half[:, 0:1], ALU.pow).then_inc(sem_, step(name, label(1)))
                        pool.wait_ge(sem_, upto(name, label(1)))
                        pool.tensor_tensor(col[:, 2:3], mvt[:, 0:1], col[:, 1:2], ALU.mult).then_inc(sem_, step(name, label(2)))
                        pool.wait_ge(sem_, upto(name, label(2)))
                        pool.tensor_scalar(col[:, 3:4], col[:, 2:3], -1.0, 0.0, ALU.mult, ALU.add).then_inc(sem_, step(name, label(3)))
                        pool.wait_ge(sem_, upto(name, label(3)))
                        return pool.tensor_scalar(dst, src, col[:, 1:2], col[:, 3:4], ALU.mult, ALU.add)

                    def rows_ln(s):
                        if s >= NT or not st.mlp:
                            return

                        def ready():
                            pool.wait_ge(dve_rows, upto("dve_rows", ("aggr", s)))
                            if s:
                                pool.wait_ge(shared_full, upto("shared_full", ("x2T", s - 1)))
                                pool.wait_ge(pool_rows, upto("pool_rows", ("quant", s - 1, 2)))
                        layer_norm(x2t[:], x2h[:], mv, mcol, "pool_rows", pool_rows, lambda k: ("ln", s, k), ready).then_inc(
                            pool_rows, step("pool_rows", ("ln", s, 4)))
                        pool.wait_ge(pool_rows, upto("pool_rows", ("ln", s, 4)))
                        pool.tensor_scalar(mcol[:, 4:5], wscale[:, 0:1], 0.5, 0.0, ALU.mult, ALU.add).then_inc(
                            pool_rows, step("pool_rows", ("ln", s, 5)))

                    def rows_quant(s):
                        if s >= NT or not st.mlp:
                            return
                        pool.wait_ge(dve_rows, upto("dve_rows", ("inv", s)))
                        pool.wait_ge(pool_rows, upto("pool_rows", ("ln", s, 5)))
                        pool.tensor_tensor(gate_scale[:, s, 0:1], up_amax[:, s:s + 1], mcol[:, 4:5], ALU.mult).then_inc(
                            pool_rows, step("pool_rows", ("quant", s, 0)))
                        pool.wait_ge(pool_rows, upto("pool_rows", ("quant", s, 0)))
                        pool.tensor_scalar(gate_scale[:, s, 1:2], gate_scale[:, s, 0:1], up_amax[:, s:s + 1], wscale[:, 1:2],
                                           ALU.mult, ALU.mult).then_inc(pool_rows, step("pool_rows", ("quant", s, 1)))
                        pool.tensor_scalar(x2h[:], x2h[:], mcol[:, 7:8], MAGIC, ALU.mult, ALU.add).then_inc(
                            pool_rows, step("pool_rows", ("quant", s, 2)))

                    for s in range(SLOTS):
                        m = s - 1
                        if m in C.apply_cross:
                            for j in range(HG):
                                pool.wait_ge(crest, upto("crest", (m, j)))
                                pool.tensor_tensor(cS[m % 2][j][:], cS[m % 2][j][:], cW[j][:], ALU.subtract).then_inc(
                                    cprob, step("cprob", (m, j)))
                        if st.cross_now:
                            pool.wait_ge(rmax_done, upto("rmax", s))
                            if s:
                                pool.wait_ge(crest, upto("crest", (s - 2, HG - 1)))
                            pool.tensor_scalar(cnb[s % 2][:], rowmax[:], -SCALE, 0.0, ALU.mult, ALU.add).then_inc(
                                cbias, step("cbias", s))
                        if st.self_now:
                            pool.wait_ge(smax, upto("smax", (s, HG - 1)))
                            if s:
                                pool.wait_ge(sexp, upto("sexp", (s - 1, HG - 1)))
                            pool.tensor_scalar(snb[:], smx[:], -SCALE, 0.0, ALU.mult, ALU.add).then_inc(sbias, step("sbias", s))
                        rows_ln(s)
                        for t, n in mlp_chunks(st, s):
                            pool.wait_ge(shared_read, upto("shared_read", (("gate", t, n), 1)))
                            pool.tensor_scalar(th[:], th[:], 1.0, 1.0, ALU.add, ALU.mult).then_inc(h_pool, step("h_pool", ("t1", t, n)))
                            pool.wait_ge(h_pool, upto("h_pool", ("t1", t, n)))
                            pool.tensor_tensor(gc[:], gc[:], th[:], ALU.mult).then_inc(h_pool, step("h_pool", ("r", t, n)))
                            if n == NF - 1:
                                pool.wait_ge(h_dve, upto("h_dve", ("inv", t)))
                                if t:
                                    pool.wait_ge(h_dve, upto("h_dve", ("out", t - 1)))
                                pool.tensor_tensor(hcol[:, 3:4], hcol[:, 1:2], wscale[:, 2:3], ALU.mult).then_inc(
                                    h_pool, step("h_pool", ("scale", t)))
                                for q in range(NF):
                                    pool.tensor_scalar(hh[:, q, :], hh[:, q, :], hcol[:, 2:3], MAGIC, ALU.mult, ALU.add).then_inc(
                                        h_pool, step("h_pool", ("q", t, q)))
                        rows_quant(s)
                        for g in groups_self(st, s, 1):
                            pool.wait_ge(shared_read, upto("shared_read", (("self_qkv", g, NT - 1), 0)))
                            pool.wait_ge(sumsq_done, upto("sumsq_done", g - 1))
                            pool.tensor_tensor(ssq[:], sqk[:], sqk[:], ALU.mult).then_inc(sq_done, step("sq_done", g))
                        for g in groups_self(st, s, 2):
                            pool.wait_ge(sumsq_done, upto("sumsq_done", g))
                            pool.tensor_scalar(srs[:], srs[:], 1.0 / HD, EPS, ALU.mult, ALU.add).then_inc(
                                rstd_done, step("rstd_done", (g, 0)))
                            pool.wait_ge(rstd_done, upto("rstd_done", (g, 0)))
                            pool.tensor_tensor(srs[:], srs[:], minus_half[:], ALU.pow).then_inc(
                                rstd_done, step("rstd_done", (g, 1)))
                            pool.wait_ge(rstd_done, upto("rstd_done", (g, 1)))
                            q = sqk[:].rearrange("p t (h d) -> p (t h) d", d=HD)
                            pool.tensor_tensor(q, q, srs[:].unsqueeze(2).to_broadcast([P, 2 * NT * HG, HD]), ALU.mult).then_inc(
                                shat_done, step("shat_done", g))
                        for f in feeds(st, s + 1):
                            if f[1] == "ctx":
                                continue
                            n, p = ring[f], normed.index(f)

                            def ready():
                                pool.wait_ge(feed_stats, upto("feed_stats", (f, 1)))
                                if p:
                                    pool.wait_ge(feed_pool, upto("feed_pool", (normed[p - 1], 4)))
                            layer_norm(feed[n % 4][:], feed[n % 4][:], fmv, fcol, "feed_pool", feed_pool, lambda k: (f, k),
                                       ready).then_inc(feed_pool, step("feed_pool", (f, 4)))

            C.end()

        def iteration(i, st):
            one_iteration(i, st)
            nc.gpsimd.sem_clear(range(min(nums), max(nums) + 1))
            nc.all_engine_barrier()

        steady = [i for i in range(LO, HI + 1) if Stages(i).key() == Stages(3).key()]
        for i in range(LO, steady[0]):
            iteration(i, Stages(i))
        with nc.Fori(steady[0], steady[-1] + 1) as i:
            iteration(i, Stages(steady[0]))
        for i in range(steady[-1] + 1, HI + 1):
            iteration(i, Stages(i))


def setup(nc, T):
    W_attn, b_attn, wa_dram, wc_dram = T["W_attn"], T["b_attn"], T["wa_dram"], T["wc_dram"]
    banks, ident, ident16, mask16, ones16, bias16 = (T[k] for k in ("banks", "ident", "ident16", "mask16", "ones16", "bias16"))
    minus_half, gb, wscale, wproj, woT = (T[k] for k in ("minus_half", "gb", "wscale", "wproj", "woT"))
    wgT, wuT, wdT = T["wgT"], T["wuT"], T["wdT"]
    with ExitStack() as tmp:
        def sb(name, shape, dt=F32):
            return tmp.enter_context(nc.sbuf_tensor(name, shape, dt))

        def sem(name):
            return tmp.enter_context(nc.semaphore(name))

        wnat = sb("wnat", [P, NC, 3 * D])
        hmean = sb("hmean", [P, NC + 1, 2 * H])
        brow = sb("brow", [1, 8 * D])
        bpart = sb("bpart", [1, 3, 8 * D], BF16)
        wx = [sb(f"wx{k}", [P, NC, D]) for k in range(2)]
        wcT = sb("wcT", [P, NC, 3, D])
        ones32 = sb("ones32", [P, P])
        s_const, s_b, s_bp, s_bd, s_w, s_mean, s_cent, s_out = (sem(f"su_{n}") for n in (
            "const", "b", "bp", "bd", "w", "mean", "cent", "out"))
        s_x = [sem(f"su_x{k}") for k in range(2)]
        s_xp, s_xa, s_res = sem("su_xp"), sem("su_xa"), sem("su_res")
        NBIAS = 4 + 3 * NG
        with nc.Block() as block:
            @block.sync
            def _(sp):
                sp.dma_start(wnat[:], W_attn.rearrange("(c p) n -> p c n", p=P)).then_inc(s_w, 16)
                sp.dma_start(brow[:, 0:3 * D], b_attn.rearrange("(a n) -> a n", a=1)).then_inc(s_b, 16)
                for g in range(NG):
                    for k, b in enumerate((T["bq"], T["bk"], T["bv"])):
                        sp.dma_start(brow[:, 3 * D + (3 * g + k) * P:3 * D + (3 * g + k + 1) * P],
                                     b[g * P:(g + 1) * P].rearrange("(a n) -> a n", a=1)).then_inc(s_b, 16)
                for k, b in enumerate((T["b_proj"], T["bo"])):
                    sp.dma_start(brow[:, (6 + k) * D:(7 + k) * D], b.rearrange("(a n) -> a n", a=1)).then_inc(s_b, 16)
                for k, v in enumerate((T["q_gamma"], T["q_beta"], T["k_gamma"], T["k_beta"])):
                    for j in range(HG):
                        sp.dma_start(gb[j * HD:(j + 1) * HD, k:k + 1], v.rearrange("(n a) -> n a", a=1)).then_inc(s_res, 16)
                sp.dma_start(wproj[:], T["W_proj"].rearrange("(c p) n -> p c n", p=P)).then_inc(s_res, 16)
                for k, w in enumerate((T["Wq"], T["Wk"], T["Wv"], T["Wo"])):
                    if k >= 2:
                        sp.wait_ge(s_xp, NC * (k - 1))
                    sp.dma_start(wx[k % 2][:], w.rearrange("(c p) n -> p c n", p=P)).then_inc(s_x[k % 2], 16)
                sp.wait_ge(s_bp, 5)
                for base, lo, n in ((0, 0, 3 * D), (32, 3 * D, 3 * D), (64, 6 * D, 2 * D)):
                    for r in range(3):
                        sp.dma_start(bias16[base + r:base + r + 1, 0:n], bpart[:, r, lo:lo + n]).then_inc(s_bd, 16)
                sp.wait_ge(s_bd, 9 * 16)
                sp.wait_ge(s_cent, 2)
                for g in range(NG):
                    for part in range(3):
                        sp.dma_start(wa_dram[g, :, :, part, :],
                                     wnat[:, :, part * D + g * P:part * D + (g + 1) * P]).then_inc(s_out, 16)
                sp.wait_ge(s_xa, 3 * NC)
                for g in range(NG):
                    for part in range(3):
                        sp.dma_start(wc_dram[g, :, :, part, :],
                                     wcT[:, :, part, g * P:(g + 1) * P]).then_inc(s_out, 16)
                sp.wait_ge(s_out, 2 * 3 * NG * 16)
                sp.wait_ge(s_res, 17 * 16)

            @block.gpsimd
            def _(pool):
                pool.memset(ident[:], 0.0).then_inc(s_const, 1)
                pool.memset(mask16[:], 0.0).then_inc(s_const, 1)
                pool.memset(ones16[:], 1.0)
                pool.memset(ones32[:], 1.0)
                pool.memset(minus_half[:], -0.5)
                pool.wait_ge(s_const, 2)
                pool.affine_select(out=ident[:], in_=ident[:], compare_op=ALU.not_equal, fill=1.0, base=0,
                                   pattern=[[-1, P]], channel_multiplier=1).then_inc(s_const, 1)
                pool.affine_select(out=mask16[:], in_=mask16[:], compare_op=ALU.is_ge, fill=MASKED, base=0,
                                   pattern=[[-1, P]], channel_multiplier=1).then_inc(s_const, 1)
                pool.wait_ge(s_const, 3)
                pool.tensor_copy(ident16[:], ident[:])

            @block.vector
            def _(dve):
                dve.wait_ge(s_w, 16)
                for c in range(NC):
                    dve.tensor_reduce(hmean[:, c, :], wnat[:, c, 0:2 * D].rearrange("p (h d) -> p h d", d=HD),
                                      AXX, ALU.add).then_inc(s_mean, 1)
                dve.wait_ge(s_b, 18 // 1 * 0 + 16 * (1 + 3 * NG + 2))
                dve.tensor_reduce(hmean[0:1, NC, :], brow[:, 0:2 * D].rearrange("p (h d) -> p h d", d=HD),
                                  AXX, ALU.add).then_inc(s_mean, 1)
                dve.wait_ge(s_mean, NC + 1)
                dve.tensor_scalar(hmean[:, 0:NC, :], hmean[:, 0:NC, :], 1.0 / HD, None, ALU.mult).then_inc(s_mean, 1)
                dve.tensor_scalar(hmean[0:1, NC, :], hmean[0:1, NC, :], 1.0 / HD, None, ALU.mult).then_inc(s_mean, 1)
                dve.wait_ge(s_mean, NC + 3)
                for c in range(NC):
                    w = wnat[:, c, 0:2 * D].rearrange("p (h d) -> p h d", d=HD)
                    ins = dve.tensor_tensor(w, w, hmean[:, c, :].unsqueeze(2).to_broadcast([P, 2 * H, HD]), ALU.subtract)
                ins.then_inc(s_cent, 1)
                b = brow[:, 0:2 * D].rearrange("p (h d) -> p h d", d=HD)
                dve.tensor_tensor(b, b, hmean[0:1, NC, :].unsqueeze(2).to_broadcast([1, 2 * H, HD]),
                                  ALU.subtract).then_inc(s_cent, 1)
                dve.wait_ge(s_cent, 2)
                dve.tensor_copy(bpart[:, 0, :], brow[:]).then_inc(s_bp, 1)
                dve.wait_ge(s_bp, 1)
                dve.tensor_tensor(brow[:], brow[:], bpart[:, 0, :], ALU.subtract).then_inc(s_bp, 1)
                dve.wait_ge(s_bp, 2)
                dve.tensor_copy(bpart[:, 1, :], brow[:]).then_inc(s_bp, 1)
                dve.wait_ge(s_bp, 3)
                dve.tensor_tensor(brow[:], brow[:], bpart[:, 1, :], ALU.subtract).then_inc(s_bp, 1)
                dve.wait_ge(s_bp, 4)
                dve.tensor_copy(bpart[:, 2, :], brow[:]).then_inc(s_bp, 1)

            @block.tensor
            def _(pe):
                pe.wait_ge(s_const, 3)
                for k in range(4):
                    pe.wait_ge(s_x[k % 2], 16 * (k // 2 + 1))
                    for o in range(NC):
                        n = k * NC + o
                        if n >= 2:
                            pe.wait_ge(s_xa, n - 1)
                        for c in range(NC):
                            mm = pe.transpose(banks[n % 2][:, c * P:(c + 1) * P], wx[k % 2][:, o, c * P:(c + 1) * P], ident[:])
                        mm.then_inc(s_xp, 1)

            @block.scalar
            def _(act):
                for k in range(4):
                    for o in range(NC):
                        n = k * NC + o
                        act.wait_ge(s_xp, n + 1)
                        dst = woT[:, :, o * P:(o + 1) * P] if k == 3 else wcT[:, :, k, o * P:(o + 1) * P]
                        act.activation(dst, banks[n % 2][:].rearrange("p (c n) -> p c n", c=NC), ACT.Copy).then_inc(s_xa, 1)

    with ExitStack() as tmp:
        def sem(name):
            return tmp.enter_context(nc.semaphore(name))

        natural = [tmp.enter_context(nc.sbuf_tensor(f"wnat{k}", [P, 16, 512], F32)) for k in range(3)]
        scratch = tmp.enter_context(nc.sbuf_tensor("scratch", [P, F], BF16))
        ones32 = tmp.enter_context(nc.sbuf_tensor("ones32b", [P, P], F32))
        sums = tmp.enter_context(nc.sbuf_tensor("sums", [P, 3, 4], F32))
        sum3 = tmp.enter_context(nc.sbuf_tensor("sum3", [P, 3], F32))
        winv = tmp.enter_context(nc.sbuf_tensor("winv", [P, 3], F32))
        s_in = [sem(f"sf_in{k}") for k in range(3)]
        s_one, s_abs, s_sum, s_tot, s_q, s_p, s_a = (sem(f"sf_{n}") for n in ("one", "abs", "sum", "tot", "q", "p", "a"))
        with nc.Block() as block:
            @block.sync
            def _(sp):
                for k, w in enumerate((T["w_gate"], T["w_up"])):
                    sp.dma_start(natural[k][:], w.rearrange("(o p) n -> p o n", p=P)).then_inc(s_in[k], 16)
                sp.dma_start(natural[2][:].rearrange("p (a q) n -> p a (q n)", a=4),
                             T["w_down"].rearrange("(a p) n -> p a n", p=P)).then_inc(s_in[2], 16)

            @block.gpsimd
            def _(pool):
                pool.memset(ones32[:], 1.0).then_inc(s_one, 1)

            @block.scalar
            def _(act):
                for k in range(3):
                    act.wait_ge(s_in[k], 16)
                    for q in range(4):
                        n = 4 * k + q
                        if n:
                            act.wait_ge(s_abs, n)
                        act.activation(scratch[:].rearrange("p (a n) -> p a n", a=4), natural[k][:, 4 * q:4 * q + 4, :],
                                       ACT.Abs, accum_out=sums[:, k, q:q + 1]).then_inc(s_abs, 1)
                for n in range(48):
                    k, u = n // 16, n % 16
                    act.wait_ge(s_p, n + 2)
                    src = banks[n % 4][:].rearrange("p (c n) -> p c n", c=4)
                    dst = (wdT[:, 4 * (u % 4):4 * (u % 4) + 4, (u // 4) * P:(u // 4 + 1) * P] if k == 2
                           else (wgT, wuT)[k][:, :, u * P:(u + 1) * P])
                    act.activation(dst, src, ACT.Copy, bias=-MAGIC, saturate=False).then_inc(s_a, 1)

            @block.vector
            def _(dve):
                dve.wait_ge(s_abs, 12)
                dve.tensor_reduce(sum3[:], sums[:], AXX, ALU.add).then_inc(s_sum, 1)
                dve.wait_ge(s_p, 1)
                dve.tensor_scalar(wscale[:], banks[7][:, 0:3], 1.0 / (F * D), 1e-5, ALU.mult, ALU.max).then_inc(s_tot, 1)
                dve.wait_ge(s_tot, 1)
                dve.reciprocal(winv[:], wscale[:]).then_inc(s_tot, 1)
                dve.wait_ge(s_tot, 2)
                for n in range(48):
                    k, u = n // 16, n % 16
                    w = natural[k][:, u, :]
                    dve.tensor_scalar(w, w, winv[:, k:k + 1], 1.0, ALU.mult, ALU.min).then_inc(s_q, 1)
                    dve.wait_ge(s_q, 2 * n + 1)
                    dve.tensor_scalar(w, w, -1.0, MAGIC, ALU.max, ALU.add).then_inc(s_q, 1)

            @block.tensor
            def _(pe):
                pe.wait_ge(s_one, 1)
                pe.wait_ge(s_sum, 1)
                pe.matmul(banks[7][:, 0:3], ones32[:], sum3[:], start=True, stop=True).then_inc(s_p, 1)
                for n in range(48):
                    k, u = n // 16, n % 16
                    if n >= 4:
                        pe.wait_ge(s_a, n - 3)
                    pe.wait_ge(s_q, 2 * n + 2)
                    for b in range(4):
                        mm = pe.transpose(banks[n % 4][:, b * P:(b + 1) * P], natural[k][:, u, b * P:(b + 1) * P], ident[:])
                    mm.then_inc(s_p, 1)


NAMES = ["x", "ctx_1024", "L0_attn_W_attn", "L0_attn_b_attn", "L0_attn_W_proj", "L0_attn_b_proj",
         "L0_attn_q_gamma", "L0_attn_q_beta", "L0_attn_k_gamma", "L0_attn_k_beta", "L0_xattn_Wq",
         "L0_xattn_bq", "L0_xattn_Wk", "L0_xattn_bk", "L0_xattn_Wv", "L0_xattn_bv", "L0_xattn_Wo",
         "L0_xattn_bo", "L0_ffn_w_gate", "L0_ffn_w_up", "L0_ffn_w_down"]


def kernel(**inputs):
    import concourse.bacc as bacc
    from concourse.bass_utils import run_bass_kernel_spmd

    nc = bacc.Bacc("TRN2", target_bir_lowering=False, num_devices=1)
    arrays, args = {}, []
    for name in NAMES:
        a = np.ascontiguousarray(inputs[name])
        arrays[f"in_{name}"] = a
        args.append(nc.dram_tensor(f"in_{name}", a.shape, mybir.dt.from_np(a.dtype), kind="ExternalInput").ap())
    out = nc.dram_tensor("out_y", (NB, S, D), F32, kind="ExternalOutput").ap()
    decoder_layer(nc, *args, out)
    r = run_bass_kernel_spmd(nc, [arrays], core_ids=[0])
    return r.results[0]["out_y"]
```

```python
from contextlib import ExitStack

import numpy as np

import concourse.bass as bass
from concourse import mybir

F32 = mybir.dt.float32
BF16 = mybir.dt.bfloat16
FP8 = mybir.dt.float8e4
ALU = mybir.AluOpType
ACT = mybir.ActivationFunctionType
AXX = mybir.AxisListType.X

P = 128
NB, S, D = 8, 512, 512
H, HD = 16, 32
F = 2048
NT = S // P
NC = D // P
HG = P // HD
NG = H // HG
NF = F // 512
KF = F // P
ROUNDS = 4
SLOTS = NG * NT
SCALE = float(HD) ** -0.5
EPS = 1e-5
MAGIC = 1.5 * 2.0 ** 23
MASKED = -1e30
REPLACED = -3e38
LO, HI = -1, NB + 2


SIGNALS = ["shared_full", "shared_read", "cscore_full", "cscore_read", "sscore_full", "sscore_read",
           "smax", "sexp", "sbias", "cbias", "cexp", "topk", "spT_full", "spT_read", "so_full", "so_recip",
           "so_norm", "cpT_full", "cpT_read", "crest", "cprob", "co_full", "co_recip", "co_norm",
           "sq_done", "rstd_done", "shat_done", "sumsq_done", "dve_rows", "pool_rows", "feed_stats",
           "feed_pool", "h_dve", "h_pool", "rmax", "wa_in", "wc_in", "feed_in0", "feed_in1", "feed_in2",
           "feed_in3", "xres_in", "x1res_in", "x1_out", "x2_out", "x2res_in", "y_out"]


class Stages:

    def __init__(self, i):
        def on(b):
            return 0 <= b < NB
        self.self_now, self.self_next, self.self_last = on(i), on(i + 1), on(i - 1)
        self.proj1 = on(i - 1)
        self.cross_now, self.cross_next, self.cross_last = on(i - 2), on(i - 1), on(i - 3)
        self.mlp = on(i - 3)

    def key(self):
        return (self.self_now, self.self_next, self.self_last, self.proj1, self.cross_now, self.cross_next,
                self.cross_last, self.mlp)


def feeds(st, s):
    order = [(src, t) for src in ("x", "x1", "ctx") for t in range(NT)]
    slots = [10, 10, 11, 11, 11, 12, 12, 12, 12, 13, 13, 13]
    return [(k, src, t) for k, (src, t) in enumerate(order) if slots[k] == s
            and (st.self_next if src == "x" else st.cross_next)]


def all_feeds(st):
    return [f for s in range(SLOTS) for f in feeds(st, s)]


def self_group(st, s):
    g = s // NT + 1
    return g if (st.self_next if g == NG else st.self_now) else None


def cross_group(st, s):
    g = s // NT + 1
    return g if (st.cross_next if g == NG else st.cross_now) else None


def mlp_chunk(st, s, early):
    t, r = (s - 4) // 3, (s - 4) % 3
    return [(t, 2 * r + (not early))] if st.mlp and s >= 4 and t < NT and r < 2 else []


def mlp_down(st, s):
    return [(s - 6) // 3] if st.mlp and s >= 6 and (s - 6) % 3 == 0 else []


def early_units(st, s):
    u = []
    if st.mlp and s < NT:
        u.append(("cross_oT", s))
    if st.proj1 and s < NT:
        u.append(("self_oT", s))
    if st.mlp and s < NT:
        u.append(("cross_out", s))
    if st.proj1 and s < NT:
        u.append(("self_out", s))
    if st.mlp and 1 <= s <= NT:
        u.append(("x2T", s - 1))
    for t, n in mlp_chunk(st, s, True):
        u += [("gate", t, n), ("up", t, n)]
    if s % NT == 3 and cross_group(st, s):
        u += [("cross_T", cross_group(st, s), k) for k in range(2)]
    return u


def late_units(st, s):
    u = [("feed", *f) for f in feeds(st, s)]
    for t in mlp_down(st, s):
        u += [("hT", t, q) for q in range(NF)]
    for t, n in mlp_chunk(st, s, False):
        u += [("gate", t, n), ("up", t, n)]
    g = self_group(st, s)
    if g:
        u += [("self_qkv", g, t) for t in ((0, 1, 2), (3,), (), ())[s % NT]]
    for t in mlp_down(st, s):
        u.append(("down", t))
    g = cross_group(st, s)
    if g:
        u += [("cross_qkv", g, t) for t in ((), (0, 1), (2, 3), ())[s % NT]]
    g = self_group(st, s)
    if s % NT == 3 and g:
        u += [("self_T", g, k) for k in range(2)]
    return u


def shared_units(st, s):
    return early_units(st, s) + late_units(st, s)


ACT_READS = {"cross_oT": 1, "self_oT": 1, "hT": 1, "x2T": 1, "gate": 2, "up": 1, "self_qkv": 2, "cross_qkv": 2,
             "self_T": 1, "cross_T": 1, "feed": 1}


ROUND_ORDER = [("max", j) for j in range(HG)] + [("replace", j) for j in range(HG)]
LAST_ORDER = [("max", 0)] + [step for j in range(1, HG) for step in (("max", j), ("replace", j - 1))] + [("replace", HG - 1)]


class Counts:

    def __init__(self, st):
        self.order, self.given = {}, {}
        add = self._add
        apply_self = [s - 1 for s in range(SLOTS) if (st.self_last if s == 0 else st.self_now)]
        apply_cross = [s - 1 for s in range(SLOTS) if (st.cross_last if s == 0 else st.cross_now)]
        self.apply_self, self.apply_cross = apply_self, apply_cross
        self.bank, self.before = {}, {}
        held = [None, None]
        n = 0
        for s in range(SLOTS):
            for u in shared_units(st, s):
                self.bank[u], self.before[u] = n % 2, held[n % 2]
                held[n % 2] = u
                n += 1
                add("shared_full", u)
                for r in range(ACT_READS.get(u[0], 0)):
                    add("shared_read", (u, r))
        for s in range(SLOTS):
            if st.cross_now if s < SLOTS - 1 else st.cross_next:
                for j in range(HG):
                    add("cscore_full", (s + 1, j))
                    add("cscore_read", (s + 1, j))
            if st.self_now:
                for j in range(HG):
                    for name in ("sscore_full", "sscore_read", "smax", "sexp"):
                        add(name, (s, j))
                add("sbias", s)
            if st.cross_now:
                add("rmax", s)
                add("cbias", s)
                for j in range(HG):
                    add("cexp", (s, j))
                for r in range(ROUNDS):
                    for half, j in ROUND_ORDER if r < ROUNDS - 1 else LAST_ORDER:
                        add("topk", (s, r, half, j))
        for m in apply_self:
            for j in range(HG):
                add("spT_full", (m, j))
                add("spT_read", (m, j))
            add("so_full", m)
            add("so_recip", m)
            add("so_norm", m)
        for m in apply_cross:
            for j in range(HG):
                add("cpT_full", (m, j))
                add("cpT_read", (m, j))
                add("crest", (m, j))
                add("cprob", (m, j))
            add("co_full", m)
            add("co_recip", m)
            add("co_norm", m)

    def _add(self, name, label):
        self.order.setdefault(name, {})[label] = len(self.order.get(name, {})) + 1

    def plan(self, name, label):
        self._add(name, label)

    def upto(self, name, label, each=1):
        return each * self.order.get(name, {}).get(label, 0)

    def step(self, name, label, each=1):
        self.given[name] = self.given.get(name, 0) + 1
        assert self.order[name][label] == self.given[name], (name, label)
        return each

    def end(self):
        for name, labels in self.order.items():
            assert self.given.get(name, 0) == len(labels), (name, self.given.get(name, 0), len(labels))


def decoder_layer(nc, x, ctx_in, W_attn, b_attn, W_proj, b_proj, q_gamma, q_beta, k_gamma, k_beta,
                  Wq, bq, Wk, bk, Wv, bv, Wo, bo, w_gate, w_up, w_down, out):
    x_rows = x.rearrange("b s d -> (b s) d")
    ctx_rows = ctx_in.rearrange("b s d -> (b s) d")
    out_rows = out.rearrange("b s d -> (b s) d")
    wa_dram = nc.dram_tensor("wa_by_group", (NG, P, NC, 3, P), F32, kind="Internal").ap()
    wc_dram = nc.dram_tensor("wc_by_group", (NG, P, NC, 3, P), F32, kind="Internal").ap()
    x1_rows = nc.dram_tensor("x1_rows", (NB * S, D), F32, kind="Internal").ap()
    x2_rows = nc.dram_tensor("x2_rows", (NB * S, D), F32, kind="Internal").ap()

    with ExitStack() as keep:
        def sb(name, shape, dt=F32, stack=keep):
            return stack.enter_context(nc.sbuf_tensor(name, shape, dt))

        def sem(name, stack=keep):
            return stack.enter_context(nc.semaphore(name))

        banks = [keep.enter_context(nc.psum_tensor(f"bank{k}", [P, 512], F32)) for k in range(8)]
        cscore_ps, sscore_ps, cpT_ps, spT_ps, co_ps, so_ps = banks[:6]
        shared_ps = banks[6:]

        ident = sb("ident", [P, P])
        ident16 = sb("ident16", [P, P], BF16)
        mask16 = sb("mask16", [P, P], BF16)
        ones16 = sb("ones16", [96, P], BF16)
        bias16 = sb("bias16", [96, 3 * D], BF16)
        minus_half = sb("minus_half", [P, 32])
        gb = sb("gb", [P, 4])
        wscale = sb("wscale", [P, 3])
        wproj = sb("wproj", [P, NC, D])
        woT = sb("woT", [P, NC, D])
        wgT = sb("wgT", [P, NC, F], FP8)
        wuT = sb("wuT", [P, NC, F], FP8)
        wdT = sb("wdT", [P, KF, D], FP8)

        setup(nc, dict(W_attn=W_attn, b_attn=b_attn, wa_dram=wa_dram, wc_dram=wc_dram, banks=banks,
                       ident=ident, ident16=ident16, mask16=mask16, ones16=ones16, bias16=bias16,
                       minus_half=minus_half, gb=gb, wscale=wscale, wproj=wproj, woT=woT, wgT=wgT, wuT=wuT,
                       wdT=wdT, bq=bq, bk=bk, bv=bv, b_proj=b_proj, bo=bo, q_gamma=q_gamma, q_beta=q_beta,
                       k_gamma=k_gamma, k_beta=k_beta, W_proj=W_proj, Wq=Wq, Wk=Wk, Wv=Wv, Wo=Wo,
                       w_gate=w_gate, w_up=w_up, w_down=w_down))

        wa = sb("wa", [P, NC, 3 * P])
        wc = sb("wc", [P, NC, 3 * P])
        feed = [sb(f"feed{k}", [P, D]) for k in range(4)]
        xT = sb("xT", [P, NC, S])
        x1T = sb("x1T", [P, NC, S])
        ctxT = sb("ctxT", [P, NC, S])
        sqk = sb("sqk", [P, NT, 2 * P])
        ssq = sb("ssq", [P, NT, 2 * P])
        srs = sb("srs", [P, 2 * NT * HG])
        sqT, skT = sb("sqT", [P, S]), sb("skT", [P, S])
        sv = [sb(f"sv{k}", [P, NT, HG, HD + 1]) for k in range(2)]
        sP = [sb(f"sP{j}", [P, S]) for j in range(HG)]
        sPT = [sb(f"sPT{k}", [P, S]) for k in range(2)]
        smx, snb = sb("smx", [P, HG]), sb("snb", [P, HG])
        so_r = sb("so_r", [P, HG])
        so = sb("so", [P, NT, D])
        cqk = sb("cqk", [P, NT, 2 * P])
        cqT, ckT = sb("cqT", [P, S]), sb("ckT", [P, S])
        cv = [sb(f"cv{k}", [P, NT, HG, HD + 1]) for k in range(2)]
        cS = [[sb(f"cS{k}_{j}", [P, S]) for j in range(HG)] for k in range(2)]
        cW = [sb(f"cW{j}", [P, S]) for j in range(HG)]
        top8 = sb("top8", [P, HG, 8])
        rowmax = sb("rowmax", [P, HG])
        cnb = [sb(f"cnb{k}", [P, HG]) for k in range(2)]
        cPT = [sb(f"cPT{k}", [P, S]) for k in range(2)]
        co_r = sb("co_r", [P, HG])
        co = sb("co", [P, NT, D])
        self_oT, cross_oT = sb("self_oT", [P, NC, P]), sb("cross_oT", [P, NC, P])
        xres = sb("xres", [P, D])
        x1res, x2t, x2h = sb("x1res", [P, D]), sb("x2t", [P, D]), sb("x2h", [P, D])
        x2T = sb("x2T", [P, NT, NC, P], BF16)
        mstat = sb("mstat", [P, 6])
        mv, mcol = sb("mv", [P, 2]), sb("mcol", [P, 8])
        gate_scale, up_amax = sb("gate_scale", [P, NT, 2]), sb("up_amax", [P, NT])
        th, uc = sb("th", [P, 512]), sb("uc", [P, 512])
        hh = sb("hh", [P, NF, 512])
        hmx, hcol = sb("hmx", [P, NF]), sb("hcol", [P, 4])
        hT = sb("hT", [P, KF, P], BF16)
        x2res = sb("x2res", [P, D])
        fstat, fmv, fcol = sb("fstat", [P, 6]), sb("fmv", [P, 2]), sb("fcol", [P, 4])

        sems = {n: sem(n) for n in SIGNALS}
        nums = [s.num for s in sems.values()]
        assert max(nums) - min(nums) == len(nums) - 1

        with nc.Block() as block:
            @block.vector
            def _(dve):
                for v in (*sv, *cv):
                    dve.memset(v[:, :, :, HD:HD + 1], 1.0)

        def one_iteration(i, st):
            C = Counts(st)
            upto, step = C.upto, C.step
            (shared_full, shared_read, cscore_full, cscore_read, sscore_full, sscore_read, smax, sexp, sbias, cbias,
             cexp, topk, spT_full, spT_read, so_full, so_recip, so_norm, cpT_full, cpT_read, crest, cprob, co_full,
             co_recip, co_norm, sq_done, rstd_done, shat_done, sumsq_done, dve_rows, pool_rows, feed_stats, feed_pool,
             h_dve, h_pool, rmax_done, wa_in, wc_in) = (sems[n] for n in SIGNALS[:37])
            feed_in = [sems[f"feed_in{k}"] for k in range(4)]
            xres_in, x1res_in, x1_out, x2_out, x2res_in, y_out = (sems[n] for n in (
                "xres_in", "x1res_in", "x1_out", "x2_out", "x2res_in", "y_out"))
            def rows(ap, b, t):
                return ap[bass.ds(b * S + t * P, P), :]

            fs = all_feeds(st)
            ring = {f: n for n, f in enumerate(fs)}
            normed = [f for f in fs if f[1] != "ctx"]
            for f in fs:
                C.plan(f"feed_in{ring[f] % 4}", f)
            for f in normed:
                for k in range(2):
                    C.plan("feed_stats", (f, k))
                for k in range(5):
                    C.plan("feed_pool", (f, k))
            was = [g for g in range(1, NG + 2) if (st.self_next if g >= NG else st.self_now)]
            wcs = [g for g in range(1, NG + 2) if (st.cross_next if g >= NG else st.cross_now)]
            for g in was[1 if st.self_now else 0:]:
                C.plan("wa_in", g)
            for g in wcs[1 if st.cross_now else 0:]:
                C.plan("wc_in", g)
            for g in was:
                if g <= NG:
                    C.plan("sq_done", g)
                    C.plan("sumsq_done", g)
                    C.plan("rstd_done", (g, 0))
                    C.plan("rstd_done", (g, 1))
                    C.plan("shat_done", g)
            for t in range(NT):
                if st.proj1:
                    C.plan("xres_in", t)
                    C.plan("x1_out", t)
                if st.mlp:
                    C.plan("x1res_in", t)
                    C.plan("x2_out", t)
                    C.plan("x2res_in", t)
                    C.plan("y_out", t)
            for s in range(SLOTS):
                if 1 <= s <= NT and st.mlp:
                    for k in ("amax", "clip", "inv"):
                        C.plan("dve_rows", (k, s - 1))
                    for k in range(3):
                        C.plan("pool_rows", ("quant", s - 1, k))
                if s < NT and st.mlp:
                    for k in ("x2", "stats", "aggr"):
                        C.plan("dve_rows", (k, s))
                    for k in range(6):
                        C.plan("pool_rows", ("ln", s, k))
                if s < NT and st.proj1:
                    C.plan("dve_rows", ("x1", s))
                for t in mlp_down(st, s - 1):
                    C.plan("h_dve", ("out", t))
                for early, at in ((False, s - 1), (True, s)):
                    for t, n in mlp_chunk(st, at, early):
                        C.plan("h_pool", ("t1", t, n))
                        C.plan("h_pool", ("r", t, n))
                        C.plan("h_dve", ("h", t, n))
                        C.plan("h_dve", ("max", t, n))
                        if n == NF - 1:
                            for k in ("amax", "clip", "inv"):
                                C.plan("h_dve", (k, t))
                            C.plan("h_pool", ("scale", t))
                            for q in range(NF):
                                C.plan("h_pool", ("q", t, q))
            for t in mlp_down(st, SLOTS - 1):
                C.plan("h_dve", ("out", t))

            def freed(eng, u):
                b = C.before[u]
                if b is None:
                    return
                if b[0] in ACT_READS:
                    eng.wait_ge(shared_read, upto("shared_read", (b, ACT_READS[b[0]] - 1)))
                elif b[0] == "cross_out":
                    eng.wait_ge(dve_rows, upto("dve_rows", ("x2", b[1])))
                elif b[0] == "self_out":
                    eng.wait_ge(dve_rows, upto("dve_rows", ("x1", b[1])))
                else:
                    eng.wait_ge(h_dve, upto("h_dve", ("out", b[1])))

            def four(ap):
                return ap.rearrange("p (c n) -> p c n", c=4)

            with nc.Block() as block:
                @block.sync
                def _(sp):
                    def load_wa(g):
                        if g - 1 in was:
                            sp.wait_ge(shared_full, upto("shared_full", ("self_qkv", g - 1, NT - 1)))
                        sp.dma_start(wa[:].rearrange("p c (k n) -> p c k n", k=3), wa_dram[g % NG]).then_inc(
                            wa_in, step("wa_in", g, 16))

                    def load_wc(g):
                        if g - 1 in wcs:
                            sp.wait_ge(shared_full, upto("shared_full", ("cross_qkv", g - 1, NT - 1)))
                        sp.dma_start(wc[:].rearrange("p c (k n) -> p c k n", k=3), wc_dram[g % NG]).then_inc(
                            wc_in, step("wc_in", g, 16))

                    def load_feed(f):
                        k, src, t = f
                        n = ring[f]
                        if n >= 4:
                            sp.wait_ge(shared_full, upto("shared_full", ("feed", *fs[n - 4])))
                        if src == "x1":
                            sp.wait_ge(x1_out, upto("x1_out", NT - 1, 16))
                        a, b = {"x": (x_rows, i + 1), "x1": (x1_rows, i - 1), "ctx": (ctx_rows, i - 1)}[src]
                        sp.dma_start(feed[n % 4][:], rows(a, b, t)).then_inc(feed_in[n % 4], step(f"feed_in{n % 4}", f, 16))

                    pending = list(fs)
                    for s in range(SLOTS):
                        if s == 0 and not st.self_now and st.self_next:
                            load_wa(NG)
                        if s == 0 and not st.cross_now and st.cross_next:
                            load_wc(NG)
                        if 1 <= s <= NT and st.mlp:
                            sp.wait_ge(dve_rows, upto("dve_rows", ("x2", s - 1)))
                            sp.dma_start(rows(x2_rows, i - 3, s - 1), x2t[:]).then_inc(x2_out, step("x2_out", s - 1, 16))
                        if s < NT and st.mlp:
                            sp.dma_start(x1res[:], rows(x1_rows, i - 3, s)).then_inc(x1res_in, step("x1res_in", s, 16))
                        if 1 <= s <= NT and st.proj1:
                            sp.wait_ge(dve_rows, upto("dve_rows", ("x1", s - 1)))
                            sp.dma_start(rows(x1_rows, i - 1, s - 1), xres[:]).then_inc(x1_out, step("x1_out", s - 1, 16))
                        if s < NT and st.proj1:
                            if s:
                                sp.wait_ge(x1_out, upto("x1_out", s - 1, 16))
                            sp.dma_start(xres[:], rows(x_rows, i - 1, s)).then_inc(xres_in, step("xres_in", s, 16))
                        g = s // NT + 2
                        if s % NT == 2 and g in was and g - 1 in was:
                            load_wa(g)
                        if s % NT == 3 and g in wcs and g - 1 in wcs:
                            load_wc(g)
                        for t in mlp_down(st, s - 1):
                            sp.wait_ge(h_dve, upto("h_dve", ("out", t)))
                            sp.dma_start(rows(out_rows, i - 3, t), x2res[:]).then_inc(y_out, step("y_out", t, 16))
                        for t in mlp_down(st, s):
                            if t == 0:
                                sp.wait_ge(x2_out, upto("x2_out", NT - 1, 16))
                            else:
                                sp.wait_ge(y_out, upto("y_out", t - 1, 16))
                            sp.dma_start(x2res[:], rows(x2_rows, i - 3, t)).then_inc(x2res_in, step("x2res_in", t, 16))
                        while pending and s >= 7 and (ring[pending[0]] < 4 or ring[pending[0]] - 4 in
                                                      [ring[f] for q in range(s) for f in feeds(st, q)]):
                            load_feed(pending.pop(0))
                    while pending:
                        load_feed(pending.pop(0))
                    for t in mlp_down(st, SLOTS - 1):
                        sp.wait_ge(h_dve, upto("h_dve", ("out", t)))
                        sp.dma_start(rows(out_rows, i - 3, t), x2res[:]).then_inc(y_out, step("y_out", t, 16))
                    if st.proj1:
                        sp.wait_ge(x1_out, 16 * NT)
                    if st.mlp:
                        sp.wait_ge(x2_out, 16 * NT)
                        sp.wait_ge(y_out, 16 * NT)
                    if st.self_next:
                        sp.wait_ge(wa_in, upto("wa_in", NG + 1, 16))
                    if st.cross_next:
                        sp.wait_ge(wc_in, upto("wc_in", NG + 1, 16))

                @block.tensor
                def _(pe):
                    def probs_self(m, j):
                        qt = m % NT
                        pe.wait_ge(sexp, upto("sexp", (m, j)))
                        if j:
                            pe.wait_ge(spT_read, upto("spT_read", (m, j - 1)))
                        elif m - 1 in C.apply_self:
                            pe.wait_ge(spT_read, upto("spT_read", (m - 1, HG - 1)))
                        for k in range(qt + 1):
                            mm = pe.transpose(spT_ps[:, k * P:(k + 1) * P], sP[j][:, k * P:(k + 1) * P], ident[:])
                        mm.then_inc(spT_full, step("spT_full", (m, j)))

                    def values_self(m, j):
                        qt, g = m % NT, (m // NT) % NG
                        pe.wait_ge(spT_read, upto("spT_read", (m, j)))
                        if j == 0 and m - 1 in C.apply_self:
                            pe.wait_ge(so_norm, upto("so_norm", m - 1))
                        for k in range(qt + 1):
                            mm = pe.matmul(so_ps[:, j * (HD + 1):(j + 1) * (HD + 1)], sPT[j % 2][:, k * P:(k + 1) * P],
                                           sv[g % 2][:, k, j, :], start=k == 0, stop=k == qt)
                        if j == HG - 1:
                            mm.then_inc(so_full, step("so_full", m))

                    def scores_self(s, j):
                        qt = s % NT
                        if j:
                            pe.wait_ge(sscore_read, upto("sscore_read", (s, j - 1)))
                        elif s:
                            pe.wait_ge(sscore_read, upto("sscore_read", (s - 1, HG - 1)))
                            if qt == 0:
                                pe.wait_ge(shared_read, upto("shared_read", (("self_T", s // NT, 1), 0)))
                        h = slice(j * HD, (j + 1) * HD)
                        pe.matmul(sscore_ps[:, 0:(qt + 1) * P], sqT[h, qt * P:(qt + 1) * P], skT[h, 0:(qt + 1) * P],
                                  start=True, stop=False)
                        pe.matmul(sscore_ps[:, qt * P:(qt + 1) * P], ident16[:], mask16[:], start=False,
                                  stop=True).then_inc(sscore_full, step("sscore_full", (s, j)))

                    def probs_cross(m, j):
                        pe.wait_ge(cprob, upto("cprob", (m, j)))
                        if j:
                            pe.wait_ge(cpT_read, upto("cpT_read", (m, j - 1)))
                        elif m - 1 in C.apply_cross:
                            pe.wait_ge(cpT_read, upto("cpT_read", (m - 1, HG - 1)))
                        for k in range(NT):
                            mm = pe.transpose(cpT_ps[:, k * P:(k + 1) * P], cS[m % 2][j][:, k * P:(k + 1) * P], ident[:])
                        mm.then_inc(cpT_full, step("cpT_full", (m, j)))

                    def values_cross(m, j):
                        g = (m // NT) % NG
                        pe.wait_ge(cpT_read, upto("cpT_read", (m, j)))
                        if j == 0 and m - 1 in C.apply_cross:
                            pe.wait_ge(co_norm, upto("co_norm", m - 1))
                        for k in range(NT):
                            mm = pe.matmul(co_ps[:, j * (HD + 1):(j + 1) * (HD + 1)], cPT[j % 2][:, k * P:(k + 1) * P],
                                           cv[g % 2][:, k, j, :], start=k == 0, stop=k == NT - 1)
                        if j == HG - 1:
                            mm.then_inc(co_full, step("co_full", m))

                    def scores_cross(n, j):
                        qt = n % NT
                        if j:
                            pe.wait_ge(cscore_read, upto("cscore_read", (n, j - 1)))
                        else:
                            pe.wait_ge(cscore_read, upto("cscore_read", (n - 1, HG - 1)))
                            if qt == 0:
                                pe.wait_ge(shared_read, upto("shared_read", (("cross_T", n // NT, 1), 0)))
                        h = slice(j * HD, (j + 1) * HD)
                        pe.matmul(cscore_ps[:], cqT[h, qt * P:(qt + 1) * P], ckT[h, :], start=True,
                                  stop=True).then_inc(cscore_full, step("cscore_full", (n, j)))

                    def turn(ps, src):
                        for c in range(4):
                            mm = pe.transpose(ps[:, c * P:(c + 1) * P], src(c), ident[:])
                        return mm

                    def unit(u, s):
                        ps = shared_ps[C.bank[u]]
                        freed(pe, u)
                        kind = u[0]
                        if kind == "cross_oT":
                            if u[1] == NT - 1:
                                pe.wait_ge(co_norm, upto("co_norm", -1))
                            mm = turn(ps, lambda c: co[:, u[1], c * P:(c + 1) * P])
                        elif kind == "self_oT":
                            if u[1] == NT - 1:
                                pe.wait_ge(so_norm, upto("so_norm", -1))
                            mm = turn(ps, lambda c: so[:, u[1], c * P:(c + 1) * P])
                        elif kind in ("cross_out", "self_out"):
                            oT, w, b = (cross_oT, woT, D) if kind == "cross_out" else (self_oT, wproj, 0)
                            pe.matmul(ps[:], ones16[64:67, :], bias16[64:67, b:b + D], start=True, stop=False)
                            pe.wait_ge(shared_read, upto("shared_read", ((kind[:-3] + "oT", u[1]), 0)))
                            for c in range(NC):
                                mm = pe.matmul(ps[:], oT[:, c, :], w[:, c, :], start=False, stop=c == NC - 1)
                        elif kind == "x2T":
                            pe.wait_ge(pool_rows, upto("pool_rows", ("quant", u[1], 2)))
                            mm = turn(ps, lambda c: x2h[:, c * P:(c + 1) * P])
                        elif kind in ("gate", "up"):
                            w = wgT if kind == "gate" else wuT
                            pe.wait_ge(shared_read, upto("shared_read", (("x2T", u[1]), 0)))
                            for c in range(NC):
                                mm = pe.matmul(ps[:], x2T[:, u[1], c, :], w[:, c, u[2] * 512:(u[2] + 1) * 512],
                                               start=c == 0, stop=c == NC - 1)
                        elif kind == "hT":
                            pe.wait_ge(h_pool, upto("h_pool", ("q", u[1], u[2])))
                            mm = turn(ps, lambda c: hh[:, u[2], c * P:(c + 1) * P])
                        elif kind == "down":
                            pe.wait_ge(shared_read, upto("shared_read", (("hT", u[1], NF - 1), 0)))
                            for c in range(KF):
                                mm = pe.matmul(ps[:], hT[:, c, :], wdT[:, c, :], start=c == 0, stop=c == KF - 1)
                        elif kind == "self_qkv":
                            g, t = u[1], u[2]
                            if t == 0:
                                pe.wait_ge(wa_in, upto("wa_in", g, 16))
                                if g == NG:
                                    pe.wait_ge(shared_read, upto("shared_read", (("feed", 3, "x", 3), 0)))
                            for part in range(3):
                                at = part * D + (g % NG) * P
                                pe.matmul(ps[:, part * P:(part + 1) * P], ones16[0:3, :], bias16[0:3, at:at + P],
                                          start=part == 0, stop=False, skip_group_check=True)
                            for c in range(NC):
                                mm = pe.matmul(ps[:, 0:3 * P], xT[:, c, t * P:(t + 1) * P], wa[:, c, :], start=False,
                                               stop=c == NC - 1, skip_group_check=True)
                        elif kind == "cross_qkv":
                            g, t = u[1], u[2]
                            if t == 0:
                                pe.wait_ge(wc_in, upto("wc_in", g, 16))
                                if g == NG:
                                    pe.wait_ge(shared_read, upto("shared_read", (("feed", 11, "ctx", 3), 0)))
                            at = (g % NG) * 3 * P
                            pe.matmul(ps[:, 0:3 * P], ones16[32:35, :], bias16[32:35, at:at + 3 * P], start=True, stop=False)
                            for c in range(NC):
                                pe.matmul(ps[:, 0:P], x1T[:, c, t * P:(t + 1) * P], wc[:, c, 0:P], start=False, stop=False)
                            for c in range(NC):
                                mm = pe.matmul(ps[:, P:3 * P], ctxT[:, c, t * P:(t + 1) * P], wc[:, c, P:3 * P],
                                               start=False, stop=c == NC - 1)
                        elif kind == "self_T":
                            pe.wait_ge(shat_done, upto("shat_done", u[1]))
                            mm = turn(ps, lambda c: sqk[:, c, u[2] * P:(u[2] + 1) * P])
                        elif kind == "cross_T":
                            pe.wait_ge(shared_read, upto("shared_read", (("cross_qkv", u[1], NT - 1), 1)))
                            mm = turn(ps, lambda c: cqk[:, c, u[2] * P:(u[2] + 1) * P])
                        else:
                            f = u[1:]
                            n = ring[f]
                            if f[1] == "ctx":
                                pe.wait_ge(feed_in[n % 4], upto(f"feed_in{n % 4}", f, 16))
                            else:
                                pe.wait_ge(feed_pool, upto("feed_pool", (f, 4)))
                            mm = turn(ps, lambda c: feed[n % 4][:, c * P:(c + 1) * P])
                        mm.then_inc(shared_full, step("shared_full", u))

                    for s in range(SLOTS):
                        for j in range(HG):
                            if s - 1 in C.apply_self:
                                probs_self(s - 1, j)
                            if st.self_now:
                                scores_self(s, j)
                            if s - 1 in C.apply_self:
                                values_self(s - 1, j)
                        for u in early_units(st, s):
                            unit(u, s)
                        for j in range(HG):
                            if s - 1 in C.apply_cross:
                                probs_cross(s - 1, j)
                            if st.cross_now if s < SLOTS - 1 else st.cross_next:
                                scores_cross(s + 1, j)
                            if s - 1 in C.apply_cross:
                                values_cross(s - 1, j)
                        for u in late_units(st, s):
                            unit(u, s)

                @block.scalar
                def _(act):
                    def unit(u):
                        ps = shared_ps[C.bank[u]]
                        kind = u[0]
                        act.wait_ge(shared_full, upto("shared_full", u))

                        def read(k, *a, **kw):
                            return act.activation(*a, **kw).then_inc(shared_read, step("shared_read", (u, k)))
                        if kind in ("cross_oT", "self_oT"):
                            if u[1]:
                                act.wait_ge(shared_full, upto("shared_full", (kind[:-2] + "out", u[1] - 1)))
                            read(0, (cross_oT if kind == "cross_oT" else self_oT)[:], four(ps[:]), ACT.Copy)
                        elif kind == "x2T":
                            read(0, x2T[:, u[1], :, :], four(ps[:]), ACT.Copy, bias=-MAGIC)
                        elif kind == "gate":
                            if (u[1], u[2]) != (0, 0):
                                prev = (u[1], u[2] - 1) if u[2] else (u[1] - 1, NF - 1)
                                act.wait_ge(h_pool, upto("h_pool", ("r", *prev)))
                            if u[2] == 0:
                                act.wait_ge(pool_rows, upto("pool_rows", ("quant", u[1], 1)))
                            read(0, th[:], ps[:], ACT.Tanh, scale=gate_scale[:, u[1], 0:1])
                            if u[1]:
                                act.wait_ge(shared_full, upto("shared_full", ("hT", u[1] - 1, u[2])))
                            read(1, hh[:, u[2], :], ps[:], ACT.Copy, scale=gate_scale[:, u[1], 1:2])
                        elif kind == "up":
                            if (u[1], u[2]) != (0, 0):
                                prev = (u[1], u[2] - 1) if u[2] else (u[1] - 1, NF - 1)
                                act.wait_ge(h_dve, upto("h_dve", ("h", *prev)))
                            read(0, uc[:], ps[:], ACT.Copy)
                        elif kind == "hT":
                            if u[1] and not u[2]:
                                act.wait_ge(shared_full, upto("shared_full", ("down", u[1] - 1)))
                            read(0, hT[:, 4 * u[2]:4 * u[2] + 4, :], four(ps[:]), ACT.Copy, bias=-MAGIC)
                        elif kind in ("self_qkv", "cross_qkv"):
                            g, t = u[1], u[2]
                            qk, v = (sqk, sv) if kind == "self_qkv" else (cqk, cv)
                            if t == 0:
                                act.wait_ge(shared_full, upto("shared_full", (kind[:-3] + "T", g - 1, 1)))
                            read(0, qk[:, t, :], ps[:, 0:2 * P], ACT.Copy)
                            if t == 0 and g >= 2:
                                full, name = (so_full, "so_full") if kind == "self_qkv" else (co_full, "co_full")
                                act.wait_ge(full, upto(name, 4 * (g - 1) - 1))
                            read(1, v[g % 2][:, t, :, 0:HD], ps[:, 2 * P:3 * P].rearrange("p (h d) -> p h d", h=HG), ACT.Copy)
                        elif kind == "self_T":
                            read(0, (sqT, skT)[u[2]][:], ps[:], ACT.Identity, scale=gb[:, 2 * u[2]:2 * u[2] + 1],
                                 bias=gb[:, 2 * u[2] + 1:2 * u[2] + 2])
                        elif kind == "cross_T":
                            read(0, (cqT, ckT)[u[2]][:], ps[:], ACT.Copy)
                        elif kind == "feed":
                            dst = {"x": xT, "x1": x1T, "ctx": ctxT}[u[2]]
                            read(0, dst[:, :, u[3] * P:(u[3] + 1) * P], four(ps[:]), ACT.Copy)

                    for s in range(SLOTS):
                        m = s - 1
                        for j in range(HG):
                            if m in C.apply_cross:
                                act.wait_ge(topk, upto("topk", (m, ROUNDS - 1, "replace", j)))
                                act.activation(cW[j][:], cW[j][:], ACT.Exp, bias=cnb[m % 2][:, j:j + 1],
                                               scale=SCALE).then_inc(crest, step("crest", (m, j)))
                            if m in C.apply_self:
                                n = (m % NT + 1) * P
                                act.wait_ge(spT_full, upto("spT_full", (m, j)))
                                act.activation(sPT[j % 2][:, 0:n], spT_ps[:, 0:n], ACT.Copy).then_inc(spT_read, step("spT_read", (m, j)))
                            if st.self_now:
                                n = (s % NT + 1) * P
                                act.wait_ge(sscore_full, upto("sscore_full", (s, j)))
                                act.activation(sP[j][:, 0:n], sscore_ps[:, 0:n], ACT.Copy).then_inc(sscore_read, step("sscore_read", (s, j)))
                        for u in early_units(st, s):
                            if u[0] in ACT_READS:
                                unit(u)
                        for j in range(HG):
                            if m in C.apply_cross:
                                act.wait_ge(cpT_full, upto("cpT_full", (m, j)))
                                act.activation(cPT[j % 2][:], cpT_ps[:], ACT.Copy).then_inc(cpT_read, step("cpT_read", (m, j)))
                            if st.cross_now if s < SLOTS - 1 else st.cross_next:
                                act.wait_ge(cscore_full, upto("cscore_full", (s + 1, j)))
                                act.activation(cS[(s + 1) % 2][j][:], cscore_ps[:], ACT.Copy).then_inc(
                                    cscore_read, step("cscore_read", (s + 1, j)))
                            if st.cross_now:
                                act.wait_ge(cbias, upto("cbias", s))
                                act.wait_ge(topk, upto("topk", (s, 0, "replace", j)))
                                act.activation(cS[s % 2][j][:], cS[s % 2][j][:], ACT.Exp, bias=cnb[s % 2][:, j:j + 1],
                                               scale=SCALE).then_inc(cexp, step("cexp", (s, j)))
                            if st.self_now:
                                n = (s % NT + 1) * P
                                act.wait_ge(sbias, upto("sbias", s))
                                act.activation(sP[j][:, 0:n], sP[j][:, 0:n], ACT.Exp, bias=snb[:, j:j + 1],
                                               scale=SCALE).then_inc(sexp, step("sexp", (s, j)))
                        for u in late_units(st, s):
                            if u[0] in ACT_READS:
                                unit(u)

                @block.vector
                def _(dve):
                    def top_step(s, r, half, j):
                        src = cS[s % 2][j] if r == 0 else cW[j]
                        if half == "max":
                            if r == 0:
                                dve.wait_ge(cscore_read, upto("cscore_read", (s, j)))
                                if s:
                                    dve.wait_ge(cbias, upto("cbias", s - 1))
                                    dve.wait_ge(topk, upto("topk", (s - 1, ROUNDS - 1, "replace", j)))
                            else:
                                dve.wait_ge(topk, upto("topk", (s, r - 1, "replace", j)))
                            dve.max(top8[:, j, :], src[:]).then_inc(topk, step("topk", (s, r, "max", j)))
                        else:
                            dve.wait_ge(topk, upto("topk", (s, r, "max", j)))
                            if r == 0:
                                dve.wait_ge(cprob, upto("cprob", (s - 1, j)))
                                dve.wait_ge(rmax_done, upto("rmax", s))
                            dve.match_replace(cW[j][:], top8[:, j, :], src[:], REPLACED).then_inc(
                                topk, step("topk", (s, r, "replace", j)))

                    def top_half(s, r, half):
                        if st.cross_now:
                            for j in range(HG):
                                top_step(s, r, half, j)

                    def row_maxima(s):
                        if st.cross_now:
                            dve.wait_ge(topk, upto("topk", (s, 0, "max", HG - 1)))
                            dve.wait_ge(cbias, upto("cbias", s - 1))
                            dve.tensor_copy(rowmax[:], top8[:, :, 0]).then_inc(rmax_done, step("rmax", s))

                    def norm(m, ps, full, recip, done, r_t, o_t, name):
                        qt, g = m % NT, (m // NT) % NG
                        dve.wait_ge(full, upto(name + "_full", m))
                        o = ps[:, 0:HG * (HD + 1)].rearrange("p (h d) -> p h d", h=HG)
                        dve.wait_ge(done, upto(name + "_norm", m - 1))
                        dve.reciprocal(r_t[:], o[:, :, HD]).then_inc(recip, step(name + "_recip", m))
                        dve.wait_ge(recip, upto(name + "_recip", m))
                        if m >= 0 and g == 0:
                            dve.wait_ge(shared_full, upto("shared_full", (("cross_oT" if name == "co" else "self_oT"), qt)))
                        dve.tensor_tensor(o_t[:, qt, g * P:(g + 1) * P].rearrange("p (h d) -> p h d", h=HG), o[:, :, 0:HD],
                                          r_t[:].unsqueeze(2).to_broadcast([P, HG, HD]), ALU.mult).then_inc(
                                              done, step(name + "_norm", m))

                    def cross_rows(s):
                        if s >= NT or not st.mlp:
                            return
                        dve.wait_ge(shared_full, upto("shared_full", ("cross_out", s)))
                        dve.wait_ge(x1res_in, upto("x1res_in", s, 16))
                        if s:
                            dve.wait_ge(x2_out, upto("x2_out", s - 1, 16))
                            dve.wait_ge(pool_rows, upto("pool_rows", ("ln", s - 1, 5)))
                        dve.tensor_tensor(x2t[:], shared_ps[C.bank[("cross_out", s)]][:], x1res[:], ALU.add).then_inc(
                            dve_rows, step("dve_rows", ("x2", s)))
                        dve.wait_ge(dve_rows, upto("dve_rows", ("x2", s)))
                        dve.bn_stats(mstat[:], x2t[:]).then_inc(dve_rows, step("dve_rows", ("stats", s)))
                        dve.wait_ge(dve_rows, upto("dve_rows", ("stats", s)))
                        dve.bn_aggr(mv[:], mstat[:]).then_inc(dve_rows, step("dve_rows", ("aggr", s)))

                    def self_rows(s):
                        if s >= NT or not st.proj1:
                            return
                        dve.wait_ge(shared_full, upto("shared_full", ("self_out", s)))
                        dve.wait_ge(xres_in, upto("xres_in", s, 16))
                        dve.tensor_tensor(xres[:], shared_ps[C.bank[("self_out", s)]][:], xres[:], ALU.add).then_inc(
                            dve_rows, step("dve_rows", ("x1", s)))

                    def row_scale(s):
                        if not 0 <= s < NT or not st.mlp:
                            return
                        dve.wait_ge(pool_rows, upto("pool_rows", ("ln", s, 5)))
                        if s:
                            dve.wait_ge(pool_rows, upto("pool_rows", ("quant", s - 1, 2)))
                        dve.tensor_reduce(up_amax[:, s:s + 1], x2h[:], AXX, ALU.max, apply_absolute_value=True).then_inc(
                            dve_rows, step("dve_rows", ("amax", s)))
                        dve.wait_ge(dve_rows, upto("dve_rows", ("amax", s)))
                        dve.tensor_scalar(up_amax[:, s:s + 1], up_amax[:, s:s + 1], 1e-5, 1.0 / 127.0, ALU.max, ALU.mult).then_inc(
                            dve_rows, step("dve_rows", ("clip", s)))
                        dve.wait_ge(dve_rows, upto("dve_rows", ("clip", s)))
                        dve.reciprocal(mcol[:, 7:8], up_amax[:, s:s + 1]).then_inc(dve_rows, step("dve_rows", ("inv", s)))

                    def mlp(s, early):
                        for t, n in mlp_chunk(st, s, early):
                            dve.wait_ge(h_pool, upto("h_pool", ("r", t, n)))
                            dve.wait_ge(shared_read, upto("shared_read", (("up", t, n), 0)))
                            dve.tensor_tensor(hh[:, n, :], hh[:, n, :], uc[:], ALU.mult).then_inc(
                                h_dve, step("h_dve", ("h", t, n)))
                            dve.wait_ge(h_dve, upto("h_dve", ("h", t, n)))
                            dve.tensor_reduce(hmx[:, n:n + 1], hh[:, n, :], AXX, ALU.max, apply_absolute_value=True).then_inc(
                                h_dve, step("h_dve", ("max", t, n)))
                            if n == NF - 1:
                                dve.wait_ge(h_dve, upto("h_dve", ("max", t, n)))
                                if t:
                                    dve.wait_ge(h_pool, upto("h_pool", ("q", t - 1, NF - 1)))
                                dve.tensor_reduce(hcol[:, 0:1], hmx[:], AXX, ALU.max).then_inc(h_dve, step("h_dve", ("amax", t)))
                                dve.wait_ge(h_dve, upto("h_dve", ("amax", t)))
                                dve.tensor_scalar(hcol[:, 1:2], hcol[:, 0:1], 1e-5, 1.0 / 127.0, ALU.max, ALU.mult).then_inc(
                                    h_dve, step("h_dve", ("clip", t)))
                                dve.wait_ge(h_dve, upto("h_dve", ("clip", t)))
                                dve.reciprocal(hcol[:, 2:3], hcol[:, 1:2]).then_inc(h_dve, step("h_dve", ("inv", t)))

                    def down(s):
                        for t in mlp_down(st, s):
                            dve.wait_ge(shared_full, upto("shared_full", ("down", t)))
                            dve.wait_ge(x2res_in, upto("x2res_in", t, 16))
                            dve.wait_ge(h_pool, upto("h_pool", ("scale", t)))
                            dve.scalar_tensor_tensor(x2res[:], shared_ps[C.bank[("down", t)]][:], hcol[:, 3:4], x2res[:],
                                                     ALU.mult, ALU.add).then_inc(h_dve, step("h_dve", ("out", t)))

                    def feed_stats_of(s):
                        for f in feeds(st, s):
                            if f[1] == "ctx":
                                continue
                            n, p = ring[f], normed.index(f)
                            dve.wait_ge(feed_in[n % 4], upto(f"feed_in{n % 4}", f, 16))
                            if p:
                                dve.wait_ge(feed_stats, upto("feed_stats", (normed[p - 1], 1)))
                            dve.bn_stats(fstat[:], feed[n % 4][:]).then_inc(feed_stats, step("feed_stats", (f, 0)))
                            dve.wait_ge(feed_stats, upto("feed_stats", (f, 0)))
                            if p:
                                dve.wait_ge(feed_pool, upto("feed_pool", (normed[p - 1], 4)))
                            dve.bn_aggr(fmv[:], fstat[:]).then_inc(feed_stats, step("feed_stats", (f, 1)))

                    def sum_squares(s):
                        g = self_group(st, s)
                        if s % NT == 3 and g:
                            dve.wait_ge(sq_done, upto("sq_done", g))
                            dve.wait_ge(shat_done, upto("shat_done", g - 1))
                            dve.tensor_reduce(srs[:], ssq[:].rearrange("p t (h d) -> p (t h) d", d=HD), AXX, ALU.add).then_inc(
                                sumsq_done, step("sumsq_done", g))

                    def norm_cross(m):
                        if m in C.apply_cross:
                            norm(m, co_ps, co_full, co_recip, co_norm, co_r, co, "co")

                    for s in range(SLOTS):
                        top_half(s, 0, "max")
                        row_maxima(s)
                        norm_cross(s - 2)
                        down(s - 1)
                        sum_squares(s)
                        top_half(s, 0, "replace")
                        row_scale(s - 1)
                        top_half(s, 1, "max")
                        mlp(s - 1, False)
                        top_half(s, 1, "replace")
                        if s - 1 in C.apply_self:
                            norm(s - 1, so_ps, so_full, so_recip, so_norm, so_r, so, "so")
                        if st.self_now:
                            n = (s % NT + 1) * P
                            for j in range(HG):
                                dve.wait_ge(sscore_read, upto("sscore_read", (s, j)))
                                if j == 0 and s:
                                    dve.wait_ge(sbias, upto("sbias", s - 1))
                                    dve.wait_ge(smax, upto("smax", (s - 1, HG - 1)))
                                dve.reduce_max(smx[:, j:j + 1], sP[j][:, 0:n], AXX).then_inc(smax, step("smax", (s, j)))
                        top_half(s, 2, "max")
                        cross_rows(s)
                        feed_stats_of(s)
                        top_half(s, 2, "replace")
                        self_rows(s)
                        mlp(s, True)
                        if st.cross_now:
                            for half, j in LAST_ORDER:
                                top_step(s, ROUNDS - 1, half, j)
                    norm_cross(SLOTS - 2)
                    down(SLOTS - 1)

                @block.gpsimd
                def _(pool):
                    def layer_norm(src, dst, mvt, col, name, sem_, label, ready):
                        ready()
                        pool.tensor_scalar(col[:, 0:1], mvt[:, 1:2], 1.0, EPS, ALU.mult, ALU.add).then_inc(sem_, step(name, label(0)))
                        pool.wait_ge(sem_, upto(name, label(0)))
                        pool.tensor_tensor(col[:, 1:2], col[:, 0:1], minus_half[:, 0:1], ALU.pow).then_inc(sem_, step(name, label(1)))
                        pool.wait_ge(sem_, upto(name, label(1)))
                        pool.tensor_tensor(col[:, 2:3], mvt[:, 0:1], col[:, 1:2], ALU.mult).then_inc(sem_, step(name, label(2)))
                        pool.wait_ge(sem_, upto(name, label(2)))
                        pool.tensor_scalar(col[:, 3:4], col[:, 2:3], -1.0, 0.0, ALU.mult, ALU.add).then_inc(sem_, step(name, label(3)))
                        pool.wait_ge(sem_, upto(name, label(3)))
                        return pool.tensor_scalar(dst, src, col[:, 1:2], col[:, 3:4], ALU.mult, ALU.add)

                    def rows_ln(s):
                        if s >= NT or not st.mlp:
                            return

                        def ready():
                            pool.wait_ge(dve_rows, upto("dve_rows", ("aggr", s)))
                            if s:
                                pool.wait_ge(shared_full, upto("shared_full", ("x2T", s - 1)))
                                pool.wait_ge(pool_rows, upto("pool_rows", ("quant", s - 1, 2)))
                        layer_norm(x2t[:], x2h[:], mv, mcol, "pool_rows", pool_rows, lambda k: ("ln", s, k), ready).then_inc(
                            pool_rows, step("pool_rows", ("ln", s, 4)))
                        pool.wait_ge(pool_rows, upto("pool_rows", ("ln", s, 4)))
                        pool.tensor_scalar(mcol[:, 4:5], wscale[:, 0:1], 0.5, 0.0, ALU.mult, ALU.add).then_inc(
                            pool_rows, step("pool_rows", ("ln", s, 5)))

                    def rows_quant(s):
                        if not 0 <= s < NT or not st.mlp:
                            return
                        pool.wait_ge(dve_rows, upto("dve_rows", ("inv", s)))
                        pool.wait_ge(pool_rows, upto("pool_rows", ("ln", s, 5)))
                        pool.tensor_tensor(gate_scale[:, s, 0:1], up_amax[:, s:s + 1], mcol[:, 4:5], ALU.mult).then_inc(
                            pool_rows, step("pool_rows", ("quant", s, 0)))
                        pool.wait_ge(pool_rows, upto("pool_rows", ("quant", s, 0)))
                        pool.tensor_scalar(gate_scale[:, s, 1:2], gate_scale[:, s, 0:1], up_amax[:, s:s + 1], wscale[:, 1:2],
                                           ALU.mult, ALU.mult).then_inc(pool_rows, step("pool_rows", ("quant", s, 1)))
                        pool.tensor_scalar(x2h[:], x2h[:], mcol[:, 7:8], MAGIC, ALU.mult, ALU.add).then_inc(
                            pool_rows, step("pool_rows", ("quant", s, 2)))

                    def silu(s, early):
                        for t, n in mlp_chunk(st, s, early):
                            pool.wait_ge(shared_read, upto("shared_read", (("gate", t, n), 1)))
                            pool.tensor_scalar(th[:], th[:], 1.0, 1.0, ALU.add, ALU.mult).then_inc(h_pool, step("h_pool", ("t1", t, n)))
                            pool.wait_ge(h_pool, upto("h_pool", ("t1", t, n)))
                            pool.tensor_tensor(hh[:, n, :], th[:], hh[:, n, :], ALU.mult).then_inc(
                                h_pool, step("h_pool", ("r", t, n)))

                    def inner_quant(s):
                        for t, n in mlp_chunk(st, s, False):
                            if n == NF - 1:
                                pool.wait_ge(h_dve, upto("h_dve", ("inv", t)))
                                if t:
                                    pool.wait_ge(h_dve, upto("h_dve", ("out", t - 1)))
                                pool.tensor_tensor(hcol[:, 3:4], hcol[:, 1:2], wscale[:, 2:3], ALU.mult).then_inc(
                                    h_pool, step("h_pool", ("scale", t)))
                                for q in range(NF):
                                    pool.tensor_scalar(hh[:, q, :], hh[:, q, :], hcol[:, 2:3], MAGIC, ALU.mult, ALU.add).then_inc(
                                        h_pool, step("h_pool", ("q", t, q)))

                    def squares(s):
                        g = self_group(st, s)
                        if s % NT == 2 and g:
                            pool.wait_ge(shared_read, upto("shared_read", (("self_qkv", g, NT - 1), 0)))
                            pool.wait_ge(sumsq_done, upto("sumsq_done", g - 1))
                            pool.tensor_tensor(ssq[:], sqk[:], sqk[:], ALU.mult).then_inc(sq_done, step("sq_done", g))

                    def head_norm(s):
                        g = self_group(st, s)
                        if s % NT == 3 and g:
                            pool.wait_ge(sumsq_done, upto("sumsq_done", g))
                            pool.tensor_scalar(srs[:], srs[:], 1.0 / HD, EPS, ALU.mult, ALU.add).then_inc(
                                rstd_done, step("rstd_done", (g, 0)))
                            pool.wait_ge(rstd_done, upto("rstd_done", (g, 0)))
                            pool.tensor_tensor(srs[:], srs[:], minus_half[:], ALU.pow).then_inc(
                                rstd_done, step("rstd_done", (g, 1)))
                            pool.wait_ge(rstd_done, upto("rstd_done", (g, 1)))
                            q = sqk[:].rearrange("p t (h d) -> p (t h) d", d=HD)
                            pool.tensor_tensor(q, q, srs[:].unsqueeze(2).to_broadcast([P, 2 * NT * HG, HD]), ALU.mult).then_inc(
                                shat_done, step("shat_done", g))

                    for s in range(SLOTS):
                        m = s - 1
                        if m in C.apply_cross:
                            for j in range(HG):
                                pool.wait_ge(crest, upto("crest", (m, j)))
                                pool.tensor_tensor(cS[m % 2][j][:], cS[m % 2][j][:], cW[j][:], ALU.subtract).then_inc(
                                    cprob, step("cprob", (m, j)))
                        silu(m, False)
                        rows_quant(m)
                        if st.cross_now:
                            pool.wait_ge(rmax_done, upto("rmax", s))
                            if s:
                                pool.wait_ge(crest, upto("crest", (s - 2, HG - 1)))
                            pool.tensor_scalar(cnb[s % 2][:], rowmax[:], -SCALE, 0.0, ALU.mult, ALU.add).then_inc(
                                cbias, step("cbias", s))
                        inner_quant(m)
                        if st.self_now:
                            pool.wait_ge(smax, upto("smax", (s, HG - 1)))
                            if s:
                                pool.wait_ge(sexp, upto("sexp", (s - 1, HG - 1)))
                            pool.tensor_scalar(snb[:], smx[:], -SCALE, 0.0, ALU.mult, ALU.add).then_inc(sbias, step("sbias", s))
                        silu(s, True)
                        squares(s)
                        head_norm(s)
                        rows_ln(s)
                        for f in feeds(st, s):
                            if f[1] == "ctx":
                                continue
                            n, p = ring[f], normed.index(f)

                            def ready():
                                pool.wait_ge(feed_stats, upto("feed_stats", (f, 1)))
                                if p:
                                    pool.wait_ge(feed_pool, upto("feed_pool", (normed[p - 1], 4)))
                            layer_norm(feed[n % 4][:], feed[n % 4][:], fmv, fcol, "feed_pool", feed_pool, lambda k: (f, k),
                                       ready).then_inc(feed_pool, step("feed_pool", (f, 4)))

            C.end()

        def iteration(i, st):
            one_iteration(i, st)
            nc.gpsimd.sem_clear(range(min(nums), max(nums) + 1))
            nc.all_engine_barrier()

        steady = [i for i in range(LO, HI + 1) if Stages(i).key() == Stages(3).key()]
        for i in range(LO, steady[0]):
            iteration(i, Stages(i))
        with nc.Fori(steady[0], steady[-1] + 1) as i:
            iteration(i, Stages(steady[0]))
        for i in range(steady[-1] + 1, HI + 1):
            iteration(i, Stages(i))


def setup(nc, T):
    W_attn, b_attn, wa_dram, wc_dram = T["W_attn"], T["b_attn"], T["wa_dram"], T["wc_dram"]
    banks, ident, ident16, mask16, ones16, bias16 = (T[k] for k in ("banks", "ident", "ident16", "mask16", "ones16", "bias16"))
    minus_half, gb, wscale, wproj, woT = (T[k] for k in ("minus_half", "gb", "wscale", "wproj", "woT"))
    wgT, wuT, wdT = T["wgT"], T["wuT"], T["wdT"]
    with ExitStack() as tmp:
        def sb(name, shape, dt=F32):
            return tmp.enter_context(nc.sbuf_tensor(name, shape, dt))

        def sem(name):
            return tmp.enter_context(nc.semaphore(name))

        wnat = sb("wnat", [P, NC, 3 * D])
        hmean = sb("hmean", [P, NC + 1, 2 * H])
        brow = sb("brow", [1, 8 * D])
        bpart = sb("bpart", [1, 3, 8 * D], BF16)
        wx = [sb(f"wx{k}", [P, NC, D]) for k in range(2)]
        wcT = sb("wcT", [P, NC, 3, D])
        ones32 = sb("ones32", [P, P])
        s_const, s_b, s_bp, s_bd, s_w, s_mean, s_cent, s_out = (sem(f"su_{n}") for n in (
            "const", "b", "bp", "bd", "w", "mean", "cent", "out"))
        s_x = [sem(f"su_x{k}") for k in range(2)]
        s_xp, s_xa, s_res = sem("su_xp"), sem("su_xa"), sem("su_res")
        NBIAS = 4 + 3 * NG
        with nc.Block() as block:
            @block.sync
            def _(sp):
                sp.dma_start(wnat[:], W_attn.rearrange("(c p) n -> p c n", p=P)).then_inc(s_w, 16)
                sp.dma_start(brow[:, 0:3 * D], b_attn.rearrange("(a n) -> a n", a=1)).then_inc(s_b, 16)
                for g in range(NG):
                    for k, b in enumerate((T["bq"], T["bk"], T["bv"])):
                        sp.dma_start(brow[:, 3 * D + (3 * g + k) * P:3 * D + (3 * g + k + 1) * P],
                                     b[g * P:(g + 1) * P].rearrange("(a n) -> a n", a=1)).then_inc(s_b, 16)
                for k, b in enumerate((T["b_proj"], T["bo"])):
                    sp.dma_start(brow[:, (6 + k) * D:(7 + k) * D], b.rearrange("(a n) -> a n", a=1)).then_inc(s_b, 16)
                for k, v in enumerate((T["q_gamma"], T["q_beta"], T["k_gamma"], T["k_beta"])):
                    for j in range(HG):
                        sp.dma_start(gb[j * HD:(j + 1) * HD, k:k + 1], v.rearrange("(n a) -> n a", a=1)).then_inc(s_res, 16)
                sp.dma_start(wproj[:], T["W_proj"].rearrange("(c p) n -> p c n", p=P)).then_inc(s_res, 16)
                for k, w in enumerate((T["Wq"], T["Wk"], T["Wv"], T["Wo"])):
                    if k >= 2:
                        sp.wait_ge(s_xp, NC * (k - 1))
                    sp.dma_start(wx[k % 2][:], w.rearrange("(c p) n -> p c n", p=P)).then_inc(s_x[k % 2], 16)
                sp.wait_ge(s_bp, 5)
                for base, lo, n in ((0, 0, 3 * D), (32, 3 * D, 3 * D), (64, 6 * D, 2 * D)):
                    for r in range(3):
                        sp.dma_start(bias16[base + r:base + r + 1, 0:n], bpart[:, r, lo:lo + n]).then_inc(s_bd, 16)
                sp.wait_ge(s_bd, 9 * 16)
                sp.wait_ge(s_cent, 2)
                for g in range(NG):
                    for part in range(3):
                        sp.dma_start(wa_dram[g, :, :, part, :],
                                     wnat[:, :, part * D + g * P:part * D + (g + 1) * P]).then_inc(s_out, 16)
                sp.wait_ge(s_xa, 3 * NC)
                for g in range(NG):
                    for part in range(3):
                        sp.dma_start(wc_dram[g, :, :, part, :],
                                     wcT[:, :, part, g * P:(g + 1) * P]).then_inc(s_out, 16)
                sp.wait_ge(s_out, 2 * 3 * NG * 16)
                sp.wait_ge(s_res, 17 * 16)

            @block.gpsimd
            def _(pool):
                pool.memset(ident[:], 0.0).then_inc(s_const, 1)
                pool.memset(mask16[:], 0.0).then_inc(s_const, 1)
                pool.memset(ones16[:], 1.0)
                pool.memset(ones32[:], 1.0)
                pool.memset(minus_half[:], -0.5)
                pool.wait_ge(s_const, 2)
                pool.affine_select(out=ident[:], in_=ident[:], compare_op=ALU.not_equal, fill=1.0, base=0,
                                   pattern=[[-1, P]], channel_multiplier=1).then_inc(s_const, 1)
                pool.affine_select(out=mask16[:], in_=mask16[:], compare_op=ALU.is_ge, fill=MASKED, base=0,
                                   pattern=[[-1, P]], channel_multiplier=1).then_inc(s_const, 1)
                pool.wait_ge(s_const, 3)
                pool.tensor_copy(ident16[:], ident[:])

            @block.vector
            def _(dve):
                dve.wait_ge(s_w, 16)
                for c in range(NC):
                    dve.tensor_reduce(hmean[:, c, :], wnat[:, c, 0:2 * D].rearrange("p (h d) -> p h d", d=HD),
                                      AXX, ALU.add).then_inc(s_mean, 1)
                dve.wait_ge(s_b, 18 // 1 * 0 + 16 * (1 + 3 * NG + 2))
                dve.tensor_reduce(hmean[0:1, NC, :], brow[:, 0:2 * D].rearrange("p (h d) -> p h d", d=HD),
                                  AXX, ALU.add).then_inc(s_mean, 1)
                dve.wait_ge(s_mean, NC + 1)
                dve.tensor_scalar(hmean[:, 0:NC, :], hmean[:, 0:NC, :], 1.0 / HD, None, ALU.mult).then_inc(s_mean, 1)
                dve.tensor_scalar(hmean[0:1, NC, :], hmean[0:1, NC, :], 1.0 / HD, None, ALU.mult).then_inc(s_mean, 1)
                dve.wait_ge(s_mean, NC + 3)
                for c in range(NC):
                    w = wnat[:, c, 0:2 * D].rearrange("p (h d) -> p h d", d=HD)
                    ins = dve.tensor_tensor(w, w, hmean[:, c, :].unsqueeze(2).to_broadcast([P, 2 * H, HD]), ALU.subtract)
                ins.then_inc(s_cent, 1)
                b = brow[:, 0:2 * D].rearrange("p (h d) -> p h d", d=HD)
                dve.tensor_tensor(b, b, hmean[0:1, NC, :].unsqueeze(2).to_broadcast([1, 2 * H, HD]),
                                  ALU.subtract).then_inc(s_cent, 1)
                dve.wait_ge(s_cent, 2)
                dve.tensor_copy(bpart[:, 0, :], brow[:]).then_inc(s_bp, 1)
                dve.wait_ge(s_bp, 1)
                dve.tensor_tensor(brow[:], brow[:], bpart[:, 0, :], ALU.subtract).then_inc(s_bp, 1)
                dve.wait_ge(s_bp, 2)
                dve.tensor_copy(bpart[:, 1, :], brow[:]).then_inc(s_bp, 1)
                dve.wait_ge(s_bp, 3)
                dve.tensor_tensor(brow[:], brow[:], bpart[:, 1, :], ALU.subtract).then_inc(s_bp, 1)
                dve.wait_ge(s_bp, 4)
                dve.tensor_copy(bpart[:, 2, :], brow[:]).then_inc(s_bp, 1)

            @block.tensor
            def _(pe):
                pe.wait_ge(s_const, 3)
                for k in range(4):
                    pe.wait_ge(s_x[k % 2], 16 * (k // 2 + 1))
                    for o in range(NC):
                        n = k * NC + o
                        if n >= 2:
                            pe.wait_ge(s_xa, n - 1)
                        for c in range(NC):
                            mm = pe.transpose(banks[n % 2][:, c * P:(c + 1) * P], wx[k % 2][:, o, c * P:(c + 1) * P], ident[:])
                        mm.then_inc(s_xp, 1)

            @block.scalar
            def _(act):
                for k in range(4):
                    for o in range(NC):
                        n = k * NC + o
                        act.wait_ge(s_xp, n + 1)
                        dst = woT[:, :, o * P:(o + 1) * P] if k == 3 else wcT[:, :, k, o * P:(o + 1) * P]
                        act.activation(dst, banks[n % 2][:].rearrange("p (c n) -> p c n", c=NC), ACT.Copy).then_inc(s_xa, 1)

    with ExitStack() as tmp:
        def sem(name):
            return tmp.enter_context(nc.semaphore(name))

        natural = [tmp.enter_context(nc.sbuf_tensor(f"wnat{k}", [P, 16, 512], F32)) for k in range(3)]
        scratch = tmp.enter_context(nc.sbuf_tensor("scratch", [P, F], BF16))
        ones32 = tmp.enter_context(nc.sbuf_tensor("ones32b", [P, P], F32))
        sums = tmp.enter_context(nc.sbuf_tensor("sums", [P, 3, 4], F32))
        sum3 = tmp.enter_context(nc.sbuf_tensor("sum3", [P, 3], F32))
        winv = tmp.enter_context(nc.sbuf_tensor("winv", [P, 3], F32))
        s_in = [sem(f"sf_in{k}") for k in range(3)]
        s_one, s_abs, s_sum, s_tot, s_q, s_p, s_a = (sem(f"sf_{n}") for n in ("one", "abs", "sum", "tot", "q", "p", "a"))
        with nc.Block() as block:
            @block.sync
            def _(sp):
                for k, w in enumerate((T["w_gate"], T["w_up"])):
                    sp.dma_start(natural[k][:], w.rearrange("(o p) n -> p o n", p=P)).then_inc(s_in[k], 16)
                sp.dma_start(natural[2][:].rearrange("p (a q) n -> p a (q n)", a=4),
                             T["w_down"].rearrange("(a p) n -> p a n", p=P)).then_inc(s_in[2], 16)

            @block.gpsimd
            def _(pool):
                pool.memset(ones32[:], 1.0).then_inc(s_one, 1)

            @block.scalar
            def _(act):
                for k in range(3):
                    act.wait_ge(s_in[k], 16)
                    for q in range(4):
                        n = 4 * k + q
                        if n:
                            act.wait_ge(s_abs, n)
                        act.activation(scratch[:].rearrange("p (a n) -> p a n", a=4), natural[k][:, 4 * q:4 * q + 4, :],
                                       ACT.Abs, accum_out=sums[:, k, q:q + 1]).then_inc(s_abs, 1)
                for n in range(48):
                    k, u = n // 16, n % 16
                    act.wait_ge(s_p, n + 2)
                    src = banks[n % 4][:].rearrange("p (c n) -> p c n", c=4)
                    dst = (wdT[:, 4 * (u % 4):4 * (u % 4) + 4, (u // 4) * P:(u // 4 + 1) * P] if k == 2
                           else (wgT, wuT)[k][:, :, u * P:(u + 1) * P])
                    act.activation(dst, src, ACT.Copy, bias=-MAGIC, saturate=False).then_inc(s_a, 1)

            @block.vector
            def _(dve):
                dve.wait_ge(s_abs, 12)
                dve.tensor_reduce(sum3[:], sums[:], AXX, ALU.add).then_inc(s_sum, 1)
                dve.wait_ge(s_p, 1)
                dve.tensor_scalar(wscale[:], banks[7][:, 0:3], 1.0 / (F * D), 1e-5, ALU.mult, ALU.max).then_inc(s_tot, 1)
                dve.wait_ge(s_tot, 1)
                dve.reciprocal(winv[:], wscale[:]).then_inc(s_tot, 1)
                dve.wait_ge(s_tot, 2)
                for n in range(48):
                    k, u = n // 16, n % 16
                    w = natural[k][:, u, :]
                    dve.tensor_scalar(w, w, winv[:, k:k + 1], 1.0, ALU.mult, ALU.min).then_inc(s_q, 1)
                    dve.wait_ge(s_q, 2 * n + 1)
                    dve.tensor_scalar(w, w, -1.0, MAGIC, ALU.max, ALU.add).then_inc(s_q, 1)

            @block.tensor
            def _(pe):
                pe.wait_ge(s_one, 1)
                pe.wait_ge(s_sum, 1)
                pe.matmul(banks[7][:, 0:3], ones32[:], sum3[:], start=True, stop=True).then_inc(s_p, 1)
                for n in range(48):
                    k, u = n // 16, n % 16
                    if n >= 4:
                        pe.wait_ge(s_a, n - 3)
                    pe.wait_ge(s_q, 2 * n + 2)
                    for b in range(4):
                        mm = pe.transpose(banks[n % 4][:, b * P:(b + 1) * P], natural[k][:, u, b * P:(b + 1) * P], ident[:])
                    mm.then_inc(s_p, 1)


NAMES = ["x", "ctx_1024", "L0_attn_W_attn", "L0_attn_b_attn", "L0_attn_W_proj", "L0_attn_b_proj",
         "L0_attn_q_gamma", "L0_attn_q_beta", "L0_attn_k_gamma", "L0_attn_k_beta", "L0_xattn_Wq",
         "L0_xattn_bq", "L0_xattn_Wk", "L0_xattn_bk", "L0_xattn_Wv", "L0_xattn_bv", "L0_xattn_Wo",
         "L0_xattn_bo", "L0_ffn_w_gate", "L0_ffn_w_up", "L0_ffn_w_down"]


def kernel(**inputs):
    import concourse.bacc as bacc
    from concourse.bass_utils import run_bass_kernel_spmd

    nc = bacc.Bacc("TRN2", target_bir_lowering=False, num_devices=1)
    arrays, args = {}, []
    for name in NAMES:
        a = np.ascontiguousarray(inputs[name])
        arrays[f"in_{name}"] = a
        args.append(nc.dram_tensor(f"in_{name}", a.shape, mybir.dt.from_np(a.dtype), kind="ExternalInput").ap())
    out = nc.dram_tensor("out_y", (NB, S, D), F32, kind="ExternalOutput").ap()
    decoder_layer(nc, *args, out)
    r = run_bass_kernel_spmd(nc, [arrays], core_ids=[0])
    return r.results[0]["out_y"]
```

```python
from contextlib import ExitStack

import numpy as np

import concourse.bass as bass
from concourse import mybir

F32 = mybir.dt.float32
F32R = mybir.dt.float32r
BF16 = mybir.dt.bfloat16
FP8 = mybir.dt.float8e4
ALU = mybir.AluOpType
ACT = mybir.ActivationFunctionType
AXX = mybir.AxisListType.X

P = 128
NB, S, D = 8, 512, 512
H, HD = 16, 32
F = 2048
NT = S // P
NC = D // P
HG = P // HD
NG = H // HG
NF = F // 512
KF = F // P
ROUNDS = 4
SLOTS = NG * NT
SCALE = float(HD) ** -0.5
EPS = 1e-5
MAGIC = 1.5 * 2.0 ** 23
MASKED = -1e30
RING = 3
REPLACED = -3e38
LO, HI = -1, NB + 2


SIGNALS = ["shared_full", "shared_read", "score_full", "score_read", "turned_full", "turned_read",
           "smax", "sexp", "sbias", "cbias", "cexp", "topk", "so_full", "so_recip",
           "so_norm", "crest", "cprob", "co_full", "co_recip", "co_norm",
           "sq_done", "rstd_done", "shat_done", "sumsq_done", "dve_rows", "pool_rows", "feed_stats",
           "feed_pool", "h_dve", "h_pool", "rmax", "w_in", "feed_in0", "feed_in1", "feed_in2",
           "head_affine", "stage_high", "stage_low", "xres_in", "x1res_in", "x1_out", "x2_out", "x2res_in", "y_out"]


class Stages:

    def __init__(self, i):
        def on(b):
            return 0 <= b < NB
        self.self_now, self.self_next, self.self_last = on(i), on(i + 1), on(i - 1)
        self.proj1 = on(i - 1)
        self.cross_now, self.cross_next, self.cross_last = on(i - 2), on(i - 1), on(i - 3)
        self.mlp = on(i - 3)

    def key(self):
        return (self.self_now, self.self_next, self.self_last, self.proj1, self.cross_now, self.cross_next,
                self.cross_last, self.mlp)


def feeds(st, s):
    order = [(src, t) for src in ("x", "x1", "ctx") for t in range(NT)]
    slots = [10, 10, 10, 11, 11, 11, 12, 12, 12, 13, 13, 13]
    return [(k, src, t) for k, (src, t) in enumerate(order) if slots[k] == s
            and (st.self_next if src == "x" else st.cross_next)]


def all_feeds(st):
    return [f for s in range(SLOTS) for f in feeds(st, s)]


def self_group(st, s):
    g = s // NT + 1
    return g if (st.self_next if g == NG else st.self_now) else None


def cross_group(st, s):
    g = s // NT + 1
    return g if (st.cross_next if g == NG else st.cross_now) else None


def mlp_chunk(st, s, early):
    t, r = (s - 4) // 3, (s - 4) % 3
    return [(t, 2 * r + (not early))] if st.mlp and s >= 4 and t < NT and r < 2 else []


def mlp_down(st, s):
    return [(s - 6) // 3] if st.mlp and s >= 6 and (s - 6) % 3 == 0 else []


def early_units(st, s):
    u = []
    for kind in ("oT", "out"):
        if st.mlp and s < NT:
            u.append(("cross_" + kind, s))
        if st.proj1 and s < NT:
            u.append(("self_" + kind, s))
    if st.mlp and 1 <= s <= NT:
        u.append(("x2T", s - 1))
    for t, n in mlp_chunk(st, s, True):
        u += [("gate", t, n), ("up", t, n)]
    if s % NT == 3 and cross_group(st, s):
        u += [("cross_k", cross_group(st, s), t) for t in range(NT)] + [("cross_q", s + 1)]
    return u


def mid_units(st, s):
    u = []
    if (s + 1) % NT and st.self_now:
        u.append(("self_q", s + 1))
    g = self_group(st, s)
    if g:
        u += [[("self_qkv", g, t) for t in range(NT - 1)], [("self_qkv", g, NT - 1)], [],
              [("self_k", g, t) for t in range(NT)]][s % NT]
    g = cross_group(st, s)
    if g:
        u += [("cross_qkv", g, t) for t in ((), (), range(NT), ())[s % NT]]
    for t in mlp_down(st, s):
        u += [("hT", t, q) for q in range(NF)]
    return u


def mid_chunk(st, s, j):
    u = mid_units(st, s)
    return [u[k] for k in range(len(u)) if k * HG // len(u) == j]


def late_units(st, s):
    u = []
    if (s + 2) % NT and (st.cross_now if s + 2 < SLOTS else st.cross_next):
        u.append(("cross_q", s + 2))
    u += [("feed", *f) for f in feeds(st, s)]
    for t, n in mlp_chunk(st, s, False):
        u += [("gate", t, n), ("up", t, n)]
    for t in mlp_down(st, s):
        u.append(("down", t))
    if s % NT == 3 and self_group(st, s):
        u.append(("self_q", s + 1))
    return u


def shared_units(st, s):
    return early_units(st, s) + mid_units(st, s) + late_units(st, s)


ACT_READS = {"cross_oT": 1, "self_oT": 1, "hT": 1, "x2T": 1, "gate": 2, "up": 1, "self_qkv": 3, "cross_qkv": 2,
             "self_k": 1, "cross_k": 1, "self_q": 1, "cross_q": 1, "feed": 1}


STACKED = {"self_q", "self_k", "cross_q", "cross_k"}
STAGES = 3


TOP_PARTS = [
    [(0, "max", j) for j in range(HG)],
    [step for j in range(HG) for step in ((0, "replace", j), (1, "max", j))],
    [(1, "replace", j) for j in range(HG)],
    [(2, "max", j) for j in range(HG)],
    [(2, "replace", j) for j in range(HG)],
    [(3, "max", 0)] + [step for j in range(1, HG) for step in ((3, "max", j), (3, "replace", j - 1))] + [(3, "replace", HG - 1)],
]


class Counts:

    def __init__(self, st):
        self.order, self.given = {}, {}
        add = self._add
        apply_self = [s - 1 for s in range(SLOTS) if (st.self_last if s == 0 else st.self_now)]
        apply_cross = [s - 1 for s in range(SLOTS) if (st.cross_last if s == 0 else st.cross_now)]
        self.apply_self, self.apply_cross = apply_self, apply_cross
        self.bank, self.before = {}, {}
        held = [None, None]
        n = 0
        self.stacked = [u for s in range(SLOTS) for u in shared_units(st, s) if u[0] in STACKED]
        for s in range(SLOTS):
            for u in shared_units(st, s):
                self.bank[u], self.before[u] = n % 2, held[n % 2]
                held[n % 2] = u
                n += 1
                add("shared_full", u)
                for r in range(ACT_READS.get(u[0], 0)):
                    add("shared_read", (u, r))
        for s in range(SLOTS):
            if st.self_now:
                for j in range(HG):
                    for name in ("smax", "sexp"):
                        add(name, (s, j))
                add("sbias", s)
            if st.cross_now:
                add("rmax", s)
                add("cbias", s)
                for j in range(HG):
                    add("cexp", (s, j))
                    add("crest", (s, j))
                    add("cprob", (s, j))
                for part in TOP_PARTS:
                    for r, half, j in part:
                        add("topk", (s, r, half, j))
        for s in range(SLOTS):
            for which, on, n, applied in (("self", st.self_now, s, apply_self), (
                    "cross", st.cross_now if s < SLOTS - 1 else st.cross_next, s + 1, apply_cross)):
                for j in range(HG):
                    if on:
                        for name in ("score_full", "score_read"):
                            add(name, (which, n, j))
                    if s - 1 in applied:
                        for name in ("turned_full", "turned_read"):
                            add(name, (which, s - 1, j))
        for m in apply_self:
            add("so_full", m)
            add("so_recip", m)
            add("so_norm", m)
        for m in apply_cross:
            add("co_full", m)
            add("co_recip", m)
            add("co_norm", m)

    def _add(self, name, label):
        self.order.setdefault(name, {})[label] = len(self.order.get(name, {})) + 1

    def two_before(self, name, label):
        return max(0, self.order[name][label] - 2)

    def plan(self, name, label):
        self._add(name, label)

    def upto(self, name, label, each=1):
        return each * self.order.get(name, {}).get(label, 0)

    def step(self, name, label, each=1):
        self.given[name] = self.given.get(name, 0) + 1
        assert self.order[name][label] == self.given[name], (name, label)
        return each

    def end(self):
        for name, labels in self.order.items():
            assert self.given.get(name, 0) == len(labels), (name, self.given.get(name, 0), len(labels))


def decoder_layer(nc, x, ctx_in, W_attn, b_attn, W_proj, b_proj, q_gamma, q_beta, k_gamma, k_beta,
                  Wq, bq, Wk, bk, Wv, bv, Wo, bo, w_gate, w_up, w_down, out):
    x_rows = x.rearrange("b s d -> (b s) d")
    ctx_rows = ctx_in.rearrange("b s d -> (b s) d")
    out_rows = out.rearrange("b s d -> (b s) d")
    wa_dram = nc.dram_tensor("wa_by_group", (NG, P, NC, 3, P), F32, kind="Internal").ap()
    wc_dram = nc.dram_tensor("wc_by_group", (NG, P, NC, 3, P), F32, kind="Internal").ap()
    x1_rows = nc.dram_tensor("x1_rows", (NB * S, D), F32, kind="Internal").ap()
    x2_rows = nc.dram_tensor("x2_rows", (NB * S, D), F32, kind="Internal").ap()

    with ExitStack() as keep:
        def sb(name, shape, dt=F32, stack=keep):
            return stack.enter_context(nc.sbuf_tensor(name, shape, dt))

        def sem(name, stack=keep):
            return stack.enter_context(nc.semaphore(name))

        banks = [keep.enter_context(nc.psum_tensor(f"bank{k}", [P, 512], F32)) for k in range(8)]
        score_ps, turned_ps, co_ps, so_ps = banks[0:2], banks[2:4], banks[4], banks[5]
        shared_ps = banks[6:]

        ident = sb("ident", [P, P])
        ident16 = sb("ident16", [P, P], BF16)
        mask16 = sb("mask16", [P, P], BF16)
        ones16 = sb("ones16", [96, P], BF16)
        bias16 = sb("bias16", [96, 3 * D], BF16)
        minus_half = sb("minus_half", [P, 32])
        ident_r = sb("ident_r", [P, P], F32R)
        gb = sb("gb", [P, 4, HD])
        wscale = sb("wscale", [P, 3])
        wproj = sb("wproj", [P, NC, D])
        woT = sb("woT", [P, NC, D])
        wgT = sb("wgT", [P, NC, F], FP8)
        wuT = sb("wuT", [P, NC, F], FP8)
        wdT = sb("wdT", [P, KF, D], FP8)

        setup(nc, dict(W_attn=W_attn, b_attn=b_attn, wa_dram=wa_dram, wc_dram=wc_dram, banks=banks,
                       ident=ident, ident16=ident16, ident_r=ident_r, mask16=mask16, ones16=ones16, bias16=bias16,
                       minus_half=minus_half, gb=gb, wscale=wscale, wproj=wproj, woT=woT, wgT=wgT, wuT=wuT,
                       wdT=wdT, bq=bq, bk=bk, bv=bv, b_proj=b_proj, bo=bo, q_gamma=q_gamma, q_beta=q_beta,
                       k_gamma=k_gamma, k_beta=k_beta, W_proj=W_proj, Wq=Wq, Wk=Wk, Wv=Wv, Wo=Wo,
                       w_gate=w_gate, w_up=w_up, w_down=w_down))

        w_group = sb("w_group", [P, NC, 3 * P])
        feed = [sb(f"feed{k}", [P, D]) for k in range(RING)]
        xT = sb("xT", [P, NC, S])
        x1T = sb("x1T", [P, NC, S])
        ctxT = sb("ctxT", [P, NC, S])
        ssq = sb("ssq", [P, NT, 2, P])
        sx = sb("sx", [P, NT, 3, P])
        srs = sb("srs", [P, 2 * NT * HG])
        stage = [sb(f"stage{k}", [P, HG, 4, HD], F32R) for k in range(STAGES)]
        sq_stack, sk_stack = sb("sq_stack", [P, HG, P], F32R), sb("sk_stack", [P, HG, S], F32R)
        sv = [sb(f"sv{k}", [P, NT, HG, HD + 1]) for k in range(2)]
        sP = [sb(f"sP{j}", [P, S]) for j in range(HG)]
        sPT = [sb(f"sPT{k}", [P, S]) for k in range(2)]
        smx, snb = sb("smx", [P, HG]), sb("snb", [P, HG])
        so_r = sb("so_r", [P, HG])
        so = sb("so", [P, NT, D])
        cqk = sb("cqk", [P, NT, 2 * P])
        cq_stack, ck_stack = sb("cq_stack", [P, HG, P], F32R), sb("ck_stack", [P, HG, S], F32R)
        cv = [sb(f"cv{k}", [P, NT, HG, HD + 1]) for k in range(2)]
        cS = [[sb(f"cS{k}_{j}", [P, S]) for j in range(HG)] for k in range(2)]
        cW = [sb(f"cW{j}", [P, S]) for j in range(HG)]
        top8 = sb("top8", [P, HG, 8])
        rowmax = sb("rowmax", [P, HG])
        cnb = [sb(f"cnb{k}", [P, HG]) for k in range(2)]
        cPT = sPT
        co_r = sb("co_r", [P, HG])
        co = sb("co", [P, NT, D])
        self_oT = sb("self_oT", [P, NC, P])
        xres, x1res = feed[0], feed[1]
        x2T = sb("x2T", [P, NT, NC, P], BF16)
        mstat = sb("mstat", [P, 6])
        mv, mcol = sb("mv", [P, 2]), sb("mcol", [P, 8])
        gate_scale, up_amax = sb("gate_scale", [P, NT, 2]), sb("up_amax", [P, NT])
        th, uc = sb("th", [P, 512]), sb("uc", [P, 512])
        x2t, x2h = th, uc
        hh = sb("hh", [P, NF, 512])
        cross_oT = hh[:, NF - 1, :].rearrange("p (c n) -> p c n", c=NC)
        hmx, hcol = sb("hmx", [P, NF]), sb("hcol", [P, 4])
        hT = sb("hT", [P, KF, P], BF16)
        x2res = sb("x2res", [P, D])
        fstat = sb("fstat", [P, 6])
        fmv, fcol = [sb(f"fmv{k}", [P, 2]) for k in range(RING)], [sb(f"fcol{k}", [P, 4]) for k in range(RING)]

        sems = {n: sem(n) for n in SIGNALS}
        nums = [s.num for s in sems.values()]
        assert max(nums) - min(nums) == len(nums) - 1

        with nc.Block() as block:
            @block.vector
            def _(dve):
                for v in (*sv, *cv):
                    dve.memset(v[:, :, :, HD:HD + 1], 1.0)

        def one_iteration(i, st):
            C = Counts(st)
            upto, step = C.upto, C.step
            (shared_full, shared_read, score_full, score_read, turned_full, turned_read, smax, sexp, sbias, cbias,
             cexp, topk, so_full, so_recip, so_norm, crest, cprob, co_full,
             co_recip, co_norm, sq_done, rstd_done, shat_done, sumsq_done, dve_rows, pool_rows, feed_stats, feed_pool,
             h_dve, h_pool, rmax_done, w_in) = (sems[n] for n in SIGNALS[:32])
            head_affine, stage_high, stage_low = (sems[n] for n in ("head_affine", "stage_high", "stage_low"))
            feed_in = [sems[f"feed_in{k}"] for k in range(RING)]
            xres_in, x1res_in, x1_out, x2_out, x2res_in, y_out = (sems[n] for n in (
                "xres_in", "x1res_in", "x1_out", "x2_out", "x2res_in", "y_out"))
            def rows(ap, b, t):
                return ap[bass.ds(b * S + t * P, P), :]

            fs = all_feeds(st)
            ring = {f: n for n, f in enumerate(fs)}
            normed = [f for f in fs if f[1] != "ctx"]
            for f in fs:
                C.plan(f"feed_in{ring[f] % RING}", f)
            for f in normed:
                for k in range(2):
                    C.plan("feed_stats", (f, k))
                for k in range(5):
                    C.plan("feed_pool", (f, k))
            was = [g for g in range(1, NG + 2) if (st.self_next if g >= NG else st.self_now)]
            wcs = [g for g in range(1, NG + 2) if (st.cross_next if g >= NG else st.cross_now)]
            uses = sorted([(4 * (g - 1) - 1, "self", g) for g in was] + [(4 * (g - 1) + 2, "cross", g) for g in wcs if g <= NG])
            loads = [(max(0, at), which, g, (uses[k - 1][1] + "_qkv", uses[k - 1][2], NT - 1) if k else None)
                     for k, (at, which, g) in enumerate(uses) if (which, g) != ("self", 1)]
            for _, which, g, _ in loads:
                C.plan("w_in", (which, g))
            for g in was:
                if g <= NG:
                    C.plan("sq_done", g)
                    C.plan("sumsq_done", g)
                    C.plan("rstd_done", (g, 0))
                    C.plan("rstd_done", (g, 1))
                    C.plan("shat_done", g)
                    for k in range(4):
                        C.plan("head_affine", (g, k))
            for u in C.stacked:
                C.plan("stage_high", u)
                C.plan("stage_low", u)
            for t in range(NT):
                if st.proj1:
                    C.plan("xres_in", t)
                    C.plan("x1_out", t)
                if st.mlp:
                    C.plan("x1res_in", t)
                    C.plan("x2_out", t)
                    C.plan("x2res_in", t)
                    C.plan("y_out", t)
            for s in range(SLOTS):
                if 1 <= s <= NT and st.mlp:
                    for k in ("amax", "clip", "inv"):
                        C.plan("dve_rows", (k, s - 1))
                    for k in range(3):
                        C.plan("pool_rows", ("quant", s - 1, k))
                if s < NT and st.mlp:
                    for k in ("x2", "stats", "aggr"):
                        C.plan("dve_rows", (k, s))
                    for k in range(6):
                        C.plan("pool_rows", ("ln", s, k))
                if s < NT and st.proj1:
                    C.plan("dve_rows", ("x1", s))
                for t in mlp_down(st, s - 1):
                    C.plan("h_dve", ("out", t))
                for early, at in ((False, s - 1), (True, s)):
                    for t, n in mlp_chunk(st, at, early):
                        C.plan("h_pool", ("t1", t, n))
                        C.plan("h_pool", ("r", t, n))
                        C.plan("h_dve", ("h", t, n))
                        C.plan("h_dve", ("max", t, n))
                        if n == NF - 1:
                            for k in ("amax", "clip", "inv"):
                                C.plan("h_dve", (k, t))
                            C.plan("h_pool", ("scale", t))
                            for q in range(NF):
                                C.plan("h_pool", ("q", t, q))
            for t in mlp_down(st, SLOTS - 1):
                C.plan("h_dve", ("out", t))

            def freed(eng, u):
                b = C.before[u]
                if b is None:
                    return
                if b[0] in ACT_READS:
                    eng.wait_ge(shared_read, upto("shared_read", (b, ACT_READS[b[0]] - 1)))
                elif b[0] == "cross_out":
                    eng.wait_ge(dve_rows, upto("dve_rows", ("x2", b[1])))
                elif b[0] == "self_out":
                    eng.wait_ge(dve_rows, upto("dve_rows", ("x1", b[1])))
                else:
                    eng.wait_ge(h_dve, upto("h_dve", ("out", b[1])))

            def source(u):
                kind, t = u[0], (u[2] if u[0].endswith("_k") else u[1] % NT)
                x_ = {"self_k": sx[:, t, 1, :], "cross_k": cqk[:, t, P:2 * P], "cross_q": cqk[:, t, 0:P],
                      "self_q": sx[:, t, 2 * (u[1] // NT % 2), :]}[kind]
                return x_.rearrange("p (h d) -> p h d", d=HD).unsqueeze(2).to_broadcast([P, HG, 2, HD])

            def parts_of(u, low):
                buf = stage[C.stacked.index(u) % STAGES]
                return buf[:, :, 2 * low:2 * low + 2, :] if u[0].endswith("_q") else buf[:, :, low::2, :]

            def four(ap):
                return ap.rearrange("p (c n) -> p c n", c=4)

            with nc.Block() as block:
                @block.sync
                def _(sp):
                    def load_weights(which, g, before):
                        if before:
                            sp.wait_ge(shared_full, upto("shared_full", before))
                        sp.dma_start(w_group[:].rearrange("p c (k n) -> p c k n", k=3),
                                     (wa_dram if which == "self" else wc_dram)[g % NG]).then_inc(
                                         w_in, step("w_in", (which, g), 16))

                    def load_feed(f):
                        k, src, t = f
                        n = ring[f]
                        if n >= RING:
                            sp.wait_ge(shared_full, upto("shared_full", ("feed", *fs[n - RING])))
                        if st.proj1:
                            sp.wait_ge(x1_out, upto("x1_out", NT - 1, 16))
                        a, b = {"x": (x_rows, i + 1), "x1": (x1_rows, i - 1), "ctx": (ctx_rows, i - 1)}[src]
                        sp.dma_start(feed[n % RING][:], rows(a, b, t)).then_inc(feed_in[n % RING], step(f"feed_in{n % RING}", f, 16))

                    pending = list(fs)
                    for s in range(SLOTS):
                        while pending and s >= 7 and (ring[pending[0]] < RING or ring[pending[0]] - RING in
                                                      [ring[f] for q in range(s) for f in feeds(st, q)]):
                            load_feed(pending.pop(0))
                        for at, which, g, before in loads:
                            if at == s:
                                load_weights(which, g, before)
                        if 1 <= s <= NT and st.mlp:
                            sp.wait_ge(dve_rows, upto("dve_rows", ("x2", s - 1)))
                            sp.dma_start(rows(x2_rows, i - 3, s - 1), x2t[:]).then_inc(x2_out, step("x2_out", s - 1, 16))
                        if s < NT and st.mlp:
                            sp.dma_start(x1res[:], rows(x1_rows, i - 3, s)).then_inc(x1res_in, step("x1res_in", s, 16))
                        if 1 <= s <= NT and st.proj1:
                            sp.wait_ge(dve_rows, upto("dve_rows", ("x1", s - 1)))
                            sp.dma_start(rows(x1_rows, i - 1, s - 1), xres[:]).then_inc(x1_out, step("x1_out", s - 1, 16))
                        if s < NT and st.proj1:
                            if s:
                                sp.wait_ge(x1_out, upto("x1_out", s - 1, 16))
                            sp.dma_start(xres[:], rows(x_rows, i - 1, s)).then_inc(xres_in, step("xres_in", s, 16))
                        for t in mlp_down(st, s - 1):
                            sp.wait_ge(h_dve, upto("h_dve", ("out", t)))
                            sp.dma_start(rows(out_rows, i - 3, t), x2res[:]).then_inc(y_out, step("y_out", t, 16))
                        for t in mlp_down(st, s):
                            if t == 0:
                                sp.wait_ge(x2_out, upto("x2_out", NT - 1, 16))
                            else:
                                sp.wait_ge(y_out, upto("y_out", t - 1, 16))
                            sp.dma_start(x2res[:], rows(x2_rows, i - 3, t)).then_inc(x2res_in, step("x2res_in", t, 16))
                    while pending:
                        load_feed(pending.pop(0))
                    for t in mlp_down(st, SLOTS - 1):
                        sp.wait_ge(h_dve, upto("h_dve", ("out", t)))
                        sp.dma_start(rows(out_rows, i - 3, t), x2res[:]).then_inc(y_out, step("y_out", t, 16))
                    if st.proj1:
                        sp.wait_ge(x1_out, 16 * NT)
                    if st.mlp:
                        sp.wait_ge(x2_out, 16 * NT)
                        sp.wait_ge(y_out, 16 * NT)
                    if st.self_next:
                        sp.wait_ge(w_in, upto("w_in", ("self", NG + 1), 16))

                @block.tensor
                def _(pe):
                    def free(name, read, label):
                        if C.two_before(name, label):
                            pe.wait_ge(read, C.two_before(name, label))

                    def probs_self(m, j):
                        qt = m % NT
                        pe.wait_ge(sexp, upto("sexp", (m, j)))
                        free("turned_read", turned_read, ("self", m, j))
                        for k in range(qt + 1):
                            mm = pe.transpose(turned_ps[j % 2][:, k * P:(k + 1) * P], sP[j][:, k * P:(k + 1) * P], ident[:])
                        mm.then_inc(turned_full, step("turned_full", ("self", m, j)))

                    def values_self(m, j):
                        qt, g = m % NT, (m // NT) % NG
                        pe.wait_ge(turned_read, upto("turned_read", ("self", m, j)))
                        if j == 0 and m - 1 in C.apply_self:
                            pe.wait_ge(so_norm, upto("so_norm", m - 1))
                        for k in range(qt + 1):
                            mm = pe.matmul(so_ps[:, j * (HD + 1):(j + 1) * (HD + 1)], sPT[j % 2][:, k * P:(k + 1) * P],
                                           sv[g % 2][:, k, j, :], start=k == 0, stop=k == qt)
                        if j == HG - 1:
                            mm.then_inc(so_full, step("so_full", m))

                    def scores_self(s, j):
                        qt = s % NT
                        free("score_read", score_read, ("self", s, j))
                        if s and not j:
                            pe.wait_ge(shared_read, upto("shared_read", (("self_q", s), 0)))
                        pe.matmul(score_ps[j % 2][:, 0:(qt + 1) * P], sq_stack[:, j, :], sk_stack[:, j, 0:(qt + 1) * P],
                                  start=True, stop=False)
                        pe.matmul(score_ps[j % 2][:, qt * P:(qt + 1) * P], ident16[:], mask16[:], start=False,
                                  stop=True).then_inc(score_full, step("score_full", ("self", s, j)))

                    def probs_cross(m, j):
                        pe.wait_ge(cprob, upto("cprob", (m, j)))
                        free("turned_read", turned_read, ("cross", m, j))
                        for k in range(NT):
                            mm = pe.transpose(turned_ps[j % 2][:, k * P:(k + 1) * P], cS[m % 2][j][:, k * P:(k + 1) * P], ident[:])
                        mm.then_inc(turned_full, step("turned_full", ("cross", m, j)))

                    def values_cross(m, j):
                        g = (m // NT) % NG
                        pe.wait_ge(turned_read, upto("turned_read", ("cross", m, j)))
                        if j == 0 and m - 1 in C.apply_cross:
                            pe.wait_ge(co_norm, upto("co_norm", m - 1))
                        for k in range(NT):
                            mm = pe.matmul(co_ps[:, j * (HD + 1):(j + 1) * (HD + 1)], cPT[j % 2][:, k * P:(k + 1) * P],
                                           cv[g % 2][:, k, j, :], start=k == 0, stop=k == NT - 1)
                        if j == HG - 1:
                            mm.then_inc(co_full, step("co_full", m))

                    def scores_cross(n, j):
                        free("score_read", score_read, ("cross", n, j))
                        if not j:
                            pe.wait_ge(shared_read, upto("shared_read", (("cross_q", n), 0)))
                        pe.matmul(score_ps[j % 2][:], cq_stack[:, j, :], ck_stack[:, j, :], start=True,
                                  stop=True).then_inc(score_full, step("score_full", ("cross", n, j)))

                    def turn(ps, src):
                        for c in range(4):
                            mm = pe.transpose(ps[:, c * P:(c + 1) * P], src(c), ident[:])
                        return mm

                    def unit(u, s):
                        ps = shared_ps[C.bank[u]]
                        freed(pe, u)
                        kind = u[0]
                        if kind == "cross_oT":
                            if u[1] == NT - 1:
                                pe.wait_ge(co_norm, upto("co_norm", -1))
                            mm = turn(ps, lambda c: co[:, u[1], c * P:(c + 1) * P])
                        elif kind == "self_oT":
                            if u[1] == NT - 1:
                                pe.wait_ge(so_norm, upto("so_norm", -1))
                            mm = turn(ps, lambda c: so[:, u[1], c * P:(c + 1) * P])
                        elif kind in ("cross_out", "self_out"):
                            oT, w, b = (cross_oT, woT, D) if kind == "cross_out" else (self_oT, wproj, 0)
                            pe.matmul(ps[:], ones16[64:67, :], bias16[64:67, b:b + D], start=True, stop=False)
                            pe.wait_ge(shared_read, upto("shared_read", ((kind[:-3] + "oT", u[1]), 0)))
                            for c in range(NC):
                                mm = pe.matmul(ps[:], oT[:, c, :], w[:, c, :], start=False, stop=c == NC - 1)
                        elif kind == "x2T":
                            pe.wait_ge(pool_rows, upto("pool_rows", ("quant", u[1], 2)))
                            mm = turn(ps, lambda c: x2h[:, c * P:(c + 1) * P])
                        elif kind in ("gate", "up"):
                            w = wgT if kind == "gate" else wuT
                            pe.wait_ge(shared_read, upto("shared_read", (("x2T", u[1]), 0)))
                            for c in range(NC):
                                mm = pe.matmul(ps[:], x2T[:, u[1], c, :], w[:, c, u[2] * 512:(u[2] + 1) * 512],
                                               start=c == 0, stop=c == NC - 1)
                        elif kind == "hT":
                            pe.wait_ge(h_pool, upto("h_pool", ("q", u[1], u[2])))
                            mm = turn(ps, lambda c: hh[:, u[2], c * P:(c + 1) * P])
                        elif kind == "down":
                            pe.wait_ge(shared_read, upto("shared_read", (("hT", u[1], NF - 1), 0)))
                            for c in range(KF):
                                mm = pe.matmul(ps[:], hT[:, c, :], wdT[:, c, :], start=c == 0, stop=c == KF - 1)
                        elif kind == "self_qkv":
                            g, t = u[1], u[2]
                            if t == 0:
                                pe.wait_ge(w_in, upto("w_in", ("self", g), 16))
                                if g == NG:
                                    pe.wait_ge(shared_read, upto("shared_read", (("feed", 3, "x", 3), 0)))
                            for part in range(3):
                                at = part * D + (g % NG) * P
                                pe.matmul(ps[:, part * P:(part + 1) * P], ones16[0:3, :], bias16[0:3, at:at + P],
                                          start=part == 0, stop=False, skip_group_check=True)
                            for c in range(NC):
                                mm = pe.matmul(ps[:, 0:3 * P], xT[:, c, t * P:(t + 1) * P], w_group[:, c, :], start=False,
                                               stop=c == NC - 1, skip_group_check=True)
                        elif kind == "cross_qkv":
                            g, t = u[1], u[2]
                            if t == 0:
                                pe.wait_ge(w_in, upto("w_in", ("cross", g), 16))
                                if g == NG:
                                    pe.wait_ge(shared_read, upto("shared_read", (("feed", 11, "ctx", 3), 0)))
                            at = (g % NG) * 3 * P
                            pe.matmul(ps[:, 0:3 * P], ones16[32:35, :], bias16[32:35, at:at + 3 * P], start=True, stop=False)
                            for c in range(NC):
                                pe.matmul(ps[:, 0:P], x1T[:, c, t * P:(t + 1) * P], w_group[:, c, 0:P], start=False, stop=False)
                            for c in range(NC):
                                mm = pe.matmul(ps[:, P:3 * P], ctxT[:, c, t * P:(t + 1) * P], w_group[:, c, P:3 * P],
                                               start=False, stop=c == NC - 1)
                        elif kind in STACKED:
                            pe.wait_ge(stage_low, upto("stage_low", u))
                            parts = stage[C.stacked.index(u) % STAGES]
                            for j in range(HG):
                                mm = pe.transpose(ps[:, j * P:(j + 1) * P].bitcast(F32R),
                                                  parts[:, j, :, :].rearrange("p r d -> p (r d)"), ident_r[:])
                        else:
                            f = u[1:]
                            n = ring[f]
                            if f[1] == "ctx":
                                pe.wait_ge(feed_in[n % RING], upto(f"feed_in{n % RING}", f, 16))
                            else:
                                pe.wait_ge(feed_pool, upto("feed_pool", (f, 4)))
                            mm = turn(ps, lambda c: feed[n % RING][:, c * P:(c + 1) * P])
                        mm.then_inc(shared_full, step("shared_full", u))

                    for s in range(SLOTS):
                        for j in range(HG):
                            if s - 1 in C.apply_self:
                                probs_self(s - 1, j)
                            if st.self_now:
                                scores_self(s, j)
                            if s - 1 in C.apply_self and j:
                                values_self(s - 1, j - 1)
                        if s - 1 in C.apply_self:
                            values_self(s - 1, HG - 1)
                        for u in early_units(st, s):
                            unit(u, s)
                        for j in range(HG):
                            if s - 1 in C.apply_cross:
                                probs_cross(s - 1, j)
                            if st.cross_now if s < SLOTS - 1 else st.cross_next:
                                scores_cross(s + 1, j)
                            for u in mid_chunk(st, s, j):
                                unit(u, s)
                            if s - 1 in C.apply_cross and j:
                                values_cross(s - 1, j - 1)
                        if s - 1 in C.apply_cross:
                            values_cross(s - 1, HG - 1)
                        for u in late_units(st, s):
                            unit(u, s)

                @block.scalar
                def _(act):
                    def unit(u):
                        ps = shared_ps[C.bank[u]]
                        kind = u[0]
                        act.wait_ge(shared_full, upto("shared_full", u))

                        def read(k, *a, **kw):
                            return act.activation(*a, **kw).then_inc(shared_read, step("shared_read", (u, k)))
                        if kind in ("cross_oT", "self_oT"):
                            if u[1]:
                                act.wait_ge(shared_full, upto("shared_full", (kind[:-2] + "out", u[1] - 1)))
                            read(0, cross_oT if kind == "cross_oT" else self_oT[:], four(ps[:]), ACT.Copy)
                        elif kind == "x2T":
                            read(0, x2T[:, u[1], :, :], four(ps[:]), ACT.Copy, bias=-MAGIC)
                        elif kind == "gate":
                            if (u[1], u[2]) != (0, 0):
                                prev = (u[1], u[2] - 1) if u[2] else (u[1] - 1, NF - 1)
                                act.wait_ge(h_pool, upto("h_pool", ("r", *prev)))
                            else:
                                act.wait_ge(x2_out, upto("x2_out", NT - 1, 16))
                            if u[2] == 0:
                                act.wait_ge(pool_rows, upto("pool_rows", ("quant", u[1], 1)))
                            read(0, th[:], ps[:], ACT.Tanh, scale=gate_scale[:, u[1], 0:1])
                            if u[1]:
                                act.wait_ge(shared_full, upto("shared_full", ("hT", u[1] - 1, u[2])))
                            read(1, hh[:, u[2], :], ps[:], ACT.Copy, scale=gate_scale[:, u[1], 1:2])
                        elif kind == "up":
                            if (u[1], u[2]) != (0, 0):
                                prev = (u[1], u[2] - 1) if u[2] else (u[1] - 1, NF - 1)
                                act.wait_ge(h_dve, upto("h_dve", ("h", *prev)))
                            read(0, uc[:], ps[:], ACT.Copy)
                        elif kind == "hT":
                            if u[1] and not u[2]:
                                act.wait_ge(shared_full, upto("shared_full", ("down", u[1] - 1)))
                            read(0, hT[:, 4 * u[2]:4 * u[2] + 4, :], four(ps[:]), ACT.Copy, bias=-MAGIC)
                        elif kind in ("self_qkv", "cross_qkv"):
                            g, t = u[1], u[2]
                            if kind == "cross_qkv":
                                if t == 0:
                                    act.wait_ge(stage_low, upto("stage_low", ("cross_q", NT * g - 1)))
                                read(0, cqk[:, t, :], ps[:, 0:2 * P], ACT.Copy)
                                v = cv
                            else:
                                if t == 0:
                                    act.wait_ge(stage_low, max(upto("stage_low", ("self_k", g - 1, NT - 1)),
                                                               upto("stage_low", ("self_q", NT * (g - 1) - 1))))
                                read(0, sx[:, t, 2 * (g % 2), :], ps[:, 0:P], ACT.Copy)
                                read(1, sx[:, t, 1, :], ps[:, P:2 * P], ACT.Copy)
                                v = sv
                            if t == 0 and g >= 2:
                                full, name = (so_full, "so_full") if kind == "self_qkv" else (co_full, "co_full")
                                act.wait_ge(full, upto(name, 4 * (g - 1) - 1))
                            read(ACT_READS[kind] - 1, v[g % 2][:, t, :, 0:HD], ps[:, 2 * P:3 * P].rearrange("p (h d) -> p h d", h=HG), ACT.Copy)
                        elif kind in ("self_k", "cross_k"):
                            read(0, (sk_stack if kind == "self_k" else ck_stack)[:, :, u[2] * P:(u[2] + 1) * P], four(ps[:]), ACT.Copy)
                        elif kind in ("self_q", "cross_q"):
                            read(0, (sq_stack if kind == "self_q" else cq_stack)[:], four(ps[:]), ACT.Copy)
                        elif kind == "feed":
                            dst = {"x": xT, "x1": x1T, "ctx": ctxT}[u[2]]
                            read(0, dst[:, :, u[3] * P:(u[3] + 1) * P], four(ps[:]), ACT.Copy)

                    def high_part(n):
                        u = C.stacked[n]
                        if n >= STAGES:
                            act.wait_ge(shared_full, upto("shared_full", C.stacked[n - STAGES]))
                        if u[0] in ("self_q", "self_k"):
                            act.wait_ge(head_affine, upto("head_affine", (u[1] if u[0] == "self_k" else u[1] // NT, 3)))
                        elif u[0] == "cross_k":
                            act.wait_ge(shared_read, upto("shared_read", (("cross_qkv", u[1], u[2]), 0)))
                        act.activation(parts_of(u, 0), source(u), ACT.Copy).then_inc(stage_high, step("stage_high", u))

                    def staged(units):
                        mine = [C.stacked.index(u) for u in units if u[0] in STACKED]
                        return mine[:STAGES], {C.stacked[n - STAGES]: n for n in mine[STAGES:]}

                    for s in range(SLOTS):
                        m = s - 1
                        for j in range(HG):
                            if m in C.apply_self:
                                n = (m % NT + 1) * P
                                act.wait_ge(turned_full, upto("turned_full", ("self", m, j)))
                                act.activation(sPT[j % 2][:, 0:n], turned_ps[j % 2][:, 0:n], ACT.Copy).then_inc(
                                    turned_read, step("turned_read", ("self", m, j)))
                            if st.self_now:
                                n = (s % NT + 1) * P
                                act.wait_ge(score_full, upto("score_full", ("self", s, j)))
                                act.activation(sP[j][:, 0:n], score_ps[j % 2][:, 0:n], ACT.Copy).then_inc(
                                    score_read, step("score_read", ("self", s, j)))
                        before, after = staged(early_units(st, s))
                        for n in before:
                            high_part(n)
                        for u in early_units(st, s):
                            if u[0] in ACT_READS:
                                unit(u)
                            if u in after:
                                high_part(after[u])
                        before, after = staged(mid_units(st, s) + late_units(st, s))
                        for n in before:
                            high_part(n)
                        for j in range(HG):
                            if m in C.apply_cross:
                                act.wait_ge(turned_full, upto("turned_full", ("cross", m, j)))
                                act.activation(cPT[j % 2][:], turned_ps[j % 2][:], ACT.Copy).then_inc(
                                    turned_read, step("turned_read", ("cross", m, j)))
                            if st.cross_now if s < SLOTS - 1 else st.cross_next:
                                act.wait_ge(score_full, upto("score_full", ("cross", s + 1, j)))
                                act.activation(cS[(s + 1) % 2][j][:], score_ps[j % 2][:], ACT.Copy).then_inc(
                                    score_read, step("score_read", ("cross", s + 1, j)))
                            if st.cross_now:
                                act.wait_ge(cbias, upto("cbias", s))
                                act.wait_ge(topk, upto("topk", (s, 0, "replace", j)))
                                act.activation(cS[s % 2][j][:], cS[s % 2][j][:], ACT.Exp, bias=cnb[s % 2][:, j:j + 1],
                                               scale=SCALE).then_inc(cexp, step("cexp", (s, j)))
                            if st.self_now:
                                n = (s % NT + 1) * P
                                act.wait_ge(sbias, upto("sbias", s))
                                act.activation(sP[j][:, 0:n], sP[j][:, 0:n], ACT.Exp, bias=snb[:, j:j + 1],
                                               scale=SCALE).then_inc(sexp, step("sexp", (s, j)))
                            for u in mid_chunk(st, s, j):
                                unit(u)
                                if u in after:
                                    high_part(after[u])
                        if st.cross_now:
                            for j in range(HG):
                                act.wait_ge(topk, upto("topk", (s, ROUNDS - 1, "replace", j)))
                                act.activation(cW[j][:], cW[j][:], ACT.Exp, bias=cnb[s % 2][:, j:j + 1],
                                               scale=SCALE).then_inc(crest, step("crest", (s, j)))
                        for u in late_units(st, s):
                            if u[0] in ACT_READS:
                                unit(u)
                            if u in after:
                                high_part(after[u])

                @block.vector
                def _(dve):
                    def top_step(s, r, half, j):
                        src = cS[s % 2][j] if r == 0 else cW[j]
                        if half == "max":
                            if r == 0:
                                dve.wait_ge(score_read, upto("score_read", ("cross", s, j)))
                                if s:
                                    dve.wait_ge(cbias, upto("cbias", s - 1))
                                    dve.wait_ge(topk, upto("topk", (s - 1, ROUNDS - 1, "replace", j)))
                            else:
                                dve.wait_ge(topk, upto("topk", (s, r - 1, "replace", j)))
                            dve.max(top8[:, j, :], src[:]).then_inc(topk, step("topk", (s, r, "max", j)))
                        else:
                            dve.wait_ge(topk, upto("topk", (s, r, "max", j)))
                            if r == 0:
                                dve.wait_ge(cprob, upto("cprob", (s - 1, j)))
                                dve.wait_ge(rmax_done, upto("rmax", s))
                            dve.match_replace(cW[j][:], top8[:, j, :], src[:], REPLACED).then_inc(
                                topk, step("topk", (s, r, "replace", j)))

                    def top_part(s, k):
                        if st.cross_now:
                            for r, half, j in TOP_PARTS[k]:
                                top_step(s, r, half, j)

                    def row_maxima(s):
                        if st.cross_now:
                            dve.wait_ge(topk, upto("topk", (s, 0, "max", HG - 1)))
                            dve.wait_ge(cbias, upto("cbias", s - 1))
                            dve.tensor_copy(rowmax[:], top8[:, :, 0]).then_inc(rmax_done, step("rmax", s))

                    def norm(m, ps, full, recip, done, r_t, o_t, name):
                        qt, g = m % NT, (m // NT) % NG
                        dve.wait_ge(full, upto(name + "_full", m))
                        o = ps[:, 0:HG * (HD + 1)].rearrange("p (h d) -> p h d", h=HG)
                        dve.wait_ge(done, upto(name + "_norm", m - 1))
                        dve.reciprocal(r_t[:], o[:, :, HD]).then_inc(recip, step(name + "_recip", m))
                        dve.wait_ge(recip, upto(name + "_recip", m))
                        if m >= 0 and g == 0:
                            dve.wait_ge(shared_full, upto("shared_full", (("cross_oT" if name == "co" else "self_oT"), qt)))
                        dve.tensor_tensor(o_t[:, qt, g * P:(g + 1) * P].rearrange("p (h d) -> p h d", h=HG), o[:, :, 0:HD],
                                          r_t[:].unsqueeze(2).to_broadcast([P, HG, HD]), ALU.mult).then_inc(
                                              done, step(name + "_norm", m))

                    def cross_rows(s):
                        if s >= NT or not st.mlp:
                            return
                        dve.wait_ge(shared_full, upto("shared_full", ("cross_out", s)))
                        dve.wait_ge(x1res_in, upto("x1res_in", s, 16))
                        if s:
                            dve.wait_ge(x2_out, upto("x2_out", s - 1, 16))
                            dve.wait_ge(pool_rows, upto("pool_rows", ("ln", s - 1, 5)))
                        dve.tensor_tensor(x2t[:], shared_ps[C.bank[("cross_out", s)]][:], x1res[:], ALU.add).then_inc(
                            dve_rows, step("dve_rows", ("x2", s)))
                        dve.wait_ge(dve_rows, upto("dve_rows", ("x2", s)))
                        dve.bn_stats(mstat[:], x2t[:]).then_inc(dve_rows, step("dve_rows", ("stats", s)))
                        dve.wait_ge(dve_rows, upto("dve_rows", ("stats", s)))
                        dve.bn_aggr(mv[:], mstat[:]).then_inc(dve_rows, step("dve_rows", ("aggr", s)))

                    def self_rows(s):
                        if s >= NT or not st.proj1:
                            return
                        dve.wait_ge(shared_full, upto("shared_full", ("self_out", s)))
                        dve.wait_ge(xres_in, upto("xres_in", s, 16))
                        dve.tensor_tensor(xres[:], shared_ps[C.bank[("self_out", s)]][:], xres[:], ALU.add).then_inc(
                            dve_rows, step("dve_rows", ("x1", s)))

                    def row_scale(s):
                        if not 0 <= s < NT or not st.mlp:
                            return
                        dve.wait_ge(pool_rows, upto("pool_rows", ("ln", s, 5)))
                        if s:
                            dve.wait_ge(pool_rows, upto("pool_rows", ("quant", s - 1, 2)))
                        dve.tensor_reduce(up_amax[:, s:s + 1], x2h[:], AXX, ALU.max, apply_absolute_value=True).then_inc(
                            dve_rows, step("dve_rows", ("amax", s)))
                        dve.wait_ge(dve_rows, upto("dve_rows", ("amax", s)))
                        dve.tensor_scalar(up_amax[:, s:s + 1], up_amax[:, s:s + 1], 1e-5, 1.0 / 127.0, ALU.max, ALU.mult).then_inc(
                            dve_rows, step("dve_rows", ("clip", s)))
                        dve.wait_ge(dve_rows, upto("dve_rows", ("clip", s)))
                        dve.reciprocal(mcol[:, 7:8], up_amax[:, s:s + 1]).then_inc(dve_rows, step("dve_rows", ("inv", s)))

                    def mlp(s, early):
                        for t, n in mlp_chunk(st, s, early):
                            dve.wait_ge(h_pool, upto("h_pool", ("r", t, n)))
                            dve.wait_ge(shared_read, upto("shared_read", (("up", t, n), 0)))
                            dve.tensor_tensor(hh[:, n, :], hh[:, n, :], uc[:], ALU.mult).then_inc(
                                h_dve, step("h_dve", ("h", t, n)))
                            dve.wait_ge(h_dve, upto("h_dve", ("h", t, n)))
                            dve.tensor_reduce(hmx[:, n:n + 1], hh[:, n, :], AXX, ALU.max, apply_absolute_value=True).then_inc(
                                h_dve, step("h_dve", ("max", t, n)))
                            if n == NF - 1:
                                dve.wait_ge(h_dve, upto("h_dve", ("max", t, n)))
                                if t:
                                    dve.wait_ge(h_pool, upto("h_pool", ("q", t - 1, NF - 1)))
                                dve.tensor_reduce(hcol[:, 0:1], hmx[:], AXX, ALU.max).then_inc(h_dve, step("h_dve", ("amax", t)))
                                dve.wait_ge(h_dve, upto("h_dve", ("amax", t)))
                                dve.tensor_scalar(hcol[:, 1:2], hcol[:, 0:1], 1e-5, 1.0 / 127.0, ALU.max, ALU.mult).then_inc(
                                    h_dve, step("h_dve", ("clip", t)))
                                dve.wait_ge(h_dve, upto("h_dve", ("clip", t)))
                                dve.reciprocal(hcol[:, 2:3], hcol[:, 1:2]).then_inc(h_dve, step("h_dve", ("inv", t)))

                    def down(s):
                        for t in mlp_down(st, s):
                            dve.wait_ge(shared_full, upto("shared_full", ("down", t)))
                            dve.wait_ge(x2res_in, upto("x2res_in", t, 16))
                            dve.wait_ge(h_pool, upto("h_pool", ("scale", t)))
                            dve.scalar_tensor_tensor(x2res[:], shared_ps[C.bank[("down", t)]][:], hcol[:, 3:4], x2res[:],
                                                     ALU.mult, ALU.add).then_inc(h_dve, step("h_dve", ("out", t)))

                    def feed_stats_of(s):
                        for f in feeds(st, s):
                            if f[1] == "ctx":
                                continue
                            n, p = ring[f], normed.index(f)
                            dve.wait_ge(feed_in[n % RING], upto(f"feed_in{n % RING}", f, 16))
                            if p:
                                dve.wait_ge(feed_stats, upto("feed_stats", (normed[p - 1], 1)))
                            dve.bn_stats(fstat[:], feed[n % RING][:]).then_inc(feed_stats, step("feed_stats", (f, 0)))
                            dve.wait_ge(feed_stats, upto("feed_stats", (f, 0)))
                            if p >= RING:
                                dve.wait_ge(feed_pool, upto("feed_pool", (normed[p - RING], 4)))
                            dve.bn_aggr(fmv[p % RING][:], fstat[:]).then_inc(feed_stats, step("feed_stats", (f, 1)))

                    def sum_squares(s):
                        g = self_group(st, s)
                        if s % NT == 2 and g:
                            dve.wait_ge(sq_done, upto("sq_done", g))
                            dve.wait_ge(shat_done, upto("shat_done", g - 1))
                            dve.tensor_reduce(srs[:], ssq[:].rearrange("p t k (h d) -> p (t k h) d", d=HD), AXX, ALU.add).then_inc(
                                sumsq_done, step("sumsq_done", g))

                    def self_maxima(s):
                        if st.self_now:
                            n = (s % NT + 1) * P
                            for j in range(HG):
                                dve.wait_ge(score_read, upto("score_read", ("self", s, j)))
                                if j == 0 and s:
                                    dve.wait_ge(sbias, upto("sbias", s - 1))
                                    dve.wait_ge(smax, upto("smax", (s - 1, HG - 1)))
                                dve.reduce_max(smx[:, j:j + 1], sP[j][:, 0:n], AXX).then_inc(smax, step("smax", (s, j)))

                    def norm_cross(m):
                        if m in C.apply_cross:
                            norm(m, co_ps, co_full, co_recip, co_norm, co_r, co, "co")

                    for s in range(SLOTS):
                        top_part(s, 0)
                        row_maxima(s)
                        top_part(s, 1)
                        norm_cross(s - 2)
                        down(s - 1)
                        self_maxima(s)
                        row_scale(s - 1)
                        mlp(s - 1, False)
                        top_part(s, 2)
                        sum_squares(s)
                        if s - 1 in C.apply_self:
                            norm(s - 1, so_ps, so_full, so_recip, so_norm, so_r, so, "so")
                        cross_rows(s)
                        top_part(s, 3)
                        self_rows(s)
                        feed_stats_of(s)
                        top_part(s, 4)
                        mlp(s, True)
                        top_part(s, 5)
                    norm_cross(SLOTS - 2)
                    down(SLOTS - 1)

                @block.gpsimd
                def _(pool):
                    def layer_norm(src, dst, mvt, col, name, sem_, label, ready):
                        ready()
                        pool.tensor_scalar(col[:, 0:1], mvt[:, 1:2], 1.0, EPS, ALU.mult, ALU.add).then_inc(sem_, step(name, label(0)))
                        pool.wait_ge(sem_, upto(name, label(0)))
                        pool.tensor_tensor(col[:, 1:2], col[:, 0:1], minus_half[:, 0:1], ALU.pow).then_inc(sem_, step(name, label(1)))
                        pool.wait_ge(sem_, upto(name, label(1)))
                        pool.tensor_tensor(col[:, 2:3], mvt[:, 0:1], col[:, 1:2], ALU.mult).then_inc(sem_, step(name, label(2)))
                        pool.wait_ge(sem_, upto(name, label(2)))
                        pool.tensor_scalar(col[:, 3:4], col[:, 2:3], -1.0, 0.0, ALU.mult, ALU.add).then_inc(sem_, step(name, label(3)))
                        pool.wait_ge(sem_, upto(name, label(3)))
                        return pool.tensor_scalar(dst, src, col[:, 1:2], col[:, 3:4], ALU.mult, ALU.add)

                    def rows_ln(s):
                        if s >= NT or not st.mlp:
                            return

                        def ready():
                            pool.wait_ge(dve_rows, upto("dve_rows", ("aggr", s)))
                            if s:
                                pool.wait_ge(shared_full, upto("shared_full", ("x2T", s - 1)))
                                pool.wait_ge(pool_rows, upto("pool_rows", ("quant", s - 1, 2)))
                        layer_norm(x2t[:], x2h[:], mv, mcol, "pool_rows", pool_rows, lambda k: ("ln", s, k), ready).then_inc(
                            pool_rows, step("pool_rows", ("ln", s, 4)))
                        pool.wait_ge(pool_rows, upto("pool_rows", ("ln", s, 4)))
                        pool.tensor_scalar(mcol[:, 4:5], wscale[:, 0:1], 0.5, 0.0, ALU.mult, ALU.add).then_inc(
                            pool_rows, step("pool_rows", ("ln", s, 5)))

                    def rows_quant(s):
                        if not 0 <= s < NT or not st.mlp:
                            return
                        pool.wait_ge(dve_rows, upto("dve_rows", ("inv", s)))
                        pool.wait_ge(pool_rows, upto("pool_rows", ("ln", s, 5)))
                        pool.tensor_tensor(gate_scale[:, s, 0:1], up_amax[:, s:s + 1], mcol[:, 4:5], ALU.mult).then_inc(
                            pool_rows, step("pool_rows", ("quant", s, 0)))
                        pool.wait_ge(pool_rows, upto("pool_rows", ("quant", s, 0)))
                        pool.tensor_scalar(gate_scale[:, s, 1:2], gate_scale[:, s, 0:1], up_amax[:, s:s + 1], wscale[:, 1:2],
                                           ALU.mult, ALU.mult).then_inc(pool_rows, step("pool_rows", ("quant", s, 1)))
                        pool.tensor_scalar(x2h[:], x2h[:], mcol[:, 7:8], MAGIC, ALU.mult, ALU.add).then_inc(
                            pool_rows, step("pool_rows", ("quant", s, 2)))

                    def silu(s, early):
                        for t, n in mlp_chunk(st, s, early):
                            pool.wait_ge(shared_read, upto("shared_read", (("gate", t, n), 1)))
                            pool.tensor_scalar(th[:], th[:], 1.0, 1.0, ALU.add, ALU.mult).then_inc(h_pool, step("h_pool", ("t1", t, n)))
                            pool.wait_ge(h_pool, upto("h_pool", ("t1", t, n)))
                            pool.tensor_tensor(hh[:, n, :], th[:], hh[:, n, :], ALU.mult).then_inc(
                                h_pool, step("h_pool", ("r", t, n)))

                    def inner_quant(s):
                        for t, n in mlp_chunk(st, s, False):
                            if n == NF - 1:
                                pool.wait_ge(h_dve, upto("h_dve", ("inv", t)))
                                if t:
                                    pool.wait_ge(h_dve, upto("h_dve", ("out", t - 1)))
                                pool.tensor_tensor(hcol[:, 3:4], hcol[:, 1:2], wscale[:, 2:3], ALU.mult).then_inc(
                                    h_pool, step("h_pool", ("scale", t)))
                                for q in range(NF):
                                    pool.tensor_scalar(hh[:, q, :], hh[:, q, :], hcol[:, 2:3], MAGIC, ALU.mult, ALU.add).then_inc(
                                        h_pool, step("h_pool", ("q", t, q)))

                    def squares(s):
                        g = self_group(st, s)
                        if s % NT == 1 and g:
                            pool.wait_ge(shared_read, upto("shared_read", (("self_qkv", g, NT - 1), 1)))
                            pool.wait_ge(sumsq_done, upto("sumsq_done", g - 1))
                            x_ = sx[:, :, g % 2:g % 2 + 2, :]
                            pool.tensor_tensor(ssq[:], x_, x_, ALU.mult).then_inc(sq_done, step("sq_done", g))

                    def head_norm(s):
                        g = self_group(st, s)
                        if s % NT == 2 and g:
                            pool.wait_ge(sumsq_done, upto("sumsq_done", g))
                            pool.tensor_scalar(srs[:], srs[:], 1.0 / HD, EPS, ALU.mult, ALU.add).then_inc(
                                rstd_done, step("rstd_done", (g, 0)))
                            pool.wait_ge(rstd_done, upto("rstd_done", (g, 0)))
                            pool.tensor_tensor(srs[:], srs[:], minus_half[:], ALU.pow).then_inc(
                                rstd_done, step("rstd_done", (g, 1)))
                            pool.wait_ge(rstd_done, upto("rstd_done", (g, 1)))
                            q = sx[:, :, g % 2:g % 2 + 2, :].rearrange("p t k (h d) -> p t (k h) d", d=HD)
                            r = srs[:].rearrange("p (t h) -> p t h", t=NT).unsqueeze(3).to_broadcast([P, NT, 2 * HG, HD])
                            pool.tensor_tensor(q, q, r, ALU.mult).then_inc(
                                shat_done, step("shat_done", g))

                    def affine(s):
                        g = self_group(st, s)
                        if s % NT == 2 and g:
                            for k in range(4):
                                part = k // 2
                                pool.wait_ge(*((head_affine, upto("head_affine", (g, k - 1))) if k % 2 else
                                               (shat_done, upto("shat_done", g))))
                                for_all = gb[:, k, :].unsqueeze(1).to_broadcast([P, HG * NT, HD])
                                x_ = sx[:, :, 1 if part else 2 * (g % 2), :].rearrange("p t (h d) -> p t h d", d=HD)
                                pool.tensor_tensor(x_, x_, for_all.rearrange("p (t h) d -> p t h d", h=HG),
                                                   ALU.add if k % 2 else ALU.mult).then_inc(
                                    head_affine, step("head_affine", (g, k)))

                    def low_parts(units):
                        for u in units:
                            if u[0] in STACKED:
                                pool.wait_ge(stage_high, upto("stage_high", u))
                                pool.tensor_tensor(parts_of(u, 1), source(u), parts_of(u, 0).bitcast(F32), ALU.subtract).then_inc(
                                    stage_low, step("stage_low", u))

                    def probabilities(m):
                        if st.cross_now:
                            for j in range(HG):
                                pool.wait_ge(crest, upto("crest", (m, j)))
                                pool.tensor_tensor(cS[m % 2][j][:], cS[m % 2][j][:], cW[j][:], ALU.subtract).then_inc(
                                    cprob, step("cprob", (m, j)))

                    def first_staged(s):
                        u = [u for u in mid_units(st, s) + late_units(st, s) if u[0] in STACKED]
                        return u[:STAGES], u[STAGES:]

                    for s in range(SLOTS):
                        m = s - 1
                        if s:
                            probabilities(m)
                        silu(m, False)
                        rows_quant(m)
                        low_parts(early_units(st, s))
                        if st.cross_now:
                            pool.wait_ge(rmax_done, upto("rmax", s))
                            if s:
                                pool.wait_ge(crest, upto("crest", (s - 2, HG - 1)))
                            pool.tensor_scalar(cnb[s % 2][:], rowmax[:], -SCALE, 0.0, ALU.mult, ALU.add).then_inc(
                                cbias, step("cbias", s))
                        if st.self_now:
                            pool.wait_ge(smax, upto("smax", (s, HG - 1)))
                            if s:
                                pool.wait_ge(sexp, upto("sexp", (s - 1, HG - 1)))
                            pool.tensor_scalar(snb[:], smx[:], -SCALE, 0.0, ALU.mult, ALU.add).then_inc(sbias, step("sbias", s))
                        first, rest = first_staged(s)
                        low_parts(first)
                        inner_quant(m)
                        silu(s, True)
                        head_norm(s)
                        affine(s)
                        low_parts(rest)
                        rows_ln(s)
                        for f in feeds(st, s):
                            if f[1] == "ctx":
                                continue
                            n, p = ring[f], normed.index(f)

                            def ready():
                                pool.wait_ge(feed_stats, upto("feed_stats", (f, 1)))
                                if p >= RING:
                                    pool.wait_ge(feed_pool, upto("feed_pool", (normed[p - RING], 4)))
                            layer_norm(feed[n % RING][:], feed[n % RING][:], fmv[p % RING], fcol[p % RING], "feed_pool", feed_pool, lambda k: (f, k),
                                       ready).then_inc(feed_pool, step("feed_pool", (f, 4)))
                        squares(s)
                    probabilities(SLOTS - 1)

            C.end()

        def iteration(i, st):
            one_iteration(i, st)
            nc.gpsimd.sem_clear(range(min(nums), max(nums) + 1))
            nc.all_engine_barrier()

        steady = [i for i in range(LO, HI + 1) if Stages(i).key() == Stages(3).key()]
        for i in range(LO, steady[0]):
            iteration(i, Stages(i))
        with nc.Fori(steady[0], steady[-1] + 1) as i:
            iteration(i, Stages(steady[0]))
        for i in range(steady[-1] + 1, HI + 1):
            iteration(i, Stages(i))


def setup(nc, T):
    W_attn, b_attn, wa_dram, wc_dram = T["W_attn"], T["b_attn"], T["wa_dram"], T["wc_dram"]
    banks, ident, ident16, mask16, ones16, bias16 = (T[k] for k in ("banks", "ident", "ident16", "mask16", "ones16", "bias16"))
    minus_half, gb, wscale, wproj, woT = (T[k] for k in ("minus_half", "gb", "wscale", "wproj", "woT"))
    wgT, wuT, wdT = T["wgT"], T["wuT"], T["wdT"]
    with ExitStack() as tmp:
        def sb(name, shape, dt=F32):
            return tmp.enter_context(nc.sbuf_tensor(name, shape, dt))

        def sem(name):
            return tmp.enter_context(nc.semaphore(name))

        wnat = sb("wnat", [P, NC, 3 * D])
        hmean = sb("hmean", [P, NC + 1, 2 * H])
        brow = sb("brow", [1, 8 * D])
        bpart = sb("bpart", [1, 3, 8 * D], BF16)
        wx = [sb(f"wx{k}", [P, NC, D]) for k in range(2)]
        wcT = sb("wcT", [P, NC, 3, D])
        s_const, s_b, s_bp, s_bd, s_w, s_mean, s_cent, s_out = (sem(f"su_{n}") for n in (
            "const", "b", "bp", "bd", "w", "mean", "cent", "out"))
        s_x = [sem(f"su_x{k}") for k in range(2)]
        s_xp, s_xa, s_res = sem("su_xp"), sem("su_xa"), sem("su_res")
        NBIAS = 4 + 3 * NG
        with nc.Block() as block:
            @block.sync
            def _(sp):
                sp.dma_start(wnat[:], W_attn.rearrange("(c p) n -> p c n", p=P)).then_inc(s_w, 16)
                sp.dma_start(brow[:, 0:3 * D], b_attn.rearrange("(a n) -> a n", a=1)).then_inc(s_b, 16)
                for g in range(NG):
                    for k, b in enumerate((T["bq"], T["bk"], T["bv"])):
                        sp.dma_start(brow[:, 3 * D + (3 * g + k) * P:3 * D + (3 * g + k + 1) * P],
                                     b[g * P:(g + 1) * P].rearrange("(a n) -> a n", a=1)).then_inc(s_b, 16)
                for k, b in enumerate((T["b_proj"], T["bo"])):
                    sp.dma_start(brow[:, (6 + k) * D:(7 + k) * D], b.rearrange("(a n) -> a n", a=1)).then_inc(s_b, 16)
                for k, v in enumerate((T["q_gamma"], T["q_beta"], T["k_gamma"], T["k_beta"])):
                    sp.dma_start(gb[:, k, :], v.partition_broadcast(P)).then_inc(s_res, 16)
                sp.dma_start(wproj[:], T["W_proj"].rearrange("(c p) n -> p c n", p=P)).then_inc(s_res, 16)
                for k, w in enumerate((T["Wq"], T["Wk"], T["Wv"], T["Wo"])):
                    if k >= 2:
                        sp.wait_ge(s_xp, NC * (k - 1))
                    sp.dma_start(wx[k % 2][:], w.rearrange("(c p) n -> p c n", p=P)).then_inc(s_x[k % 2], 16)
                sp.wait_ge(s_cent, 2)
                for g in range(NG):
                    for part in range(3):
                        sp.dma_start(wa_dram[g, :, :, part, :],
                                     wnat[:, :, part * D + g * P:part * D + (g + 1) * P]).then_inc(s_out, 16)
                sp.wait_ge(s_bp, 5)
                for base, lo, n in ((0, 0, 3 * D), (32, 3 * D, 3 * D), (64, 6 * D, 2 * D)):
                    for r in range(3):
                        sp.dma_start(bias16[base + r:base + r + 1, 0:n], bpart[:, r, lo:lo + n]).then_inc(s_bd, 16)
                sp.wait_ge(s_bd, 9 * 16)
                sp.wait_ge(s_out, 2 * 3 * NG * 16)
                sp.wait_ge(s_res, 5 * 16)

            @block.gpsimd
            def _(pool):
                pool.memset(ident[:], 0.0).then_inc(s_const, 1)
                pool.memset(mask16[:], 0.0).then_inc(s_const, 1)
                pool.memset(ones16[:], 1.0)
                pool.memset(minus_half[:], -0.5)
                pool.wait_ge(s_const, 2)
                pool.affine_select(out=ident[:], in_=ident[:], compare_op=ALU.not_equal, fill=1.0, base=0,
                                   pattern=[[-1, P]], channel_multiplier=1).then_inc(s_const, 1)
                pool.affine_select(out=mask16[:], in_=mask16[:], compare_op=ALU.is_ge, fill=MASKED, base=0,
                                   pattern=[[-1, P]], channel_multiplier=1).then_inc(s_const, 1)
                pool.wait_ge(s_const, 3)
                pool.tensor_copy(ident16[:], ident[:])
                pool.tensor_copy(T["ident_r"][:], ident[:])

            @block.vector
            def _(dve):
                dve.wait_ge(s_w, 16)
                for c in range(NC):
                    dve.tensor_reduce(hmean[:, c, :], wnat[:, c, 0:2 * D].rearrange("p (h d) -> p h d", d=HD),
                                      AXX, ALU.add).then_inc(s_mean, 1)
                dve.wait_ge(s_b, 16 * (1 + 3 * NG + 2))
                dve.tensor_reduce(hmean[0:1, NC, :], brow[:, 0:2 * D].rearrange("p (h d) -> p h d", d=HD),
                                  AXX, ALU.add).then_inc(s_mean, 1)
                dve.wait_ge(s_mean, NC + 1)
                dve.tensor_scalar(hmean[:, 0:NC, :], hmean[:, 0:NC, :], 1.0 / HD, None, ALU.mult).then_inc(s_mean, 1)
                dve.tensor_scalar(hmean[0:1, NC, :], hmean[0:1, NC, :], 1.0 / HD, None, ALU.mult).then_inc(s_mean, 1)
                dve.wait_ge(s_mean, NC + 3)
                for c in range(NC):
                    w = wnat[:, c, 0:2 * D].rearrange("p (h d) -> p h d", d=HD)
                    ins = dve.tensor_tensor(w, w, hmean[:, c, :].unsqueeze(2).to_broadcast([P, 2 * H, HD]), ALU.subtract)
                ins.then_inc(s_cent, 1)
                b = brow[:, 0:2 * D].rearrange("p (h d) -> p h d", d=HD)
                dve.tensor_tensor(b, b, hmean[0:1, NC, :].unsqueeze(2).to_broadcast([1, 2 * H, HD]),
                                  ALU.subtract).then_inc(s_cent, 1)
                dve.wait_ge(s_cent, 2)
                dve.tensor_copy(bpart[:, 0, :], brow[:]).then_inc(s_bp, 1)
                dve.wait_ge(s_bp, 1)
                dve.tensor_tensor(brow[:], brow[:], bpart[:, 0, :], ALU.subtract).then_inc(s_bp, 1)
                dve.wait_ge(s_bp, 2)
                dve.tensor_copy(bpart[:, 1, :], brow[:]).then_inc(s_bp, 1)
                dve.wait_ge(s_bp, 3)
                dve.tensor_tensor(brow[:], brow[:], bpart[:, 1, :], ALU.subtract).then_inc(s_bp, 1)
                dve.wait_ge(s_bp, 4)
                dve.tensor_copy(bpart[:, 2, :], brow[:]).then_inc(s_bp, 1)

            @block.tensor
            def _(pe):
                pe.wait_ge(s_const, 3)
                for k in range(4):
                    pe.wait_ge(s_x[k % 2], 16 * (k // 2 + 1))
                    for o in range(NC):
                        n = k * NC + o
                        if n >= 2:
                            pe.wait_ge(s_xa, n - 1)
                        for c in range(NC):
                            mm = pe.transpose(banks[n % 2][:, c * P:(c + 1) * P], wx[k % 2][:, o, c * P:(c + 1) * P], ident[:])
                        mm.then_inc(s_xp, 1)

            @block.scalar
            def _(act):
                for k in range(4):
                    for o in range(NC):
                        n = k * NC + o
                        act.wait_ge(s_xp, n + 1)
                        dst = woT[:, :, o * P:(o + 1) * P] if k == 3 else wcT[:, :, k, o * P:(o + 1) * P]
                        act.activation(dst, banks[n % 2][:].rearrange("p (c n) -> p c n", c=NC), ACT.Copy).then_inc(s_xa, 1)
                    if k == 2:
                        act.wait_ge(s_xa, 3 * NC)
                        for g in range(NG):
                            for part in range(3):
                                act.dma_start(wc_dram[g, :, :, part, :],
                                              wcT[:, :, part, g * P:(g + 1) * P]).then_inc(s_out, 16)

    with ExitStack() as tmp:
        def sem(name):
            return tmp.enter_context(nc.semaphore(name))

        natural = [tmp.enter_context(nc.sbuf_tensor(f"wnat{k}", [P, 16, 512], F32)) for k in range(3)]
        scratch = tmp.enter_context(nc.sbuf_tensor("scratch", [P, F], BF16))
        ones32 = tmp.enter_context(nc.sbuf_tensor("ones32b", [P, P], F32))
        sums = tmp.enter_context(nc.sbuf_tensor("sums", [P, 3, 4], F32))
        sum3 = tmp.enter_context(nc.sbuf_tensor("sum3", [P, 3], F32))
        winv = tmp.enter_context(nc.sbuf_tensor("winv", [P, 3], F32))
        s_in = [sem(f"sf_in{k}") for k in range(3)]
        s_one, s_abs, s_sum, s_mean, s_tot, s_q, s_p, s_a = (sem(f"sf_{n}") for n in (
            "one", "abs", "sum", "mean", "tot", "q", "p", "a"))
        with nc.Block() as block:
            @block.sync
            def _(sp):
                for k, w in enumerate((T["w_gate"], T["w_up"])):
                    sp.dma_start(natural[k][:], w.rearrange("(o p) n -> p o n", p=P)).then_inc(s_in[k], 16)
                sp.dma_start(natural[2][:].rearrange("p (a q) n -> p a (q n)", a=4),
                             T["w_down"].rearrange("(a p) n -> p a n", p=P)).then_inc(s_in[2], 16)

            @block.gpsimd
            def _(pool):
                pool.memset(ones32[:], 1.0).then_inc(s_one, 1)

            @block.scalar
            def _(act):
                def absolute(k):
                    act.wait_ge(s_in[k], 16)
                    for q in range(4):
                        n = 4 * k + q
                        if n:
                            act.wait_ge(s_abs, n)
                        act.activation(scratch[:].rearrange("p (a n) -> p a n", a=4), natural[k][:, 4 * q:4 * q + 4, :],
                                       ACT.Abs, accum_out=sums[:, k, q:q + 1]).then_inc(s_abs, 1)

                absolute(0)
                for k in range(3):
                    if k + 1 < 3:
                        absolute(k + 1)
                    for u in range(16):
                        n = 16 * k + u
                        act.wait_ge(s_p, n + 1)
                        src = banks[n % 4][:].rearrange("p (c n) -> p c n", c=4)
                        dst = (wdT[:, 4 * (u % 4):4 * (u % 4) + 4, (u // 4) * P:(u // 4 + 1) * P] if k == 2
                               else (wgT, wuT)[k][:, :, u * P:(u + 1) * P])
                        act.activation(dst, src, ACT.Copy, bias=-MAGIC, saturate=False).then_inc(s_a, 1)

            @block.vector
            def _(dve):
                for k in range(3):
                    dve.wait_ge(s_abs, 4 * (k + 1))
                    dve.tensor_reduce(sum3[:, k:k + 1], sums[:, k, :], AXX, ALU.add).then_inc(s_sum, 1)
                    dve.wait_ge(s_mean, k + 1)
                    dve.tensor_scalar(wscale[:, k:k + 1], banks[7][:, k:k + 1], 1.0 / (F * D), 1e-5, ALU.mult,
                                      ALU.max).then_inc(s_tot, 1)
                    dve.wait_ge(s_tot, 2 * k + 1)
                    dve.reciprocal(winv[:, k:k + 1], wscale[:, k:k + 1]).then_inc(s_tot, 1)
                    dve.wait_ge(s_tot, 2 * k + 2)
                    for u in range(16):
                        n = 16 * k + u
                        w = natural[k][:, u, :]
                        dve.tensor_scalar(w, w, winv[:, k:k + 1], 1.0, ALU.mult, ALU.min).then_inc(s_q, 1)
                        dve.wait_ge(s_q, 2 * n + 1)
                        dve.tensor_scalar(w, w, -1.0, MAGIC, ALU.max, ALU.add).then_inc(s_q, 1)

            @block.tensor
            def _(pe):
                pe.wait_ge(s_one, 1)
                for k in range(3):
                    pe.wait_ge(s_sum, k + 1)
                    if k:
                        pe.wait_ge(s_tot, 2 * k)
                    pe.matmul(banks[7][:, k:k + 1], ones32[:], sum3[:, k:k + 1], start=True, stop=True).then_inc(s_mean, 1)
                    for u in range(16):
                        n = 16 * k + u
                        if n >= 4:
                            pe.wait_ge(s_a, n - 3)
                        pe.wait_ge(s_q, 2 * n + 2)
                        for b in range(4):
                            mm = pe.transpose(banks[n % 4][:, b * P:(b + 1) * P], natural[k][:, u, b * P:(b + 1) * P], ident[:])
                        mm.then_inc(s_p, 1)


NAMES = ["x", "ctx_1024", "L0_attn_W_attn", "L0_attn_b_attn", "L0_attn_W_proj", "L0_attn_b_proj",
         "L0_attn_q_gamma", "L0_attn_q_beta", "L0_attn_k_gamma", "L0_attn_k_beta", "L0_xattn_Wq",
         "L0_xattn_bq", "L0_xattn_Wk", "L0_xattn_bk", "L0_xattn_Wv", "L0_xattn_bv", "L0_xattn_Wo",
         "L0_xattn_bo", "L0_ffn_w_gate", "L0_ffn_w_up", "L0_ffn_w_down"]


def kernel(**inputs):
    import concourse.bacc as bacc
    from concourse.bass_utils import run_bass_kernel_spmd

    nc = bacc.Bacc("TRN2", target_bir_lowering=False, num_devices=1)
    arrays, args = {}, []
    for name in NAMES:
        a = np.ascontiguousarray(inputs[name])
        arrays[f"in_{name}"] = a
        args.append(nc.dram_tensor(f"in_{name}", a.shape, mybir.dt.from_np(a.dtype), kind="ExternalInput").ap())
    out = nc.dram_tensor("out_y", (NB, S, D), F32, kind="ExternalOutput").ap()
    decoder_layer(nc, *args, out)
    r = run_bass_kernel_spmd(nc, [arrays], core_ids=[0])
    return r.results[0]["out_y"]
```
